# Optimizing a Trainium2 kernel written in Bass

```python
import numpy as np
import jax
import jax.numpy as jnp

def _softmax(x, axis=-1):
    return jax.nn.softmax(x, axis=axis)

def _gelu(x):
    return jax.nn.gelu(x, approximate=True)

def _silu(x):
    return jax.nn.silu(x)

def _sigmoid(x):
    return jax.nn.sigmoid(x)

def _layernorm(x, axis=-1, eps=1e-05):
    m = jnp.mean(x, axis=axis, keepdims=True)
    v = jnp.var(x, axis=axis, keepdims=True)
    return (x - m) / jnp.sqrt(v + eps)

def _scatter_add(tgt, idx, src, axis=0):
    return tgt.at[idx].add(src)

def _segment_sum(src, seg, n):
    return jax.ops.segment_sum(src, seg, n)
kernel_name = 'mk_sandwich_d2_jaxref_r8_dd29c8'

def setup_inputs(seed: int=0):
    np.random.seed(seed)
    _w = jnp.asarray

    def _L0_attn_setup():
        import jax, jax.numpy as jnp
        import numpy as np
        D_MODEL = 128
        D_STATE = 16
        D_CONV = 4
        EXPAND = 2
        D_INNER = D_MODEL * EXPAND
        B, L = (2, 128)
        key = jax.random.key(seed)
        ks = jax.random.split(key, 8)
        x = jax.random.normal(ks[0], (B, L, D_MODEL), dtype=jnp.float32)
        W_in = jax.random.normal(ks[1], (2 * D_INNER, D_MODEL), dtype=jnp.float32) / np.sqrt(D_MODEL)
        conv_w = jax.random.normal(ks[2], (D_INNER, 1, D_CONV), dtype=jnp.float32) / np.sqrt(D_CONV)
        conv_b = jnp.zeros((D_INNER,), dtype=jnp.float32)
        W_x = jax.random.normal(ks[3], (2 * D_STATE + 1, D_INNER), dtype=jnp.float32) / np.sqrt(D_INNER)
        w_dt = jax.random.normal(ks[4], (D_INNER,), dtype=jnp.float32) * 0.01
        dt_init = jnp.exp(jax.random.uniform(ks[5], (D_INNER,)) * (np.log(0.1) - np.log(0.001)) + np.log(0.001))
        b_dt = jnp.log(jnp.expm1(dt_init))
        A_log = jnp.log(jnp.broadcast_to(jnp.arange(1, D_STATE + 1, dtype=jnp.float32), (D_INNER, D_STATE)))
        D_param = jnp.ones((D_INNER,), dtype=jnp.float32)
        W_out = jax.random.normal(ks[6], (D_MODEL, D_INNER), dtype=jnp.float32) / np.sqrt(D_INNER)
        return {'x': x, 'W_in': W_in, 'conv_w': conv_w, 'conv_b': conv_b, 'W_x': W_x, 'w_dt': w_dt, 'b_dt': b_dt, 'A_log': A_log, 'D_param': D_param, 'W_out': W_out}
    _L0_attn_in = _L0_attn_setup()

    def _L0_ffn_setup():
        import jax, jax.numpy as jnp
        import numpy as np
        DIM = 128
        DEPTH = 6
        HEADS = 16
        DIM_HEAD = 64
        WINDOW = 32
        INNER = HEADS * DIM_HEAD
        DIM_INNER = int(DIM * 4 * 2 / 3)
        QK_SCALE = 8.0

        def shift_tokens(t):
            a, s = jnp.split(t, 2, -1)
            s = jnp.pad(s, ((0, 0), (1, 0), (0, 0)))[:, :-1]
            return jnp.concatenate([a, s], -1)

        def l2norm(t):
            return t / jnp.maximum(jnp.linalg.norm(t, axis=-1, keepdims=True), 1e-12)

        def rotate_half(x):
            x1, x2 = jnp.split(x, 2, -1)
            return jnp.concatenate([-x2, x1], -1)

        def rotary_tables(n):
            half = jnp.arange(0, DIM_HEAD, 2, dtype=jnp.float32)
            inv_freq = 1.0 / 10000.0 ** (half / DIM_HEAD)
            t = jnp.arange(n, dtype=jnp.float32)
            freqs = t[:, None] * inv_freq[None, :]
            freqs = jnp.concatenate([freqs, freqs], -1)
            base_scale = (half + 0.4 * DIM_HEAD) / (1.4 * DIM_HEAD)
            power = (t - n // 2) / (WINDOW // 2)
            scale = base_scale[None, :] ** power[:, None]
            scale = jnp.concatenate([scale, scale], -1)
            return (freqs, scale)

        def local_attention(q, k, v):
            b, h, n, d = q.shape
            w = WINDOW
            nw = n // w
            bq = q.reshape(b, h, nw, w, d)
            bk = k.reshape(b, h, nw, w, d)
            bv = v.reshape(b, h, nw, w, d)

            def look(t):
                p = jnp.pad(t, ((0, 0), (0, 0), (1, 0), (0, 0), (0, 0)))
                return jnp.concatenate([p[:, :, :nw], p[:, :, 1:]], axis=3)
            bk2, bv2 = (look(bk), look(bv))
            seq = jnp.arange(n).reshape(nw, w)
            seq_p = jnp.pad(seq, ((1, 0), (0, 0)), constant_values=-1)
            jt = jnp.concatenate([seq_p[:nw], seq_p[1:]], axis=1)
            it = seq[:, :, None]
            jb = jt[:, None, :]
            mask = (it < jb) | (it > jb + w) | (jb == -1)
            sim = jnp.einsum('bhwie,bhwje->bhwij', bq, bk2) * QK_SCALE
            sim = jnp.where(mask, -jnp.finfo(sim.dtype).max, sim)
            attn = jax.nn.softmax(sim, -1)
            out = jnp.einsum('bhwij,bhwje->bhwie', attn, bv2)
            return out.reshape(b, h, n, d)

        def attn_layer(x, Wqkv, qs, ksc, Wo):
            b, n, _ = x.shape
            qkv = x @ Wqkv
            q, k, v = jnp.split(qkv, 3, -1)
            sh = lambda t: t.reshape(b, n, HEADS, DIM_HEAD).transpose(0, 2, 1, 3)
            q, k, v = (sh(q), sh(k), sh(v))
            q = l2norm(q) * qs
            k = l2norm(k) * ksc
            freqs, scale = rotary_tables(n)
            cos, sin = (jnp.cos(freqs), jnp.sin(freqs))
            q = q * cos * scale + rotate_half(q) * sin * scale
            inv = 1.0 / scale
            k = k * cos * inv + rotate_half(k) * sin * inv
            out = local_attention(q, k, v)
            out = out.transpose(0, 2, 1, 3).reshape(b, n, INNER)
            return out @ Wo

        def ffn_layer(x, g, bln, W1, b1, W2, b2):
            mu = x.mean(-1, keepdims=True)
            var = ((x - mu) ** 2).mean(-1, keepdims=True)
            xn = (x - mu) / jnp.sqrt(var + 1e-05) * g + bln
            hg = xn @ W1 + b1
            a, gate = jnp.split(hg, 2, -1)
            return a * jax.nn.gelu(gate, approximate=False) @ W2 + b2
        key = jax.random.key(seed)
        ks = jax.random.split(key, 8)
        B, N = (2, 256)
        init = lambda k, shape: jax.random.normal(k, shape, jnp.float32) * 0.02
        return {'x': jax.random.normal(ks[0], (B, N, DIM), jnp.float32), 'Wqkv': init(ks[1], (DEPTH, DIM, 3 * INNER)), 'q_scale': jnp.ones((DEPTH, DIM_HEAD), jnp.float32), 'k_scale': jnp.ones((DEPTH, DIM_HEAD), jnp.float32), 'Wo': init(ks[2], (DEPTH, INNER, DIM)), 'ln_g': jnp.ones((DEPTH, DIM), jnp.float32), 'ln_b': jnp.zeros((DEPTH, DIM), jnp.float32), 'W1': init(ks[3], (DEPTH, DIM, 2 * DIM_INNER)), 'b1': jnp.zeros((DEPTH, 2 * DIM_INNER), jnp.float32), 'W2': init(ks[4], (DEPTH, DIM_INNER, DIM)), 'b2': jnp.zeros((DEPTH, DIM), jnp.float32)}
    _L0_ffn_in = _L0_ffn_setup()

    def _L1_attn_setup():
        import math
        import jax, jax.numpy as jnp
        import numpy as np
        B, L, D_MODEL, N_HEADS = (4, 512, 128, 16)
        HEAD_DIM = D_MODEL // N_HEADS
        NUM_LANDMARKS = 128

        def _split_heads(t):
            b, l, _ = t.shape
            return t.reshape(b, l, N_HEADS, HEAD_DIM).transpose(0, 2, 1, 3)

        def _iterative_inv(mat, n_iter=6):
            I = jnp.eye(mat.shape[-1], dtype=mat.dtype)
            K = mat
            V = K.swapaxes(-1, -2) / jnp.max(jnp.sum(K, axis=-2))
            for _ in range(n_iter):
                KV = jnp.matmul(K, V)
                V = jnp.matmul(0.25 * V, 13.0 * I - jnp.matmul(KV, 15.0 * I - jnp.matmul(KV, 7.0 * I - KV)))
            return V
        key = jax.random.key(seed)
        ks = jax.random.split(key, 7)
        s = 1.0 / math.sqrt(D_MODEL)
        return {'x': jax.random.normal(ks[0], (B, L, D_MODEL), dtype=jnp.float32), 'Wq': jax.random.uniform(ks[1], (D_MODEL, D_MODEL), jnp.float32, -s, s), 'bq': jax.random.uniform(ks[2], (D_MODEL,), jnp.float32, -s, s), 'Wk': jax.random.uniform(ks[3], (D_MODEL, D_MODEL), jnp.float32, -s, s), 'bk': jax.random.uniform(ks[4], (D_MODEL,), jnp.float32, -s, s), 'Wv': jax.random.uniform(ks[5], (D_MODEL, D_MODEL), jnp.float32, -s, s), 'bv': jax.random.uniform(ks[6], (D_MODEL,), jnp.float32, -s, s)}
    _L1_attn_in = _L1_attn_setup()

    def _L1_ffn_setup():
        import jax, jax.numpy as jnp
        import numpy as np
        B, S, D, E, K = (4, 256, 128, 8, 2)
        H = 4 * D
        key = jax.random.key(seed)
        k0, k1, k2, k3 = jax.random.split(key, 4)
        x = jax.random.normal(k0, (B, S, D), dtype=jnp.float32)
        router_w = jax.random.normal(k1, (E, D), dtype=jnp.float32) * 0.02
        w1 = jax.random.normal(k2, (E, H, D), dtype=jnp.float32) * 0.02
        w2 = jax.random.normal(k3, (E, D, H), dtype=jnp.float32) * 0.02
        return {'x': x, 'router_w': router_w, 'w1': w1, 'w2': w2}
    _L1_ffn_in = _L1_ffn_setup()
    _d = {'L0_attn_x': _L0_attn_in['x'], 'L0_attn_W_in': _L0_attn_in['W_in'], 'L0_attn_conv_w': _L0_attn_in['conv_w'], 'L0_attn_conv_b': _L0_attn_in['conv_b'], 'L0_attn_W_x': _L0_attn_in['W_x'], 'L0_attn_w_dt': _L0_attn_in['w_dt'], 'L0_attn_b_dt': _L0_attn_in['b_dt'], 'L0_attn_A_log': _L0_attn_in['A_log'], 'L0_attn_D_param': _L0_attn_in['D_param'], 'L0_attn_W_out': _L0_attn_in['W_out'], 'L0_ffn_Wqkv': _L0_ffn_in['Wqkv'], 'L0_ffn_q_scale': _L0_ffn_in['q_scale'], 'L0_ffn_k_scale': _L0_ffn_in['k_scale'], 'L0_ffn_Wo': _L0_ffn_in['Wo'], 'L0_ffn_ln_g': _L0_ffn_in['ln_g'], 'L0_ffn_ln_b': _L0_ffn_in['ln_b'], 'L0_ffn_W1': _L0_ffn_in['W1'], 'L0_ffn_b1': _L0_ffn_in['b1'], 'L0_ffn_W2': _L0_ffn_in['W2'], 'L0_ffn_b2': _L0_ffn_in['b2'], 'L1_attn_Wq': _L1_attn_in['Wq'], 'L1_attn_bq': _L1_attn_in['bq'], 'L1_attn_Wk': _L1_attn_in['Wk'], 'L1_attn_bk': _L1_attn_in['bk'], 'L1_attn_Wv': _L1_attn_in['Wv'], 'L1_attn_bv': _L1_attn_in['bv'], 'L1_ffn_router_w': _L1_ffn_in['router_w'], 'L1_ffn_w1': _L1_ffn_in['w1'], 'L1_ffn_w2': _L1_ffn_in['w2']}
    _x0 = _d['L0_attn_x']
    _d['L0_attn_x'] = jax.random.normal(jax.random.fold_in(jax.random.key(seed), 1), (2, 1024, 128), dtype=_x0.dtype)
    del _x0
    return _d

def reference(L0_attn_x, L0_attn_W_in, L0_attn_conv_w, L0_attn_conv_b, L0_attn_W_x, L0_attn_w_dt, L0_attn_b_dt, L0_attn_A_log, L0_attn_D_param, L0_attn_W_out, L0_ffn_Wqkv, L0_ffn_q_scale, L0_ffn_k_scale, L0_ffn_Wo, L0_ffn_ln_g, L0_ffn_ln_b, L0_ffn_W1, L0_ffn_b1, L0_ffn_W2, L0_ffn_b2, L1_attn_Wq, L1_attn_bq, L1_attn_Wk, L1_attn_bk, L1_attn_Wv, L1_attn_bv, L1_ffn_router_w, L1_ffn_w1, L1_ffn_w2):

    def _L0_attn_ref(x, W_in, conv_w, conv_b, W_x, w_dt, b_dt, A_log, D_param, W_out):
        import jax, jax.numpy as jnp
        import numpy as np
        D_MODEL = 128
        D_STATE = 16
        D_CONV = 4
        EXPAND = 2
        D_INNER = D_MODEL * EXPAND
        B, L = (2, 128)
        d_inner = conv_w.shape[0]
        d_conv = conv_w.shape[2]
        d_state = (W_x.shape[0] - 1) // 2
        b, l, _ = x.shape
        xz = jnp.einsum('bld,ed->ble', x, W_in)
        xc, z = jnp.split(xz, 2, axis=-1)
        xc = xc.transpose(0, 2, 1)
        xc = jax.lax.conv_general_dilated(xc, conv_w, window_strides=(1,), padding=[(d_conv - 1, 0)], dimension_numbers=('NCH', 'OIH', 'NCH'), feature_group_count=d_inner)
        xc = xc + conv_b[None, :, None]
        xc = jax.nn.silu(xc.transpose(0, 2, 1))
        xp = jnp.einsum('bld,ed->ble', xc, W_x)
        delta = jax.nn.softplus(xp[..., -1:] * w_dt + b_dt)
        B_in = xp[..., :d_state]
        C = xp[..., d_state:2 * d_state]
        A = -jnp.exp(A_log)
        dA = jnp.exp(delta[..., None] * A)
        dBx = (delta * xc)[..., None] * B_in[:, :, None, :]

        def step(h, inp):
            dA_t, dBx_t, C_t = inp
            h = dA_t * h + dBx_t
            y_t = jnp.einsum('bdn,bn->bd', h, C_t)
            return (h, y_t)
        h0 = jnp.zeros((b, d_inner, d_state), dtype=x.dtype)
        _, ys = jax.lax.scan(step, h0, (dA.transpose(1, 0, 2, 3), dBx.transpose(1, 0, 2, 3), C.transpose(1, 0, 2)))
        y = ys.transpose(1, 0, 2) + D_param * xc
        y = y * jax.nn.silu(z)
        return jnp.einsum('ble,de->bld', y, W_out)

    def _L0_ffn_ref(x, Wqkv, q_scale, k_scale, Wo, ln_g, ln_b, W1, b1, W2, b2):
        import jax, jax.numpy as jnp
        import numpy as np
        DIM = 128
        DEPTH = 6
        HEADS = 16
        DIM_HEAD = 64
        WINDOW = 32
        INNER = HEADS * DIM_HEAD
        DIM_INNER = int(DIM * 4 * 2 / 3)
        QK_SCALE = 8.0

        def shift_tokens(t):
            a, s = jnp.split(t, 2, -1)
            s = jnp.pad(s, ((0, 0), (1, 0), (0, 0)))[:, :-1]
            return jnp.concatenate([a, s], -1)

        def l2norm(t):
            return t / jnp.maximum(jnp.linalg.norm(t, axis=-1, keepdims=True), 1e-12)

        def rotate_half(x):
            x1, x2 = jnp.split(x, 2, -1)
            return jnp.concatenate([-x2, x1], -1)

        def rotary_tables(n):
            half = jnp.arange(0, DIM_HEAD, 2, dtype=jnp.float32)
            inv_freq = 1.0 / 10000.0 ** (half / DIM_HEAD)
            t = jnp.arange(n, dtype=jnp.float32)
            freqs = t[:, None] * inv_freq[None, :]
            freqs = jnp.concatenate([freqs, freqs], -1)
            base_scale = (half + 0.4 * DIM_HEAD) / (1.4 * DIM_HEAD)
            power = (t - n // 2) / (WINDOW // 2)
            scale = base_scale[None, :] ** power[:, None]
            scale = jnp.concatenate([scale, scale], -1)
            return (freqs, scale)

        def local_attention(q, k, v):
            b, h, n, d = q.shape
            w = WINDOW
            nw = n // w
            bq = q.reshape(b, h, nw, w, d)
            bk = k.reshape(b, h, nw, w, d)
            bv = v.reshape(b, h, nw, w, d)

            def look(t):
                p = jnp.pad(t, ((0, 0), (0, 0), (1, 0), (0, 0), (0, 0)))
                return jnp.concatenate([p[:, :, :nw], p[:, :, 1:]], axis=3)
            bk2, bv2 = (look(bk), look(bv))
            seq = jnp.arange(n).reshape(nw, w)
            seq_p = jnp.pad(seq, ((1, 0), (0, 0)), constant_values=-1)
            jt = jnp.concatenate([seq_p[:nw], seq_p[1:]], axis=1)
            it = seq[:, :, None]
            jb = jt[:, None, :]
            mask = (it < jb) | (it > jb + w) | (jb == -1)
            sim = jnp.einsum('bhwie,bhwje->bhwij', bq, bk2) * QK_SCALE
            sim = jnp.where(mask, -jnp.finfo(sim.dtype).max, sim)
            attn = jax.nn.softmax(sim, -1)
            out = jnp.einsum('bhwij,bhwje->bhwie', attn, bv2)
            return out.reshape(b, h, n, d)

        def attn_layer(x, Wqkv, qs, ksc, Wo):
            b, n, _ = x.shape
            qkv = x @ Wqkv
            q, k, v = jnp.split(qkv, 3, -1)
            sh = lambda t: t.reshape(b, n, HEADS, DIM_HEAD).transpose(0, 2, 1, 3)
            q, k, v = (sh(q), sh(k), sh(v))
            q = l2norm(q) * qs
            k = l2norm(k) * ksc
            freqs, scale = rotary_tables(n)
            cos, sin = (jnp.cos(freqs), jnp.sin(freqs))
            q = q * cos * scale + rotate_half(q) * sin * scale
            inv = 1.0 / scale
            k = k * cos * inv + rotate_half(k) * sin * inv
            out = local_attention(q, k, v)
            out = out.transpose(0, 2, 1, 3).reshape(b, n, INNER)
            return out @ Wo

        def ffn_layer(x, g, bln, W1, b1, W2, b2):
            mu = x.mean(-1, keepdims=True)
            var = ((x - mu) ** 2).mean(-1, keepdims=True)
            xn = (x - mu) / jnp.sqrt(var + 1e-05) * g + bln
            hg = xn @ W1 + b1
            a, gate = jnp.split(hg, 2, -1)
            return a * jax.nn.gelu(gate, approximate=False) @ W2 + b2
        for i in range(DEPTH):
            x = attn_layer(shift_tokens(x), Wqkv[i], q_scale[i], k_scale[i], Wo[i]) + x
            x = ffn_layer(shift_tokens(x), ln_g[i], ln_b[i], W1[i], b1[i], W2[i], b2[i]) + x
        return x

    def _L1_attn_ref(x, Wq, bq, Wk, bk, Wv, bv):
        import math
        import jax, jax.numpy as jnp
        import numpy as np
        B, L, D_MODEL, N_HEADS = (4, 512, 128, 16)
        HEAD_DIM = D_MODEL // N_HEADS
        NUM_LANDMARKS = 128

        def _split_heads(t):
            b, l, _ = t.shape
            return t.reshape(b, l, N_HEADS, HEAD_DIM).transpose(0, 2, 1, 3)

        def _iterative_inv(mat, n_iter=6):
            I = jnp.eye(mat.shape[-1], dtype=mat.dtype)
            K = mat
            V = K.swapaxes(-1, -2) / jnp.max(jnp.sum(K, axis=-2))
            for _ in range(n_iter):
                KV = jnp.matmul(K, V)
                V = jnp.matmul(0.25 * V, 13.0 * I - jnp.matmul(KV, 15.0 * I - jnp.matmul(KV, 7.0 * I - KV)))
            return V
        Q = _split_heads(x @ Wq.T + bq)
        K = _split_heads(x @ Wk.T + bk)
        V = _split_heads(x @ Wv.T + bv)
        b, h, l, d = Q.shape
        scale = 1.0 / math.sqrt(math.sqrt(HEAD_DIM))
        Q = Q * scale
        K = K * scale
        seg = l // NUM_LANDMARKS
        Q_lm = Q.reshape(b, h, NUM_LANDMARKS, seg, d).mean(axis=-2)
        K_lm = K.reshape(b, h, NUM_LANDMARKS, seg, d).mean(axis=-2)
        kernel_1 = jax.nn.softmax(jnp.einsum('bhld,bhmd->bhlm', Q, K_lm), axis=-1)
        kernel_2 = jax.nn.softmax(jnp.einsum('bhmd,bhnd->bhmn', Q_lm, K_lm), axis=-1)
        kernel_3 = jax.nn.softmax(jnp.einsum('bhmd,bhld->bhml', Q_lm, K), axis=-1)
        X = jnp.matmul(jnp.matmul(kernel_1, _iterative_inv(kernel_2)), jnp.matmul(kernel_3, V))
        out = X.transpose(0, 2, 1, 3).reshape(b, l, h * d)
        return out

    def _L1_ffn_ref(x, router_w, w1, w2):
        import jax, jax.numpy as jnp
        import numpy as np
        B, S, D, E, K = (4, 256, 128, 8, 2)
        H = 4 * D
        b, s, d = x.shape
        e = router_w.shape[0]
        logits = jnp.einsum('bsd,ed->bse', x, router_w)
        probs = jax.nn.softmax(logits, axis=-1)
        topk_vals, topk_idx = jax.lax.top_k(probs, K)
        x_flat = x.reshape(b * s, d)
        vals = topk_vals.reshape(b * s, K)
        idx = topk_idx.reshape(b * s, K)
        out = jnp.zeros_like(x_flat)
        for eid in range(e):
            w = jnp.sum(jnp.where(idx == eid, vals, jnp.zeros((), x.dtype)), axis=-1)
            h = jax.nn.gelu(x_flat @ w1[eid].T, approximate=False)
            y = h @ w2[eid].T
            out = out + w[:, None] * y
        return out.reshape(b, s, d)
    x = L0_attn_x
    x = x + _layernorm(_L0_attn_ref(_layernorm(x, axis=-1), L0_attn_W_in, L0_attn_conv_w, L0_attn_conv_b, L0_attn_W_x, L0_attn_w_dt, L0_attn_b_dt, L0_attn_A_log, L0_attn_D_param, L0_attn_W_out), axis=-1)
    x = x + _layernorm(_L0_ffn_ref(_layernorm(x, axis=-1), L0_ffn_Wqkv, L0_ffn_q_scale, L0_ffn_k_scale, L0_ffn_Wo, L0_ffn_ln_g, L0_ffn_ln_b, L0_ffn_W1, L0_ffn_b1, L0_ffn_W2, L0_ffn_b2), axis=-1)
    x = x + _layernorm(_L1_attn_ref(_layernorm(x, axis=-1), L1_attn_Wq, L1_attn_bq, L1_attn_Wk, L1_attn_bk, L1_attn_Wv, L1_attn_bv), axis=-1)
    x = x + _layernorm(_L1_ffn_ref(_layernorm(x, axis=-1), L1_ffn_router_w, L1_ffn_w1, L1_ffn_w2), axis=-1)
    return x

_drawn_inputs = setup_inputs


def setup_inputs(seed=0):
    import zlib

    import numpy as np

    out = dict(_drawn_inputs(seed))
    spreads = {'L0_attn_conv_b': (0.0, 0.1),
     'L0_attn_D_param': (1.0, 0.2),
     'L0_ffn_q_scale': (1.0, 0.55),
     'L0_ffn_k_scale': (1.0, 0.6),
     'L0_ffn_ln_g': (1.0, 0.6),
     'L0_ffn_ln_b': (0.0, 0.549),
     'L0_ffn_b1': (0.0, 0.1),
     'L0_ffn_b2': (0.0, 0.1)}
    factors = {'L0_attn_w_dt': 23.47, 'L1_attn_bk': 64.0}
    for name, (base, spread) in spreads.items():
        noise = np.random.default_rng([zlib.crc32(name.encode()), seed]).standard_normal(out[name].shape)
        drawn = base * np.exp(spread * noise) if base else spread * noise
        out[name] = jnp.asarray(drawn.astype(out[name].dtype))
    for name, factor in factors.items():
        out[name] = (out[name] * factor).astype(out[name].dtype)
    return out
```

```python
from contextlib import ExitStack

import numpy as np
import concourse.bass as bass
from concourse import mybir

FP32 = mybir.dt.float32
BF16 = mybir.dt.bfloat16
ACT = mybir.ActivationFunctionType
ALU = mybir.AluOpType
AX = mybir.AxisListType

P = 128
B, L = 2, 1024
T = B * L
NT = T // P
NB = L // P
CH = 512
EPS = 1e-5

DI = 256
DC = DI // P
NS = 16
TAPS = 4


class Chain:

    def __init__(self, engine, sem, count=0):
        self.engine, self.sem, self.count = engine, sem, count

    def __call__(self, step):
        self.count += 1
        step.then_inc(self.sem, 1)
        self.engine.wait_ge(self.sem, self.count)


class NormSemaphores:

    def __init__(self, nc, sems):
        self.sems = [sems.enter_context(nc.semaphore(f"n_{n}")) for n in
                     ("var_ready", "std_ready", "z_ready", "x_ready", "turned", "copied", "stored", "chain")]
        self.stds = self.fours = self.chained = 0


def norm_stage(nc, shared, name, X, Y, ZT, ident, store=None, Z=None):
    with ExitStack() as ctx:
        st = ctx.enter_context(nc.sbuf_tensor(f"{name}_stats", [P, NT, 6], FP32))
        mv = ctx.enter_context(nc.sbuf_tensor(f"{name}_mean_var", [P, NT, 2], FP32))
        sd = ctx.enter_context(nc.sbuf_tensor(f"{name}_std", [P, NT], FP32))
        rstd = ctx.enter_context(nc.sbuf_tensor(f"{name}_rstd", [P, NT], FP32))
        st2 = ctx.enter_context(nc.sbuf_tensor(f"{name}_stats2", [P, NT, 6], FP32))
        mv2 = ctx.enter_context(nc.sbuf_tensor(f"{name}_mean_var2", [P, NT, 2], FP32))
        sd2 = ctx.enter_context(nc.sbuf_tensor(f"{name}_std2", [P, NT], FP32))
        rstd2 = ctx.enter_context(nc.sbuf_tensor(f"{name}_rstd2", [P, NT], FP32))
        yn = ctx.enter_context(nc.sbuf_tensor(f"{name}_normed", [P, NT, P], FP32))
        if Z is None:
            Z = ctx.enter_context(nc.sbuf_tensor(f"{name}_normed2", [P, NT, P], FP32))
        ps = ctx.enter_context(nc.psum_tensor(f"{name}_ps", [P, 4, CH], FP32))
        var_ready, std_ready, z_ready, x_ready, turned, copied, stored, chain_sem = shared.sems
        stds, fours, chained = shared.stds, shared.fours, shared.chained
        block = ctx.enter_context(nc.Block())
        passes = 1 if Y is not None else 0

        @block.vector
        def _(dve):
            link = Chain(dve, chain_sem, chained)

            def normalise(src, out, stats, mean_var, std, recip, turn, ready):
                for t in range(NT):
                    last = nc.vector.bn_stats(stats[:, t, :], src[:, t, :])
                link(last)
                for t in range(NT):
                    last = nc.vector.bn_aggr(mean_var[:, t, :], stats[:, t, :])
                link(last)
                nc.vector.tensor_scalar(std[:], mean_var[:, :, 1], EPS, None, ALU.add).then_inc(var_ready, 1)
                dve.wait_ge(std_ready, stds + turn)
                link(nc.vector.reciprocal(recip[:], std[:]))
                for t in range(NT):
                    step = nc.vector.tensor_scalar(out[:, t, :], src[:, t, :], mean_var[:, t, 0:1], recip[:, t:t + 1],
                                                   ALU.subtract, ALU.mult)
                    if ready is not None and t % 4 == 3:
                        step.then_inc(ready, 1)
                return step

            if Y is not None:
                link(normalise(Y, yn, st, mv, sd, rstd, 1, None))
                step = nc.vector.tensor_tensor(X[:], X[:], yn[:], ALU.add)
                if store is not None:
                    step.then_inc(x_ready, 1)
                else:
                    link(step)
            if store is None:
                normalise(X, Z, st2, mv2, sd2, rstd2, passes + 1, z_ready)
            shared.chained = link.count

        @block.scalar
        def _(act):
            if Y is not None:
                act.wait_ge(var_ready, stds + 1)
                nc.scalar.activation(sd[:], sd[:], ACT.Sqrt).then_inc(std_ready, 1)
            if store is None:
                act.wait_ge(var_ready, stds + passes + 1)
                nc.scalar.activation(sd2[:], sd2[:], ACT.Sqrt).then_inc(std_ready, 1)
                for g in range(4):
                    act.wait_ge(turned, fours + g + 1)
                    nc.scalar.activation(ZT[:, CH * g:CH * (g + 1)], ps[:, g, :], ACT.Copy).then_inc(copied, 1)

        @block.tensor
        def _(pe):
            if store is None:
                for g in range(4):
                    pe.wait_ge(z_ready, fours + g + 1)
                    for t in range(4 * g, 4 * g + 4):
                        step = nc.tensor.transpose(ps[:, g, P * (t % 4):P * (t % 4) + P], Z[:, t, :], ident[:])
                    step.then_inc(turned, 1)

        @block.sync
        def _(sp):
            if store is not None:
                sp.wait_ge(x_ready, 1)
                sp.dma_start(store, X[:]).then_inc(stored, 16)
                sp.wait_ge(stored, 16)

        shared.stds += passes + (store is None)
        shared.fours += 4 * (store is None)


def mamba_stage(nc, sems, XT, Y, ident, w, dram):
    with ExitStack() as ctx:
        def sb(name, shape, dt=FP32):
            return ctx.enter_context(nc.sbuf_tensor(f"m_{name}", shape, dt))

        def sem(name):
            return sems.enter_context(nc.semaphore(f"m_{name}"))

        w_in, w_x, w_out, conv_w, conv_b, w_dt, b_dt, a_log, d_par, sel = (
            sb("w_in", [P, 4 * P]), sb("w_x", [P, DC, 2 * NS + 1]), sb("w_out", [P, DC, P]), sb("conv_w", [P, DC, TAPS]),
            sb("conv_b", [P, DC]), sb("w_dt", [P, DC]), sb("b_dt", [P, DC]), sb("a_log", [P, DC, NS]), sb("d_par", [P, DC]),
            sb("sel", [96, 2 * NS, P], BF16))
        dt_col = sb("dt_col", [P, DC, P])
        A = sb("A", [P, DC, NS])
        pad = sb("pad", [P, DC, B, TAPS - 1 + L])
        conv = sb("conv", [P, DC, B, L])
        xc = sb("xc", [P, DC, B, L])
        zs = sb("zs", [P, DC, B, L])
        delta = sb("delta", [P, DC, B, L])
        du = conv
        ex, u = pad, sb("u", [P, DC, B, L])
        bc = sb("bc", [32, 3, T], BF16)
        rest = sb("rest", [32, 2, T])
        stack = sb("stack", [96, T], BF16)
        dA = sb("dA", [P, 2, L])
        dbx = sb("dbx", [P, 2, L])
        h = sb("h", [P, 2, L])
        c_sb = sb("c_sb", [P, 2, L])
        hc = sb("hc", [P, 2, L])
        yT = u
        ps = ctx.enter_context(nc.psum_tensor("m_ps", [P, 8, CH], FP32))
        loaded, ready0, xz, xz_used, conved, silued = sem("loaded"), sem("ready0"), sem("xz"), sem("xz_used"), sem("conved"), sem("silued")
        bc_ps, dt_ps, split, stacked, dt_used, soft, softed = sem("bc_ps"), sem("dt_ps"), sem("split"), sem("stacked"), sem("dt_used"), sem("soft"), sem("softed")
        b_ready, c_ready, c_copied, dA_ready, dbx_done, scanned, hc_done, y_acc, y_used = (
            sem("b_ready"), sem("c_ready"), sem("c_copied"), sem("dA_ready"), sem("dbx_done"), sem("scanned"), sem("hc_done"),
            sem("y_acc"), sem("y_used"))
        out_ps, out_done, du_done, chain_sem, achain_sem = sem("out_ps"), sem("out_done"), sem("du_done"), sem("chain"), sem("achain")
        block = ctx.enter_context(nc.Block())
        LOADS = [(w_in, dram["w_in"]), (w_x, dram["w_x"]), (w_out, dram["w_out"]), (conv_w, dram["conv_w"]), (conv_b, dram["conv_b"]),
                 (w_dt, dram["w_dt"]), (b_dt, dram["b_dt"]), (a_log, dram["a_log"]), (d_par, dram["d_par"]), (sel, dram["sel"])]
        units = [(b, n, dc) for b in range(B) for n in range(NS) for dc in range(DC)]

        @block.sync
        def _(sp):
            for dst, src in LOADS:
                sp.dma_start(dst[:], src).then_inc(loaded, 16)

        @block.tensor
        def _(pe):
            pe.wait_ge(loaded, 16 * len(LOADS))
            for i in range(16):
                c, e = i // 4, i % 4
                if i >= 8:
                    pe.wait_ge(xz_used, i - 7)
                nc.tensor.matmul(ps[:, i % 8, :], w_in[:, P * e:P * e + P], XT[:, CH * c:CH * c + CH], start=True,
                                 stop=True).then_inc(xz, 1)
            pe.wait_ge(silued, DC)
            pe.wait_ge(xz_used, 16)
            pe.wait_ge(ready0, 1)
            for c in range(4):
                b, o = c // 2, CH * (c % 2)
                for dc in range(DC):
                    step = nc.tensor.matmul(ps[0:32, c, :], w_x[:, dc, 0:32], xc[:, dc, b, o:o + CH], start=dc == 0, stop=dc == DC - 1)
                step.then_inc(bc_ps, 1)
            for c in range(4):
                b, o = c // 2, CH * (c % 2)
                for dc in range(DC):
                    step = nc.tensor.matmul(ps[:, 4 + c, :], dt_col[:, dc, :], xc[:, dc, b, o:o + CH], start=dc == 0, stop=dc == DC - 1)
                step.then_inc(dt_ps, 1)
            pe.wait_ge(stacked, 3)
            pe.wait_ge(dt_used, 4)
            pe.wait_ge(split, 1)

            def spread(v):
                b, n = divmod(v, NS)
                if v >= 1:
                    pe.wait_ge(dbx_done, DC * v)
                for i in range(2):
                    step = nc.tensor.matmul(ps[:, 4 + i, :], sel[:, n, :], stack[:, L * b + CH * i:L * b + CH * i + CH], start=True, stop=True)
                step.then_inc(b_ready, 1)
                if v >= 1:
                    pe.wait_ge(c_copied, v)
                for i in range(2):
                    step = nc.tensor.matmul(ps[:, 6 + i, :], sel[:, NS + n, :], stack[:, L * b + CH * i:L * b + CH * i + CH], start=True, stop=True)
                step.then_inc(c_ready, 1)

            spread(0)
            for v in range(B * NS):
                b, n = divmod(v, NS)
                if v + 1 < B * NS:
                    spread(v + 1)
                if n == 0 and b:
                    pe.wait_ge(y_used, DC * b)
                for dc in range(DC):
                    pe.wait_ge(hc_done, DC * v + dc + 1)
                    for i in range(2):
                        step = nc.tensor.matmul(ps[:, 2 * dc + i, :], ident[:], hc[:, dc, CH * i:CH * i + CH], start=n == 0, stop=n == NS - 1)
                    step.then_inc(y_acc, 1)
            pe.wait_ge(y_used, DC * B)
            for t in range(NT):
                b, o = t // NB, P * (t % NB)
                for dc in range(DC):
                    step = nc.tensor.matmul(ps[:, t // 4, P * (t % 4):P * (t % 4) + P], yT[:, dc, b, o:o + P], w_out[:, dc, :],
                                            start=dc == 0, stop=dc == DC - 1)
                if t % 4 == 3:
                    step.then_inc(out_ps, 1)

        @block.scalar
        def _(act):
            act.wait_ge(loaded, 16 * len(LOADS))
            link = Chain(act, achain_sem)
            for i in range(16):
                c, e = i // 4, i % 4
                b, o = c // 2, CH * (c % 2)
                act.wait_ge(xz, i + 1)
                if e < 2:
                    step = nc.scalar.activation(pad[:, e, b, TAPS - 1 + o:TAPS - 1 + o + CH], ps[:, i % 8, :], ACT.Copy)
                else:
                    step = nc.scalar.activation(zs[:, e - 2, b, o:o + CH], ps[:, i % 8, :], ACT.Silu)
                step.then_inc(xz_used, 1)
            for dc in range(DC):
                act.wait_ge(conved, dc + 1)
                nc.scalar.activation(xc[:, dc], conv[:, dc], ACT.Silu).then_inc(silued, 1)
            link(nc.scalar.activation(A[:], a_log[:], ACT.Exp))
            act.wait_ge(conved, DC)
            for dc in range(DC):
                for c in range(4):
                    b, o = c // 2, CH * (c % 2)
                    act.wait_ge(dt_ps, c + 1)
                    nc.scalar.activation(ex[:, dc, b, o:o + CH], ps[:, 4 + c, :], ACT.Abs, bias=b_dt[:, dc:dc + 1], scale=w_dt[:, dc:dc + 1])
                    step = nc.scalar.activation(delta[:, dc, b, o:o + CH], ps[:, 4 + c, :], ACT.Relu, bias=b_dt[:, dc:dc + 1],
                                                scale=w_dt[:, dc:dc + 1])
                    if dc == DC - 1:
                        step.then_inc(dt_used, 1)
            act.wait_ge(dt_used, 4)
            for dc in range(DC):
                nc.scalar.activation(u[:, dc], ex[:, dc, :, 0:L], ACT.Exp, scale=-1.0).then_inc(soft, 1)
            for i in range(3):
                if i == 0:
                    act.wait_ge(split, 1)
                nc.scalar.activation(stack[32 * i:32 * i + 32, :], bc[:, i, :], ACT.Copy).then_inc(stacked, 1)
            for dc in range(DC):
                act.wait_ge(softed, dc + 1)
                nc.scalar.activation(ex[:, dc, :, 0:L], ex[:, dc, :, 0:L], ACT.Ln).then_inc(soft, 1)
            act.wait_ge(du_done, DC)
            for v in range(B * NS):
                b, n = divmod(v, NS)
                for dc in range(DC):
                    k = DC * v + dc
                    if k >= 2:
                        act.wait_ge(scanned, k - 1)
                    nc.scalar.activation(dA[:, dc], delta[:, dc, b], ACT.Exp, scale=A[:, dc, n:n + 1]).then_inc(dA_ready, 1)
                act.wait_ge(c_ready, v + 1)
                if v >= 2:
                    act.wait_ge(hc_done, DC * (v - 1))
                nc.scalar.activation(c_sb[:, v % 2], ps[:, 6:8, :].rearrange("p a c -> p (a c)"), ACT.Copy).then_inc(c_copied, 1)
            for g in range(4):
                act.wait_ge(out_ps, g + 1)
                nc.scalar.activation(Y[:, 4 * g:4 * g + 4, :].rearrange("p a c -> p (a c)"), ps[:, g, :], ACT.Copy).then_inc(out_done, 1)

        @block.vector
        def _(dve):
            link = Chain(dve, chain_sem)
            nc.vector.memset(pad[:, :, :, 0:TAPS - 1], 0.0)
            dve.wait_ge(loaded, 16 * len(LOADS))
            nc.vector.tensor_copy(dt_col[:], w_x[:, :, 2 * NS:2 * NS + 1].to_broadcast([P, DC, P])).then_inc(ready0, 1)
            dve.wait_ge(ready0, 1)
            dve.wait_ge(xz_used, 16)
            for k in range(TAPS):
                for dc in range(DC):
                    src = pad[:, dc, :, k:k + L]
                    if k == 0:
                        step = nc.vector.tensor_scalar(conv[:, dc], src, conv_w[:, dc, 0:1], conv_b[:, dc:dc + 1], ALU.mult, ALU.add)
                    else:
                        step = nc.vector.scalar_tensor_tensor(conv[:, dc], src, conv_w[:, dc, k:k + 1], conv[:, dc], ALU.mult, ALU.add)
                    if k == TAPS - 1:
                        step.then_inc(conved, 1)
                if k < TAPS - 1:
                    link(step)
            dve.wait_ge(bc_ps, 4)
            src = ps[0:32, 0:4, :].rearrange("p a c -> p (a c)")
            link(nc.vector.tensor_copy(bc[:, 0, :], src))
            link(nc.vector.tensor_tensor(rest[:, 0, :], src, bc[:, 0, :], ALU.subtract))
            link(nc.vector.tensor_copy(bc[:, 1, :], rest[:, 0, :]))
            link(nc.vector.tensor_tensor(rest[:, 1, :], rest[:, 0, :], bc[:, 1, :], ALU.subtract))
            nc.vector.tensor_copy(bc[:, 2, :], rest[:, 1, :]).then_inc(split, 1)
            for dc in range(DC):
                dve.wait_ge(soft, dc + 1)
                link(nc.vector.tensor_scalar(ex[:, dc, :, 0:L], u[:, dc], 1.0, None, ALU.add))
                link(nc.vector.scalar_tensor_tensor(delta[:, dc], u[:, dc], 1.0, delta[:, dc], ALU.mult, ALU.add))
                nc.vector.tensor_scalar(u[:, dc], ex[:, dc, :, 0:L], 1.0, None, ALU.subtract).then_inc(softed, 1)
            dve.wait_ge(softed, DC)
            link(nc.vector.tensor_scalar(A[:], A[:], -1.0, None, ALU.mult))
            for dc in range(DC):
                dve.wait_ge(soft, DC + dc + 1)
                link(nc.vector.tensor_tensor(delta[:, dc], delta[:, dc], u[:, dc], ALU.subtract))
                link(nc.vector.tensor_tensor(delta[:, dc], delta[:, dc], ex[:, dc, :, 0:L], ALU.add))
                nc.vector.tensor_tensor(du[:, dc], delta[:, dc], xc[:, dc], ALU.mult).then_inc(du_done, 1)
            dve.wait_ge(du_done, DC)

            def times_b(k):
                b, n, dc = units[k]
                if dc == 0:
                    dve.wait_ge(b_ready, k // DC + 1)
                if k >= 2:
                    dve.wait_ge(scanned, k - 1)
                nc.vector.tensor_tensor(dbx[:, dc], du[:, dc, b], ps[:, 4:6, :].rearrange("p a c -> p (a c)"), ALU.mult)\
                    .then_inc(dbx_done, 1)

            times_b(0)
            for k, (b, n, dc) in enumerate(units):
                if k + 1 < len(units):
                    times_b(k + 1)
                dve.wait_ge(dA_ready, k + 1)
                dve.wait_ge(dbx_done, k + 1)
                if k >= 2:
                    dve.wait_ge(hc_done, k - 1)
                nc.vector.tensor_tensor_scan(h[:, dc], dA[:, dc], dbx[:, dc], 0.0, ALU.mult, ALU.add).then_inc(scanned, 1)
                if n == NS - 1:
                    dve.wait_ge(y_acc, k + 1)
                    link(nc.vector.scalar_tensor_tensor(yT[:, dc, b], xc[:, dc, b], d_par[:, dc:dc + 1],
                                                        ps[:, 2 * dc:2 * dc + 2, :].rearrange("p a c -> p (a c)"), ALU.mult, ALU.add))
                    nc.vector.tensor_tensor(yT[:, dc, b], yT[:, dc, b], zs[:, dc, b], ALU.mult).then_inc(y_used, 1)

        @block.gpsimd
        def _(pool):
            for k, (b, n, dc) in enumerate(units):
                pool.wait_ge(scanned, k + 1)
                if dc == 0:
                    pool.wait_ge(c_copied, k // DC + 1)
                if k >= 2:
                    pool.wait_ge(y_acc, k - 1)
                nc.gpsimd.tensor_tensor(hc[:, dc], h[:, dc], c_sb[:, (k // DC) % 2], ALU.mult).then_inc(hc_done, 1)

DEPTH = 6
H2, D2 = 16, 64
INNER = H2 * D2
HP = H2 // 2
WIN = 32
NW = P // WIN
FF = 341
FC = 3
FROWS = [128, 128, FF - 256]
QK_SCALE = 8.0
DVE_LINKS = 4 * NT + 4


def local_stage(nc, sems, XT, Y, ident, dram):
    with ExitStack() as ctx:
        def sb(name, shape, dt=FP32):
            return ctx.enter_context(nc.sbuf_tensor(f"l_{name}", shape, dt))

        def sem(name):
            return sems.enter_context(nc.semaphore(f"l_{name}"))

        x = XT
        wqk, wv, wo = sb("wqk", [P, 2 * INNER]), sb("wv", [P, 2, HP * D2]), sb("wo", [P, HP, P])
        w1, w2, vec = sb("w1", [P, 2 * FF]), sb("w2", [P, FC, P]), sb("vec", [P, 9])
        scales, base, table = sb("scales", [P, 4, 1, D2]), sb("base", [P, 4, NB, D2]), sb("table", [P, 4, NB, D2])
        mask = sb("mask", [P, 2, 1, 2 * WIN])
        mean_w, eps, ln256 = sb("mean_w", [P, P]), sb("eps", [P, 1]), sb("ln256", [P, 1])
        xs = sb("xs", [P, B, WIN + L])
        raw, sq, tc, ts, qk = (sb(n, [P, 2, H2, D2]) for n in ("raw", "sq", "tc", "ts", "qk"))
        ssq, lnq, rn = sb("ssq", [P, 2, H2, 1]), sb("lnq", [P, 2 * H2]), sb("rn", [P, 2, H2, 1])
        qT, kT, vw = sb("qT", [P, HP, P]), sb("kT", [P, 2, HP, WIN + P]), sb("vw", [P, 2, NW, HP * D2])
        E, PT = sb("E", [P, H2, 2 * WIN]), sb("PT", [P, HP, P])
        mx, rs = sb("mx", [P, H2, 1]), sb("rs", [P, H2, 1])
        O, OT = sb("O", [P, H2, D2]), sb("OT", [P, HP, P])
        cen, csq, rstd, xn = (sb(n, [P, 2, CH]) for n in ("cen", "csq", "rstd", "xn"))
        gl, hb = sb("gl", [P, 2, CH]), sb("hb", [P, 2, FC, CH])
        ps = ctx.enter_context(nc.psum_tensor("l_ps", [P, 8, CH], FP32))

        def slot(i):
            return ps[:, 2 * i:2 * i + 2, :].rearrange("p a c -> p (a c)")

        consts_in, wqk_in, wv_in, wo_in, w1_in, w2_in, vec_in, scales_in, table_ready = (
            sem("consts_in"), sem("wqk_in"), sem("wv_in"), sem("wo_in"), sem("w1_in"), sem("w2_in"), sem("vec_in"), sem("scales_in"),
            sem("table_ready"))
        consts_set, k_zero, xa_ready, xf_ready = sem("consts_set"), sem("k_zero"), sem("xa_ready"), sem("xf_ready")
        q_ps, k_ps, v0_ps, v1_ps, pt_ps, o_ps, qt_ps, kt_ps, ot_ps, wo_ps, s_ps = (
            sem(n) for n in ("q_ps", "k_ps", "v0_ps", "v1_ps", "pt_ps", "o_ps", "qt_ps", "kt_ps", "ot_ps", "wo_ps", "s_ps"))
        q_raw, k_raw, sq_done, v0_done, v1_done, pt_done, rn_half, rn_done, qt_done, kt_done, ot_done, exp_done = (
            sem(n) for n in ("q_raw", "k_raw", "sq_done", "v0_done", "v1_done", "pt_done", "rn_half", "rn_done", "qt_done", "kt_done", "ot_done",
                             "exp_done"))
        masked, sub_done, rotq, rotk, ssq_done, qn_done, kn_done, o_done, wo_used, addq, addk = (
            sem(n) for n in ("masked", "sub_done", "rotq", "rotk", "ssq_done", "qn_done", "kn_done", "o_done", "wo_used", "addq", "addk"))
        m_ps, cen_done, csq_done, var_ps, lv_done, rstd_done, xn_done, y_ps, y_used = (
            sem(n) for n in ("m_ps", "cen_done", "csq_done", "var_ps", "lv_done", "rstd_done", "xn_done", "y_ps", "y_used"))
        ag_ps, gl_done, h_done = sem("ag_ps"), sem("gl_done"), sem("h_done")
        chain_sem, out_ps, out_done, pe_passed, pool_passed = sem("chain"), sem("out_ps"), sem("out_done"), sem("pe_passed"), sem("pool_passed")
        block = ctx.enter_context(nc.Block())

        @block.sync
        def _(sp):
            for dst, name in ((base, "base"), (mask, "mask")):
                sp.dma_start(dst[:], dram[name]).then_inc(consts_in, 16)
            with sp.Fori(0, DEPTH) as i:
                sp.wait_ge(table_ready, i + 1)
                sp.dma_start(scales[:], dram["scales"][bass.ds(i, 1)].rearrange("a p k o d -> p (a k) o d")).then_inc(scales_in, 16)
                sp.wait_ge(v1_ps, i * 16 + 1)
                sp.dma_start(wqk[:], dram["wqk"][bass.ds(i, 1)].rearrange("a p n -> p (a n)")).then_inc(wqk_in, 16)
                sp.dma_start(wv[:], dram["wvl"][bass.ds(i, 1)].rearrange("a p k n -> p (a k) n")).then_inc(wv_in, 16)
                sp.wait_ge(wo_ps, i * 16 + 1)
                sp.dma_start(wo[:], dram["wo"][bass.ds(i, 1)].rearrange("a p k n -> p (a k) n")).then_inc(wo_in, 16)
                sp.wait_ge(y_used, i * 4 + 1)
                sp.dma_start(w1[:], dram["w1l"][bass.ds(i, 1)].rearrange("a p n -> p (a n)")).then_inc(w1_in, 16)
                sp.dma_start(w2[:], dram["w2l"][bass.ds(i, 1)].rearrange("a p k n -> p (a k) n")).then_inc(w2_in, 16)
                sp.dma_start(vec[:], dram["vec"][bass.ds(i, 1)].rearrange("a p n -> p (a n)")).then_inc(vec_in, 16)

        @block.gpsimd
        def _(pool):
            nc.gpsimd.memset(xs[:], 0.0).then_inc(consts_set, 1)
            nc.gpsimd.memset(kT[:, 0, :, 0:WIN], 0.0).then_inc(k_zero, 1)
            nc.gpsimd.memset(mean_w[:], 1.0 / P).then_inc(consts_set, 1)
            nc.gpsimd.memset(eps[:], EPS).then_inc(consts_set, 1)
            nc.gpsimd.memset(ln256[:], float(np.log(256.0))).then_inc(table_ready, 1)
            pool.wait_ge(consts_in, 32)
            with pool.Fori(0, DEPTH) as i:
                pool.wait_ge(scales_in, i * 16 + 16)
                for k in range(4):
                    step = nc.gpsimd.tensor_tensor(table[:, k], base[:, k], scales[:, k].to_broadcast([P, NB, D2]), ALU.mult)
                step.then_inc(table_ready, 1)
                for b in range(B):
                    for t in range(NB):
                        n = NB * b + t
                        for half, rot, add in ((0, rotq, addq), (1, rotk, addk)):
                            pool.wait_ge(rot, i * 16 + n + 1)
                            nc.gpsimd.tensor_tensor(qk[:, half], tc[:, half], ts[:, half], ALU.add).then_inc(add, 1)
                        if t == NB - 1:
                            pool.wait_ge(s_ps, i * 16 + n)
                            pool.sem_inc(pool_passed, 1)
                            nc.gpsimd.memset(kT[:, 0, :, 0:WIN], 0.0).then_inc(k_zero, 1)

        @block.tensor
        def _(pe):
            pe.sem_inc(v1_ps, 1)
            pe.sem_inc(wo_ps, 1)
            pe.wait_ge(consts_set, 3)
            with pe.Fori(0, DEPTH) as i:
                for b in range(B):
                    def at(t, b=b):
                        return i * 16 + (NB * b + t + 1)

                    pe.wait_ge(xa_ready, i * 2 + b + 1)
                    if b == 0:
                        pe.wait_ge(wqk_in, i * 16 + 16)
                        pe.wait_ge(wv_in, i * 16 + 16)
                        pe.wait_ge(wo_in, i * 16 + 16)
                    for s in range(NB + 1):
                        here, before = s < NB, s >= 1
                        if here:
                            cols = slice(WIN + P * s, WIN + P * s + P)
                            for half, done, si in ((0, q_ps, 0), (1, k_ps, 1)):
                                if s == 1:
                                    pe.wait_ge((q_raw, k_raw)[half], at(0))
                                if s >= 2:
                                    pe.wait_ge((ot_done, wo_used)[half], at(s - 2))
                                for c in range(2):
                                    step = nc.tensor.matmul(ps[:, 2 * si + c, :], xs[:, b, cols], wqk[:, INNER * half + CH * c:INNER * half + CH * c + CH],
                                                            start=True, stop=True)
                                step.then_inc(done, 1)
                            for half, done in ((0, v0_ps), (1, v1_ps)):
                                if s >= 1:
                                    pe.wait_ge((masked, kt_done)[half], at(s - 1))
                                for c in range(2):
                                    w = 2 * half + c
                                    for par in range(2):
                                        step = nc.tensor.matmul(ps[64 * par:64 * par + 64, 4 + w, :], xs[:, b, P * s + WIN * w:P * s + WIN * w + 2 * WIN],
                                                                wv[:, par, :], start=True, stop=True)
                                step.then_inc(done, 1)
                        if before:
                            pe.wait_ge(q_raw, at(s)) if here else pe.wait_ge(ot_done, at(s - 2))
                            pe.wait_ge(exp_done, at(s - 1))
                            for hp in range(HP):
                                step = nc.tensor.transpose(ps[:, hp // 4, P * (hp % 4):P * (hp % 4) + P], E[:, 2 * hp:2 * hp + 2, :], ident[:])
                            step.then_inc(pt_ps, 1)
                            pe.wait_ge(k_raw, at(s)) if here else pe.wait_ge(wo_used, at(s - 2))
                            pe.wait_ge(pt_done, at(s - 1))
                            pe.wait_ge(v1_done, at(s - 1))
                            pe.sem_inc(pe_passed, 1)
                            for h in range(H2):
                                hp, rows = h // 2, slice(64 * (h % 2), 64 * (h % 2) + 64)
                                for w in range(NW):
                                    step = nc.tensor.matmul(ps[WIN * w:WIN * w + WIN, 2 + h % 2, D2 * hp:D2 * hp + D2],
                                                            PT[rows, hp, WIN * w:WIN * w + WIN], vw[rows, (s - 1) % 2, w, D2 * hp:D2 * hp + D2],
                                                            start=True, stop=True)
                            step.then_inc(o_ps, 1)
                        if here:
                            for half, used, ready, done in ((0, v0_done, qn_done, qt_ps), (1, v1_done, kn_done, kt_ps)):
                                pe.wait_ge(used, at(s))
                                pe.wait_ge(ready, at(s))
                                for hp in range(HP):
                                    step = nc.tensor.transpose(ps[:, 4 + 2 * half + hp // 4, P * (hp % 4):P * (hp % 4) + P],
                                                               qk[:, half, 2 * hp:2 * hp + 2, :], ident[:])
                                step.then_inc(done, 1)
                        if before:
                            pe.wait_ge(o_done, at(s - 1))
                            for hp in range(HP):
                                step = nc.tensor.transpose(ps[:, hp // 4, P * (hp % 4):P * (hp % 4) + P], O[:, 2 * hp:2 * hp + 2, :], ident[:])
                            step.then_inc(ot_ps, 1)
                            pe.wait_ge(ot_done, at(s - 1))
                            for hp in range(HP):
                                step = nc.tensor.matmul(ps[:, 2, 0:P], wo[:, hp, :], OT[:, hp, :], start=hp == 0, stop=hp == HP - 1)
                            step.then_inc(wo_ps, 1)
                        if here:
                            pe.wait_ge(qt_done, at(s))
                            pe.wait_ge(kt_done, at(s))
                            if s == 0:
                                pe.wait_ge(k_zero, i * 2 + b + 1)
                            pe.sem_inc(pe_passed, 1)
                            for h in range(H2):
                                hp, rows = h // 2, slice(64 * (h % 2), 64 * (h % 2) + 64)
                                for w in range(NW):
                                    step = nc.tensor.matmul(ps[WIN * w:WIN * w + WIN, 4 + h % 2, D2 * hp:D2 * hp + D2],
                                                            qT[rows, hp, WIN * w:WIN * w + WIN], kT[rows, s % 2, hp, WIN * w:WIN * w + 2 * WIN],
                                                            start=True, stop=True)
                            step.then_inc(s_ps, 1)

                    def fat(c, b=b):
                        return i * 4 + (2 * b + c + 1)

                    pe.wait_ge(xf_ready, i * 2 + b + 1)
                    if b == 0:
                        pe.wait_ge(w1_in, i * 16 + 16)
                        pe.wait_ge(w2_in, i * 16 + 16)
                    for c in range(2):
                        nc.tensor.matmul(ps[:, c, :], mean_w[:], xs[:, b, WIN + CH * c:WIN + CH * c + CH], start=True, stop=True).then_inc(m_ps, 1)
                    for c in range(2):
                        pe.wait_ge(csq_done, fat(c))
                        nc.tensor.matmul(ps[:, 2 + c, :], mean_w[:], csq[:, c, :], start=True, stop=True).then_inc(var_ps, 1)
                    for c in range(2):
                        pe.wait_ge(xn_done, fat(c))
                        for k in range(FC):
                            j = FC * c + k
                            if j >= 2:
                                pe.wait_ge(h_done, i * 12 + (6 * b + j - 1))
                            for part in range(2):
                                step = nc.tensor.matmul(ps[0:FROWS[k], 4 + 2 * (j % 2) + part, :], w1[:, FF * part + P * k:FF * part + P * k + FROWS[k]],
                                                        xn[:, c, :], start=True, stop=True)
                            step.then_inc(ag_ps, 1)
                    for c in range(2):
                        pe.wait_ge(h_done, i * 12 + (6 * b + 3 * c + 3))
                        for k in range(FC):
                            step = nc.tensor.matmul(ps[:, c, :], w2[0:FROWS[k], k, :], hb[0:FROWS[k], c, k, :], start=k == 0, stop=k == FC - 1)
                        step.then_inc(y_ps, 1)
            pe.wait_ge(y_used, 1 + 4 * DEPTH)
            for g in range(4):
                for t in range(4):
                    step = nc.tensor.transpose(ps[:, g, P * t:P * t + P], x[:, CH * g + P * t:CH * g + P * t + P], ident[:])
                step.then_inc(out_ps, 1)

        @block.scalar
        def _(act):
            act.wait_ge(consts_set, 3)
            act.wait_ge(table_ready, 1)
            with act.Fori(0, DEPTH) as i:
                for b in range(B):
                    def at(t, b=b):
                        return i * 16 + (NB * b + t + 1)

                    for s in range(NB + 1):
                        here, before = s < NB, s >= 1
                        if here:
                            for half, src, done in ((0, q_ps, q_raw), (1, k_ps, k_raw)):
                                act.wait_ge(src, at(s))
                                nc.scalar.activation(raw[:, half].rearrange("p h d -> p (h d)"), slot(half), ACT.Copy).then_inc(done, 1)
                        if before:
                            act.wait_ge(sub_done, at(s - 1))
                            nc.scalar.activation(E[:], E[:], ACT.Exp).then_inc(exp_done, 1)
                        if here:
                            act.wait_ge(k_raw, at(s))
                            nc.scalar.activation(sq[:], raw[:], ACT.Square).then_inc(sq_done, 1)
                            for half, src, done in ((0, v0_ps, v0_done), (1, v1_ps, v1_done)):
                                act.wait_ge(src, at(s) if half == 0 else at(s) + 1)
                                nc.scalar.activation(vw[:, s % 2, 2 * half:2 * half + 2].rearrange("p w c -> p (w c)"), slot(2 + half), ACT.Copy)\
                                    .then_inc(done, 1)
                        if before:
                            act.wait_ge(pt_ps, at(s - 1))
                            nc.scalar.activation(PT[:].rearrange("p h c -> p (h c)"), slot(0), ACT.Copy).then_inc(pt_done, 1)
                        if here:
                            act.wait_ge(ssq_done, at(s))
                            nc.scalar.activation(lnq[:], ssq[:].rearrange("p a h o -> p (a h o)"), ACT.Ln, scale=65536.0).then_inc(rn_half, 1)
                            act.wait_ge(rn_half, at(s))
                            nc.scalar.activation(rn[:].rearrange("p a h o -> p (a h o)"), lnq[:], ACT.Exp, bias=ln256[:, 0:1], scale=-0.5).then_inc(rn_done, 1)
                            act.wait_ge(qt_ps, at(s))
                            nc.scalar.activation(qT[:].rearrange("p h c -> p (h c)"), slot(2), ACT.Copy).then_inc(qt_done, 1)
                            act.wait_ge(kt_ps, at(s))
                            src = slot(3).rearrange("p (h c) -> p h c", h=HP)
                            if s + 1 < NB:
                                nc.scalar.activation(kT[:, (s + 1) % 2, :, 0:WIN], src[:, :, P - WIN:P], ACT.Copy)
                            nc.scalar.activation(kT[:, s % 2, :, WIN:WIN + P], src, ACT.Copy).then_inc(kt_done, 1)
                        if before:
                            act.wait_ge(ot_ps, at(s - 1))
                            nc.scalar.activation(OT[:].rearrange("p h c -> p (h c)"), slot(0), ACT.Copy).then_inc(ot_done, 1)

                    def fat(c, b=b):
                        return i * 4 + (2 * b + c + 1)

                    for c in range(2):
                        act.wait_ge(cen_done, fat(c))
                        nc.scalar.activation(csq[:, c, :], cen[:, c, :], ACT.Square).then_inc(csq_done, 1)
                    for c in range(2):
                        act.wait_ge(var_ps, fat(c))
                        nc.scalar.activation(rstd[:, c, :], ps[:, 2 + c, :], ACT.Ln, bias=eps[:, 0:1]).then_inc(lv_done, 1)
                    for c in range(2):
                        act.wait_ge(lv_done, fat(c))
                        nc.scalar.activation(rstd[:, c, :], rstd[:, c, :], ACT.Exp, scale=-0.5).then_inc(rstd_done, 1)
                    if b == 0:
                        act.wait_ge(vec_in, i * 16 + 16)
                    for j in range(2 * FC):
                        k = j % FC
                        act.wait_ge(ag_ps, i * 12 + (6 * b + j + 1))
                        if j >= 2:
                            act.wait_ge(h_done, i * 12 + (6 * b + j - 1))
                        nc.scalar.activation(gl[0:FROWS[k], j % 2, :], ps[0:FROWS[k], 5 + 2 * (j % 2), :], ACT.Gelu,
                                             bias=vec[0:FROWS[k], 5 + k:6 + k]).then_inc(gl_done, 1)
            for g in range(4):
                act.wait_ge(out_ps, g + 1)
                nc.scalar.activation(Y[:, 4 * g:4 * g + 4, :].rearrange("p a c -> p (a c)"), ps[:, g, :], ACT.Copy).then_inc(out_done, 1)

        @block.vector
        def _(dve):
            dve.wait_ge(consts_set, 3)
            dve.wait_ge(consts_in, 32)
            dve.sem_inc(y_used, 1)
            with dve.Fori(0, DEPTH) as i:
                links = [0]

                def link(step):
                    links[0] += 1
                    step.then_inc(chain_sem, 1)
                    dve.wait_ge(chain_sem, i * DVE_LINKS + links[0])

                for b in range(B):
                    def at(t, b=b):
                        return i * 16 + (NB * b + t + 1)

                    def shift(ready, b=b):
                        nc.vector.tensor_copy(xs[0:64, b, WIN:WIN + L], x[0:64, L * b:L * b + L])
                        nc.vector.tensor_copy(xs[64:P, b, WIN + 1:WIN + L], x[64:P, L * b:L * b + L - 1]).then_inc(ready, 1)

                    shift(xa_ready)
                    if b == 0:
                        dve.wait_ge(table_ready, i + 2)
                    for s in range(NB + 1):
                        here, before = s < NB, s >= 1
                        if before:
                            dve.wait_ge(s_ps, at(s - 1))
                            for par in range(2):
                                step = nc.vector.scalar_tensor_tensor(E[:, par::2, :], ps[:, 4 + par, :].rearrange("p (h k) -> p h k", h=HP), QK_SCALE,
                                                                      mask[:, 0 if s == 1 else 1].to_broadcast([P, HP, 2 * WIN]), ALU.mult, ALU.add)
                            step.then_inc(masked, 1)
                            dve.wait_ge(masked, at(s - 1))
                            link(nc.vector.tensor_reduce(mx[:, :, 0], E[:], AX.X, ALU.max))
                            nc.vector.tensor_tensor(E[:], E[:], mx[:].to_broadcast([P, H2, 2 * WIN]), ALU.subtract).then_inc(sub_done, 1)
                        if here:
                            for half, src, done in ((0, q_raw, rotq), (1, k_raw, rotk)):
                                dve.wait_ge(src, at(s))
                                tab = [table[:, 2 * half + j, s:s + 1, :] for j in range(2)]
                                nc.vector.tensor_tensor(tc[:, half], raw[:, half], tab[0].to_broadcast([P, H2, D2]), ALU.mult)
                                hd = D2 // 2
                                nc.vector.tensor_tensor(ts[:, half, :, 0:hd], raw[:, half, :, hd:D2], tab[1][:, :, 0:hd].to_broadcast([P, H2, hd]), ALU.mult)
                                nc.vector.tensor_tensor(ts[:, half, :, hd:D2], raw[:, half, :, 0:hd], tab[1][:, :, hd:D2].to_broadcast([P, H2, hd]), ALU.mult)\
                                    .then_inc(done, 1)
                            dve.wait_ge(sq_done, at(s))
                            link(nc.vector.tensor_reduce(ssq[:, :, :, 0], sq[:], AX.X, ALU.add))
                            nc.vector.tensor_scalar(ssq[:], ssq[:], 1e-24, None, ALU.max).then_inc(ssq_done, 1)
                        if before:
                            dve.wait_ge(exp_done, at(s - 1))
                            link(nc.vector.tensor_reduce(rs[:, :, 0], E[:], AX.X, ALU.add))
                            link(nc.vector.reciprocal(rs[:], rs[:]))
                        if here:
                            dve.wait_ge(rn_done, at(s))
                            for half, add, done in ((0, addq, qn_done), (1, addk, kn_done)):
                                dve.wait_ge(add, at(s))
                                nc.vector.tensor_tensor(qk[:, half], qk[:, half], rn[:, half].to_broadcast([P, H2, D2]), ALU.mult).then_inc(done, 1)
                        if before:
                            dve.wait_ge(o_ps, at(s - 1))
                            nc.vector.tensor_tensor(O[:].rearrange("p (h a) d -> p a h d", a=2), slot(1).rearrange("p (a h d) -> p a h d", a=2, h=HP),
                                                    rs[:].rearrange("p (h a) o -> p a h o", a=2).to_broadcast([P, 2, HP, D2]), ALU.mult)\
                                .then_inc(o_done, 1)
                            dve.wait_ge(wo_ps, at(s - 1) + 1)
                            cols = slice(L * b + P * (s - 1), L * b + P * s)
                            nc.vector.tensor_tensor(x[:, cols], x[:, cols], ps[:, 2, 0:P], ALU.add).then_inc(wo_used, 1)
                    dve.wait_ge(wo_used, at(NB - 1))
                    shift(xf_ready)
                    dve.wait_ge(xf_ready, i * 2 + b + 1)

                    def fat(c, b=b):
                        return i * 4 + (2 * b + c + 1)

                    for c in range(2):
                        dve.wait_ge(m_ps, fat(c))
                        nc.vector.tensor_tensor(cen[:, c, :], xs[:, b, WIN + CH * c:WIN + CH * c + CH], ps[:, c, :], ALU.subtract).then_inc(cen_done, 1)
                    if b == 0:
                        dve.wait_ge(vec_in, i * 16 + 16)
                    for c in range(2):
                        dve.wait_ge(rstd_done, fat(c))
                        link(nc.vector.tensor_tensor(xn[:, c, :], cen[:, c, :], rstd[:, c, :], ALU.mult))
                        nc.vector.tensor_scalar(xn[:, c, :], xn[:, c, :], vec[:, 0:1], vec[:, 1:2], ALU.mult, ALU.add).then_inc(xn_done, 1)
                    for j in range(2 * FC):
                        k = j % FC
                        dve.wait_ge(gl_done, i * 12 + (6 * b + j + 1))
                        nc.vector.scalar_tensor_tensor(hb[0:FROWS[k], j // FC, k, :], ps[0:FROWS[k], 4 + 2 * (j % 2), :], vec[0:FROWS[k], 2 + k:3 + k],
                                                       gl[0:FROWS[k], j % 2, :], ALU.add, ALU.mult).then_inc(h_done, 1)
                    for c in range(2):
                        dve.wait_ge(y_ps, fat(c))
                        cols = slice(L * b + CH * c, L * b + CH * c + CH)
                        nc.vector.scalar_tensor_tensor(x[:, cols], ps[:, c, :], vec[:, 8:9], x[:, cols], ALU.add, ALU.add).then_inc(y_used, 1)
                    dve.wait_ge(y_used, i * 4 + (2 * b + 2 + 1))
                assert links[0] == DVE_LINKS, links[0]


H3 = 16
D3 = P // H3
LM = 128
SEG = L // LM
NU = B * H3
NG = NU // 4
ITERS = 6
E1 = D3 + 1


def nystrom_stage(nc, sems, XT, Y, ident, dram):
    with ExitStack() as ctx:
        def sb(name, shape, dt=FP32):
            return ctx.enter_context(nc.sbuf_tensor(f"y_{name}", shape, dt))

        def sem(name):
            return sems.enter_context(nc.semaphore(f"y_{name}"))

        wq, wk, wv = sb("wq", [P, P]), sb("wk", [P, P]), sb("wv", [P, P])
        bq, bk, bv = sb("bq", [P, 1]), sb("bk", [P, 1]), sb("bv", [P, P])
        head_mask = sb("head_mask", [P, H3, 1])
        eyes = sb("eyes", [P, 3, 1, P])
        ones = sb("ones", [P, P])
        QT, KT = sb("QT", [P, T]), sb("KT", [P, T])
        V9 = sb("V9", [P, NT, H3, E1])
        q_lm, k_lm = sb("q_lm", [P, B * LM]), sb("k_lm", [P, B * LM])
        QM, KM = sb("QM", [P, B, H3, LM]), sb("KM", [P, B, H3, LM])
        K2T, V, W = sb("K2T", [P, NG, 4, LM]), sb("V", [P, NG, 4, LM]), sb("W", [P, NG, 4, LM])
        KV, A = sb("KV", [P, NG, 4, LM]), sb("A", [P, NG, 4, LM])
        P3, P3T = KV[:, 0:4].rearrange("p a h m -> p (a h m)"), KV[:, 4:8].rearrange("p a h m -> p (a h m)")
        E, ET = KV[:, 0:4].rearrange("p (u a) h m -> p u (a h) m", u=2), KV[:, 4:8].rearrange("p (u a) h m -> p u (a h) m", u=2)
        m2, s2 = sb("m2", [P, NG, 4, 1]), sb("s2", [P, NG, 4, 1])
        cmax, rc = sb("cmax", [P, NG]), sb("rc", [P, 2])
        m3 = sb("m3", [P, 2, 2])
        T3, r3 = sb("T3", [P, NU, D3]), sb("r3", [P, NU, 1])
        G, Y9 = sb("G", [P, NU, D3]), sb("Y9", [P, NU, E1])
        m1, r1 = sb("m1", [P, 2, 8, 1]), sb("r1", [P, 2, H3, 1])
        ps = ctx.enter_context(nc.psum_tensor("y_ps", [P, 8, CH], FP32))

        def bank(i, n=1):
            return ps[:, i:i + n, :].rearrange("p a c -> p (a c)")

        loaded, qkv, qkv_used, masked, k2_ps, k2_sub, k2_exp, k2_done, col_ps, col_max = (
            sem("loaded"), sem("qkv"), sem("qkv_used"), sem("masked"), sem("k2_ps"), sem("k2_sub"), sem("k2_exp"), sem("k2_done"),
            sem("col_ps"), sem("col_max"))
        tr2, tr2_used, v0, s3, m3_ready, e3, tr3, tr3_a, tr3_d, t3 = (
            sem("tr2"), sem("tr2_used"), sem("v0"), sem("s3"), sem("m3_ready"), sem("e3"), sem("tr3"), sem("tr3_a"), sem("tr3_d"), sem("t3"))
        t3_done, kv_ps, kv_act, a_ready, p_ps, v_ps, w_ps, v_ready, w_ready = (
            sem("t3_done"), sem("kv_ps"), sem("kv_act"), sem("a_ready"), sem("p_ps"), sem("v_ps"), sem("w_ps"), sem("v_ready"), sem("w_ready"))
        g_ps, g_done, y_ps, y_done, s1, e1_sub, e1_exp, tr1, tr1_used, o1, o1_used = (
            sem("g_ps"), sem("g_done"), sem("y_ps"), sem("y_done"), sem("s1"), sem("e1_sub"), sem("e1_exp"), sem("tr1"), sem("tr1_used"),
            sem("o1"), sem("o1_used"))
        chain_sem = sem("chain")
        block = ctx.enter_context(nc.Block())
        LOADS = [(wq, "wq"), (wk, "wk"), (wv, "wv"), (bq, "bq"), (bk, "bk"), (bv, "bv"), (head_mask, "head_mask"), (eyes, "eyes")]
        SC = float(np.float32(1.0 / np.sqrt(np.sqrt(D3))))
        QUARTER = 0.25

        @block.sync
        def _(sp):
            for dst, name in LOADS:
                sp.dma_start(dst[:], dram[name]).then_inc(loaded, 16)

        @block.tensor
        def _(pe):
            pe.wait_ge(loaded, 16 * len(LOADS))
            for i in range(12):
                if i >= 8:
                    pe.wait_ge(qkv_used, i - 7)
                if i < 8:
                    c = i % 4
                    step = nc.tensor.matmul(bank(i), (wq if i < 4 else wk)[:], XT[:, CH * c:CH * c + CH], start=True, stop=True)
                else:
                    for t in range(4 * (i - 8), 4 * (i - 8) + 4):
                        step = nc.tensor.matmul(ps[:, i - 8, P * (t % 4):P * (t % 4) + P], XT[:, P * t:P * t + P], wv[:],
                                                start=True, stop=True)
                step.then_inc(qkv, 1)
            pe.wait_ge(masked, 4)
            pe.wait_ge(qkv_used, 12)
            for g in range(NG):
                b, o = g // 4, 4 * (g % 4)
                nc.tensor.matmul(bank(g), q_lm[:, LM * b:LM * b + LM], KM[:, b, o:o + 4, :], start=True, stop=True).then_inc(k2_ps, 1)
            for g in range(NG):
                pe.wait_ge(k2_done, g + 1)
                nc.tensor.matmul(bank(g), ones[:], W[:, g], start=True, stop=True).then_inc(col_ps, 1)
            for g in range(NG):
                pe.wait_ge(col_max, g + 1)
                for i in range(4):
                    step = nc.tensor.transpose(ps[:, g, LM * i:LM * i + LM], W[:, g, i, :], ident[:])
                step.then_inc(tr2, 1)

            def scores3(u):
                b, h = divmod(u, H3)
                pe.wait_ge(tr2_used, NG) if u < 2 else pe.wait_ge(e3, u - 1)
                for i in range(2):
                    step = nc.tensor.matmul(bank(2 * (u % 2) + i), QM[:, b, h, :], KT[:, L * b + CH * i:L * b + CH * i + CH], start=True, stop=True)
                step.then_inc(s3, 1)

            scores3(0)
            for u in range(NU):
                b, h = divmod(u, H3)
                if u + 1 < NU:
                    scores3(u + 1)
                pe.wait_ge(e3, u + 1)
                if u:
                    pe.wait_ge(tr3_a, u)
                    pe.wait_ge(tr3_d, u)
                for i in range(NB):
                    step = nc.tensor.transpose(ps[:, 4 + i // 4, LM * (i % 4):LM * (i % 4) + LM], P3[:, L * (u % 2) + P * i:L * (u % 2) + P * i + P], ident[:])
                step.then_inc(tr3, 1)
                pe.wait_ge(tr3_a, u + 1)
                pe.wait_ge(tr3_d, u + 1)
                for i in range(NB):
                    step = nc.tensor.matmul(ps[:, 6, E1 * u:E1 * u + E1], P3T[:, L * (u % 2) + P * i:L * (u % 2) + P * i + P], V9[:, NB * b + i, h, :],
                                            start=i == 0, stop=i == NB - 1)
                step.then_inc(t3, 1)
            pe.wait_ge(t3_done, 1)
            pe.wait_ge(v0, NG)
            bnk = [0]

            def four(lhs, rhs, g, used, value, done):
                if used is not None:
                    pe.wait_ge(used, value)
                for i in range(4):
                    step = nc.tensor.matmul(ps[:, g, LM * i:LM * i + LM], lhs[:, g, i, :], rhs[:, g, i, :], start=True, stop=True)
                step.then_inc(done, 1)

            for it in range(ITERS):
                last = it == ITERS - 1
                for g in range(NG):
                    if it:
                        pe.wait_ge(v_ready, NG * (it - 1) + g + 1)
                    four(K2T, V, g, w_ready if it else None, NG * (it - 1) + g + 1, kv_ps)
                for k in range(2):
                    for g in range(NG):
                        pe.wait_ge(kv_act, NG * it + g + 1)
                        four(KV, A, g, a_ready, 3 * NG * it + NG * k + g + 1, p_ps)
                if not last:
                    for g in range(NG):
                        four(W, A, g, a_ready, 3 * NG * it + 2 * NG + g + 1, v_ps)
                    for g in range(NG):
                        four(A, W, g, v_ready, NG * it + g + 1, w_ps)
            for g in range(NG):
                pe.wait_ge(a_ready, 3 * NG * (ITERS - 1) + 2 * NG + g + 1)
            for u in range(NU):
                step = nc.tensor.matmul(ps[:, 0, D3 * u:D3 * u + D3], A[:, u // 4, u % 4, :], T3[:, u, :], start=True, stop=True)
            step.then_inc(g_ps, 1)
            pe.wait_ge(g_done, 1)
            for u in range(NU):
                step = nc.tensor.matmul(ps[:, 1, D3 * u:D3 * u + D3], W[:, u // 4, u % 4, :], G[:, u, :], start=True, stop=True)
            step.then_inc(y_ps, 1)

            def scores1(u):
                t, half = divmod(u, 2)
                b = t // NB
                pe.wait_ge(y_done, 1) if u < 2 else pe.wait_ge(e1_sub, u - 1)
                for i in range(2):
                    step = nc.tensor.matmul(bank(2 * (u % 2) + i), QT[:, P * t:P * t + P], KM[:, b, 8 * half + 4 * i:8 * half + 4 * i + 4, :], start=True, stop=True)
                step.then_inc(s1, 1)

            def turn(u):
                pe.wait_ge(e1_exp, u + 1)
                if u:
                    pe.wait_ge(tr1_used, u)
                for i in range(8):
                    step = nc.tensor.transpose(ps[:, 4 + i // 4, LM * (i % 4):LM * (i % 4) + LM], E[:, u % 2, i, :], ident[:])
                step.then_inc(tr1, 1)

            scores1(0)
            scores1(1)
            turn(0)
            for u in range(2 * NT):
                t, half = divmod(u, 2)
                b = t // NB
                if u + 2 < 2 * NT:
                    scores1(u + 2)
                pe.wait_ge(tr1_used, u + 1)
                if half == 0 and t >= 2:
                    pe.wait_ge(o1_used, t - 1)
                for i in range(8):
                    h = 8 * half + i
                    step = nc.tensor.matmul(ps[:, 6 + t % 2, E1 * h:E1 * h + E1], ET[:, u % 2, i, :], Y9[:, H3 * b + h, :], start=True, stop=True)
                if half:
                    step.then_inc(o1, 1)
                if u + 1 < 2 * NT:
                    turn(u + 1)

        @block.scalar
        def _(act):
            act.wait_ge(loaded, 16 * len(LOADS))
            for g in range(NG):
                act.wait_ge(k2_sub, g + 1)
                nc.scalar.activation(W[:, g], W[:, g], ACT.Exp).then_inc(k2_exp, 1)
            for g in range(NG):
                act.wait_ge(tr2, g + 1)
                nc.scalar.activation(K2T[:, g].rearrange("p h m -> p (h m)"), bank(g), ACT.Copy).then_inc(tr2_used, 1)
            for u in range(NU):
                act.wait_ge(m3_ready, u + 1)
                if u >= 2:
                    act.wait_ge(tr3, u - 1)
                nc.scalar.activation(P3[:, L * (u % 2):L * (u % 2) + L], bank(2 * (u % 2), 2), ACT.Exp, bias=m3[:, u % 2, 1:2]).then_inc(e3, 1)
                act.wait_ge(tr3, u + 1)
                if u >= 2:
                    act.wait_ge(t3, u - 1)
                nc.scalar.activation(P3T[:, L * (u % 2):L * (u % 2) + CH], bank(4), ACT.Copy).then_inc(tr3_a, 1)
            for it in range(ITERS):
                for g in range(NG):
                    act.wait_ge(kv_ps, NG * it + g + 1)
                    if it == 0:
                        act.wait_ge(t3, NU)
                    nc.scalar.activation(KV[:, g].rearrange("p h m -> p (h m)"), bank(g), ACT.Copy).then_inc(kv_act, 1)
                if it == ITERS - 1:
                    break
                for g in range(NG):
                    act.wait_ge(v_ps, NG * it + g + 1)
                    nc.scalar.activation(V[:, g].rearrange("p h m -> p (h m)"), bank(g), ACT.Copy, scale=QUARTER).then_inc(v_ready, 1)
                for g in range(NG):
                    act.wait_ge(w_ps, NG * it + g + 1)
                    nc.scalar.activation(W[:, g].rearrange("p h m -> p (h m)"), bank(g), ACT.Copy, scale=QUARTER).then_inc(w_ready, 1)
            act.wait_ge(g_ps, 1)
            nc.scalar.activation(G[:].rearrange("p u d -> p (u d)"), ps[:, 0, 0:NU * D3], ACT.Copy).then_inc(g_done, 1)
            for u in range(2 * NT):
                act.wait_ge(e1_sub, u + 1)
                nc.scalar.activation(E[:, u % 2], E[:, u % 2], ACT.Exp).then_inc(e1_exp, 1)
                act.wait_ge(tr1, u + 1)
                if u >= 4:
                    act.wait_ge(o1, (u - 2) // 2)
                nc.scalar.activation(ET[:, u % 2].rearrange("p h m -> p (h m)"), bank(4, 2), ACT.Copy).then_inc(tr1_used, 1)

        @block.vector
        def _(dve):
            link = Chain(dve, chain_sem)
            nc.vector.memset(ones[:], 1.0)
            nc.vector.memset(V9[:, :, :, D3:E1], 1.0)
            nc.vector.memset(Y9[:, :, D3:E1], 1.0)
            dve.wait_ge(loaded, 16 * len(LOADS))
            for i in range(12):
                dve.wait_ge(qkv, i + 1)
                if i < 8:
                    dst, bias = (QT, bq) if i < 4 else (KT, bk)
                    c = i % 4
                    step = nc.vector.tensor_scalar(dst[:, CH * c:CH * c + CH], bank(i), bias[:, 0:1], SC, ALU.add, ALU.mult)
                else:
                    c = i - 8
                    for t in range(4):
                        step = nc.vector.tensor_tensor(V9[:, 4 * c + t, :, 0:D3], ps[:, c, P * t:P * t + P].rearrange("p (h d) -> p h d", h=H3),
                                                       bv[:].rearrange("p (h d) -> p h d", h=H3), ALU.add)
                step.then_inc(qkv_used, 1)
            dve.wait_ge(qkv_used, 12)
            for src, lm in ((QT, q_lm), (KT, k_lm)):
                step = nc.vector.tensor_reduce(lm[:], src[:].rearrange("p (m s) -> p m s", s=SEG), AX.X, ALU.add)
            link(step)
            for lm in (q_lm, k_lm):
                step = nc.vector.tensor_scalar(lm[:], lm[:], 1.0 / SEG, None, ALU.mult)
            link(step)
            for b in range(B):
                for lm, dst in ((q_lm, QM), (k_lm, KM)):
                    nc.vector.tensor_tensor(dst[:, b], lm[:, LM * b:LM * b + LM].rearrange("p (o m) -> p o m", o=1).to_broadcast([P, H3, LM]),
                                            head_mask[:].to_broadcast([P, H3, LM]), ALU.mult).then_inc(masked, 1)
            for g in range(NG):
                src = ps[:, g, :].rearrange("p (h m) -> p h m", h=4)
                dve.wait_ge(k2_ps, g + 1)
                link(nc.vector.tensor_reduce(m2[:, g, :, 0], src, AX.X, ALU.max))
                nc.vector.tensor_tensor(W[:, g], src, m2[:, g].to_broadcast([P, 4, LM]), ALU.subtract).then_inc(k2_sub, 1)
            for g in range(NG):
                dve.wait_ge(k2_exp, g + 1)
                link(nc.vector.tensor_reduce(s2[:, g, :, 0], W[:, g], AX.X, ALU.add))
                link(nc.vector.reciprocal(s2[:, g], s2[:, g]))
                nc.vector.tensor_tensor(W[:, g], W[:, g], s2[:, g].to_broadcast([P, 4, LM]), ALU.mult).then_inc(k2_done, 1)
            for g in range(NG):
                dve.wait_ge(col_ps, g + 1)
                nc.vector.tensor_reduce(cmax[:, g:g + 1], bank(g), AX.X, ALU.max).then_inc(col_max, 1)
            dve.wait_ge(col_max, NG)
            link(nc.vector.tensor_reduce(rc[:, 0:1], cmax[:], AX.X, ALU.max))
            link(nc.vector.reciprocal(rc[:, 1:2], rc[:, 0:1]))
            dve.wait_ge(tr2_used, NG)
            for g in range(NG):
                nc.vector.tensor_scalar(V[:, g], K2T[:, g], rc[:, 1:2], None, ALU.mult)
                nc.vector.tensor_scalar(W[:, g], W[:, g], rc[:, 1:2], None, ALU.mult).then_inc(v0, 1)
            dve.wait_ge(v0, NG)
            for u in range(NU):
                dve.wait_ge(s3, u + 1)
                if u >= 2:
                    dve.wait_ge(e3, u - 1)
                link(nc.vector.tensor_reduce(m3[:, u % 2, 0:1], bank(2 * (u % 2), 2), AX.X, ALU.max))
                nc.vector.tensor_scalar(m3[:, u % 2, 1:2], m3[:, u % 2, 0:1], -1.0, None, ALU.mult).then_inc(m3_ready, 1)
                if u:
                    dve.wait_ge(tr3, u)
                    if u >= 3:
                        dve.wait_ge(t3, u - 2)
                    nc.vector.tensor_copy(P3T[:, L * ((u - 1) % 2) + CH:L * ((u - 1) % 2) + L], bank(5)).then_inc(tr3_d, 1)
            dve.wait_ge(tr3, NU)
            dve.wait_ge(t3, NU - 2)
            nc.vector.tensor_copy(P3T[:, L * ((NU - 1) % 2) + CH:L * ((NU - 1) % 2) + L], bank(5)).then_inc(tr3_d, 1)
            dve.wait_ge(t3, NU)
            t3v = ps[:, 6, 0:NU * E1].rearrange("p (u e) -> p u e", e=E1)
            link(nc.vector.reciprocal(r3[:], t3v[:, :, D3:E1]))
            nc.vector.tensor_tensor(T3[:], t3v[:, :, 0:D3], r3[:].to_broadcast([P, NU, D3]), ALU.mult).then_inc(t3_done, 1)
            for it in range(ITERS):
                for k in range(3):
                    for g in range(NG):
                        if k == 0:
                            dve.wait_ge(kv_act, NG * it + g + 1)
                        else:
                            dve.wait_ge(p_ps, 2 * NG * it + NG * (k - 1) + g + 1)
                        src = ps[:, g, :].rearrange("p (h m) -> p h m", h=4)
                        nc.vector.scalar_tensor_tensor(A[:, g], src, -1.0, eyes[:, k].to_broadcast([P, 4, P]), ALU.mult, ALU.add)\
                            .then_inc(a_ready, 1)
            dve.wait_ge(y_ps, 1)
            nc.vector.tensor_scalar(Y9[:, :, 0:D3], ps[:, 1, 0:NU * D3].rearrange("p (u d) -> p u d", d=D3), QUARTER, None, ALU.mult)\
                .then_inc(y_done, 1)

            def finish(t):
                dve.wait_ge(o1, t + 1)
                ov = ps[:, 6 + t % 2, 0:H3 * E1].rearrange("p (h e) -> p h e", e=E1)
                link(nc.vector.reciprocal(r1[:, t % 2], ov[:, :, D3:E1]))
                nc.vector.tensor_tensor(Y[:, t, :].rearrange("p (h d) -> p h d", h=H3), ov[:, :, 0:D3], r1[:, t % 2].to_broadcast([P, H3, D3]),
                                        ALU.mult).then_inc(o1_used, 1)

            for u in range(2 * NT):
                src = ps[:, 2 * (u % 2):2 * (u % 2) + 2, :].rearrange("p a (h m) -> p (a h) m", m=LM)
                dve.wait_ge(s1, u + 1)
                link(nc.vector.tensor_reduce(m1[:, u % 2, :, 0], src, AX.X, ALU.max))
                if u >= 2:
                    dve.wait_ge(tr1, u - 1)
                nc.vector.tensor_tensor(E[:, u % 2], src, m1[:, u % 2].to_broadcast([P, 8, LM]), ALU.subtract).then_inc(e1_sub, 1)
                if u % 2 == 1 and u >= 3:
                    finish(u // 2 - 1)
            finish(NT - 1)


NE = 8
HID = 4 * P
HC = HID // P


def moe_stage(nc, sems, XT, Y, dram):
    with ExitStack() as ctx:
        def sb(name, shape, dt=FP32):
            return ctx.enter_context(nc.sbuf_tensor(f"e_{name}", shape, dt))

        def sem(name):
            return sems.enter_context(nc.semaphore(f"e_{name}"))

        router, w1, w2, prio = sb("router", [P, NE]), sb("w1", [P, NE, HID]), sb("w2", [P, NE, HC, P]), sb("prio", [P, 1, NE])
        pr, eq, f1, f2, p2 = (sb(n, [P, NT, NE]) for n in ("pr", "eq", "f1", "f2", "p2"))
        mx, sm = sb("mx", [P, NT, 1]), sb("sm", [P, NT, 1])
        gate = sb("gate", [P, NT, NE])
        Hb = sb("H", [P, 2, HC, CH])
        ps = ctx.enter_context(nc.psum_tensor("e_ps", [P, 8, CH], FP32))
        loaded, w1_in, w2_in, lg_ps, sub_done, exp_done, gelu, up, down, scaled, chain_sem = (
            sem("loaded"), sem("w1_in"), sem("w2_in"), sem("lg_ps"), sem("sub_done"), sem("exp_done"), sem("gelu"), sem("up"), sem("down"),
            sem("scaled"), sem("chain"))
        block = ctx.enter_context(nc.Block())
        units = [(e, c) for e in range(NE) for c in range(T // CH)]
        logits = ps[:, 6, 0:NT * NE].rearrange("p (t e) -> p t e", e=NE)

        @block.sync
        def _(sp):
            sp.dma_start(router[:], dram["router"]).then_inc(loaded, 16)
            sp.dma_start(prio[:], dram["prio"]).then_inc(loaded, 16)
            sp.dma_start(w1[:], dram["w1"]).then_inc(w1_in, 16)
            sp.dma_start(w2[:], dram["w2"]).then_inc(w2_in, 16)

        @block.tensor
        def _(pe):
            pe.wait_ge(loaded, 32)
            for t in range(NT):
                step = nc.tensor.matmul(ps[:, 6, NE * t:NE * t + NE], XT[:, P * t:P * t + P], router[:], start=True, stop=True)
            step.then_inc(lg_ps, 1)
            pe.wait_ge(w1_in, 16)

            def hidden(k):
                e, c = units[k]
                for j in range(HC):
                    if k:
                        pe.wait_ge(gelu, HC * (k - 1) + j + 1)
                    nc.tensor.matmul(ps[:, j, :], w1[:, e, P * j:P * j + P], XT[:, CH * c:CH * c + CH], start=True, stop=True).then_inc(up, 1)

            hidden(0)
            pe.wait_ge(w2_in, 16)
            for k, (e, c) in enumerate(units):
                if k + 1 < len(units):
                    hidden(k + 1)
                pe.wait_ge(gelu, HC * (k + 1))
                if k >= 2:
                    pe.wait_ge(scaled, k - 1)
                for t in range(4):
                    for j in range(HC):
                        step = nc.tensor.matmul(ps[:, 4 + k % 2, P * t:P * t + P], Hb[:, k % 2, j, P * t:P * t + P], w2[:, e, j, :],
                                                start=j == 0, stop=j == HC - 1)
                step.then_inc(down, 1)

        @block.scalar
        def _(act):
            act.wait_ge(sub_done, 1)
            nc.scalar.activation(pr[:], pr[:], ACT.Exp).then_inc(exp_done, 1)
            for k, (e, c) in enumerate(units):
                if k >= 2:
                    act.wait_ge(down, k - 1)
                for j in range(HC):
                    act.wait_ge(up, HC * k + j + 1)
                    nc.scalar.activation(Hb[:, k % 2, j, :], ps[:, j, :], ACT.Gelu).then_inc(gelu, 1)

        @block.vector
        def _(dve):
            link = Chain(dve, chain_sem)
            full = [P, NT, NE]
            dve.wait_ge(lg_ps, 1)
            link(nc.vector.tensor_reduce(mx[:, :, 0], logits, AX.X, ALU.max))
            nc.vector.tensor_tensor(pr[:], logits, mx[:].to_broadcast(full), ALU.subtract).then_inc(sub_done, 1)
            dve.wait_ge(exp_done, 1)
            link(nc.vector.tensor_reduce(sm[:, :, 0], pr[:], AX.X, ALU.add))
            link(nc.vector.reciprocal(sm[:], sm[:]))
            link(nc.vector.tensor_tensor(pr[:], pr[:], sm[:].to_broadcast(full), ALU.mult))
            for src, found in ((pr, f1), (p2, f2)):
                link(nc.vector.tensor_reduce(mx[:, :, 0], src[:], AX.X, ALU.max))
                link(nc.vector.tensor_tensor(eq[:], src[:], mx[:].to_broadcast(full), ALU.is_equal))
                link(nc.vector.tensor_tensor(eq[:], eq[:], prio[:].to_broadcast(full), ALU.mult))
                link(nc.vector.tensor_reduce(mx[:, :, 0], eq[:], AX.X, ALU.max))
                link(nc.vector.tensor_tensor(found[:], eq[:], mx[:].to_broadcast(full), ALU.is_equal))
                if src is pr:
                    link(nc.vector.scalar_tensor_tensor(p2[:], f1[:], -2.0, pr[:], ALU.mult, ALU.add))
            link(nc.vector.tensor_tensor(f1[:], f1[:], f2[:], ALU.add))
            link(nc.vector.tensor_tensor(gate[:], pr[:], f1[:], ALU.mult))
            for k, (e, c) in enumerate(units):
                dve.wait_ge(down, k + 1)
                if k >= 4:
                    dve.wait_ge(scaled, k - 3)
                for i in range(4):
                    t = 4 * c + i
                    src = ps[:, 4 + k % 2, P * i:P * i + P]
                    if e == 0:
                        step = nc.vector.tensor_scalar(Y[:, t, :], src, gate[:, t, e:e + 1], None, ALU.mult)
                    else:
                        step = nc.vector.scalar_tensor_tensor(Y[:, t, :], src, gate[:, t, e:e + 1], Y[:, t, :], ALU.mult, ALU.add)
                step.then_inc(scaled, 1)



STAGES = [0, 1, 2, 3]


def load_stage(nc, sems, X, ident, dram):
    with ExitStack() as ctx:
        loaded = sems.enter_context(nc.semaphore("x_loaded"))
        block = ctx.enter_context(nc.Block())

        @block.sync
        def _(sp):
            sp.dma_start(X[:], dram["x"].rearrange("(t p) d -> p t d", p=P)).then_inc(loaded, 16)
            sp.dma_start(ident[:], dram["ident"]).then_inc(loaded, 16)
            sp.wait_ge(loaded, 32)


def program(nc, dram, out, upto=9):
    with ExitStack() as ctx, ExitStack() as sems:
        X = ctx.enter_context(nc.sbuf_tensor("X", [P, NT, P], FP32))
        Y = ctx.enter_context(nc.sbuf_tensor("Y", [P, NT, P], FP32))
        XT = ctx.enter_context(nc.sbuf_tensor("XT", [P, T], FP32))
        ident = ctx.enter_context(nc.sbuf_tensor("ident", [P, P], FP32))
        shared = NormSemaphores(nc, sems)
        load_stage(nc, sems, X, ident, dram)
        stages = STAGES
        norm_stage(nc, shared, "n0", X, None, XT, ident)
        for i, s in enumerate(stages):
            if s == 0:
                mamba_stage(nc, sems, XT, Y, ident, None, dram)
            if s == 1:
                local_stage(nc, sems, XT, Y, ident, dram)
            if s == 2:
                nystrom_stage(nc, sems, XT, Y, ident, dram)
            if s == 3:
                moe_stage(nc, sems, XT, Y, dram)
            if i + 1 < len(stages):
                norm_stage(nc, shared, f"n{i + 1}", X, Y, XT, ident)
        norm_stage(nc, shared, "n9", X, Y, None, ident, store=out.rearrange("(t p) d -> p t d", p=P))


def kernel(**inputs):
    import concourse.bacc as _bacc
    from concourse import bass_utils
    import ml_dtypes
    a = {k: np.asarray(v) for k, v in inputs.items()}
    split = lambda v: np.ascontiguousarray(v.reshape((DC, P) + v.shape[1:]).swapaxes(0, 1))
    sel = np.zeros((96, 2 * NS, P), ml_dtypes.bfloat16)
    for r in range(96):
        sel[r, r % 32, :] = 1
    arrays = {
        "x": a["L0_attn_x"].reshape(T, P), "ident": np.eye(P, dtype=np.float32), "sel": sel,
        "w_in": np.ascontiguousarray(a["L0_attn_W_in"].T), "w_x": split(np.ascontiguousarray(a["L0_attn_W_x"].T)),
        "w_out": split(np.ascontiguousarray(a["L0_attn_W_out"].T)), "conv_w": split(a["L0_attn_conv_w"].reshape(DI, TAPS)),
        "conv_b": split(a["L0_attn_conv_b"]), "w_dt": split(a["L0_attn_w_dt"]), "b_dt": split(a["L0_attn_b_dt"]),
        "wq": a["L1_attn_Wq"].T, "wk": a["L1_attn_Wk"].T, "wv": a["L1_attn_Wv"].T, "bq": a["L1_attn_bq"].reshape(P, 1),
        "bk": a["L1_attn_bk"].reshape(P, 1), "bv": np.broadcast_to(a["L1_attn_bv"], (P, P)),
        "head_mask": np.repeat(np.eye(H3, dtype=np.float32), D3, axis=0).reshape(P, H3, 1),
        "eyes": np.stack([np.eye(P, dtype=np.float32) * k for k in (7, 15, 13)], axis=1).reshape(P, 3, 1, P),
        "router": a["L1_ffn_router_w"].T, "w1": a["L1_ffn_w1"].transpose(2, 0, 1),
        "w2": a["L1_ffn_w2"].reshape(NE, P, HC, P).transpose(3, 0, 2, 1),
        "prio": np.broadcast_to(np.arange(NE, 0, -1, dtype=np.float32), (P, 1, NE)),
        "a_log": split(a["L0_attn_A_log"]), "d_par": split(a["L0_attn_D_param"]),
    }
    qkv = a["L0_ffn_Wqkv"]
    half = np.arange(0, D2, 2, dtype=np.float32)
    freqs = np.arange(L, dtype=np.float32)[:, None] * (np.float32(1) / np.float32(10000.0) ** (half / np.float32(D2)))[None, :]
    freqs = np.concatenate([freqs, freqs], -1)
    power = ((np.arange(L) - L // 2) / (WIN // 2)).astype(np.float32)
    scale = ((half + np.float32(0.4 * D2)) / np.float32(1.4 * D2))[None, :] ** power[:, None]
    scale = np.concatenate([scale, scale], -1)
    sign = np.where(np.arange(D2) < D2 // 2, -1, 1).astype(np.float32)
    cos, sin = np.cos(freqs), np.sin(freqs) * sign
    base = np.stack([cos * scale, sin * scale, cos / scale, sin / scale]).astype(np.float32)
    q, key = np.arange(P)[:, None] % WIN, np.arange(2 * WIN)[None, :] - WIN
    seen = (key <= q) & (q - key <= WIN)
    first = seen & ((np.arange(P)[:, None] >= WIN) | (key >= 0))
    swap = lambda v: np.concatenate([v[:, D2 // 2:], v[:, :D2 // 2]], -1)
    qs, ks = a["L0_ffn_q_scale"], a["L0_ffn_k_scale"]
    chunks = lambda v: np.pad(v, [(0, 0), (0, FC * P - FF)]).reshape(DEPTH, FC, P).transpose(0, 2, 1)
    arrays |= {
        "wqk": qkv[:, :, :2 * INNER], "wvl": qkv[:, :, 2 * INNER:].reshape(DEPTH, P, HP, 2, D2).transpose(0, 1, 3, 2, 4).reshape(DEPTH, P, 2, HP * D2),
        "wo": a["L0_ffn_Wo"].reshape(DEPTH, HP, P, P).transpose(0, 2, 1, 3), "w1l": a["L0_ffn_W1"],
        "w2l": np.pad(a["L0_ffn_W2"], [(0, 0), (0, FC * P - FF), (0, 0)]).reshape(DEPTH, FC, P, P).transpose(0, 2, 1, 3),
        "vec": np.concatenate([a["L0_ffn_ln_g"][:, :, None], a["L0_ffn_ln_b"][:, :, None], chunks(a["L0_ffn_b1"][:, :FF]), chunks(a["L0_ffn_b1"][:, FF:]),
                               a["L0_ffn_b2"][:, :, None]], axis=2),
        "scales": np.broadcast_to(np.stack([qs, swap(qs), ks, swap(ks)], 1)[:, None, :, None, :], (DEPTH, P, 4, 1, D2)),
        "base": base.reshape(4, NB, P, D2).transpose(2, 0, 1, 3),
        "mask": np.where(np.stack([first, seen]), 0, -3e38).astype(np.float32).transpose(1, 0, 2).reshape(P, 2, 1, 2 * WIN),
    }
    arrays = {n: np.ascontiguousarray(v) for n, v in arrays.items()}
    nc = _bacc.Bacc("TRN2", target_bir_lowering=False, num_devices=1)
    dram = {n: nc.dram_tensor(f"in_{n}", v.shape, mybir.dt.from_np(v.dtype), kind="ExternalInput").ap() for n, v in arrays.items()}
    out = nc.dram_tensor("out", (T, P), FP32, kind="ExternalOutput").ap()
    program(nc, dram, out)
    r = bass_utils.run_bass_kernel_spmd(nc, [{f"in_{n}": v for n, v in arrays.items()}], core_ids=[0])
    return r.results[0]["out"].reshape(B, L, P)
```

```python
from contextlib import ExitStack

import numpy as np
import concourse.bass as bass
from concourse import mybir

FP32 = mybir.dt.float32
BF16 = mybir.dt.bfloat16
ACT = mybir.ActivationFunctionType
ALU = mybir.AluOpType
AX = mybir.AxisListType

P = 128
B, L = 2, 1024
T = B * L
NT = T // P
NB = L // P
CH = 512
EPS = 1e-5

DI = 256
DC = DI // P
NS = 16
TAPS = 4


class Chain:

    def __init__(self, engine, sem, count=0):
        self.engine, self.sem, self.count = engine, sem, count

    def __call__(self, step):
        self.count += 1
        step.then_inc(self.sem, 1)
        self.engine.wait_ge(self.sem, self.count)


class NormSemaphores:

    def __init__(self, nc, sems):
        self.sems = [sems.enter_context(nc.semaphore(f"n_{n}")) for n in
                     ("var_ready", "std_ready", "z_ready", "x_ready", "turned", "copied", "stored", "chain")]
        self.stds = self.fours = self.chained = 0


def norm_stage(nc, shared, name, X, Y, ZT, ident, store=None, Z=None):
    with ExitStack() as ctx:
        st = ctx.enter_context(nc.sbuf_tensor(f"{name}_stats", [P, NT, 6], FP32))
        mv = ctx.enter_context(nc.sbuf_tensor(f"{name}_mean_var", [P, NT, 2], FP32))
        sd = ctx.enter_context(nc.sbuf_tensor(f"{name}_std", [P, NT], FP32))
        rstd = ctx.enter_context(nc.sbuf_tensor(f"{name}_rstd", [P, NT], FP32))
        st2 = ctx.enter_context(nc.sbuf_tensor(f"{name}_stats2", [P, NT, 6], FP32))
        mv2 = ctx.enter_context(nc.sbuf_tensor(f"{name}_mean_var2", [P, NT, 2], FP32))
        sd2 = ctx.enter_context(nc.sbuf_tensor(f"{name}_std2", [P, NT], FP32))
        rstd2 = ctx.enter_context(nc.sbuf_tensor(f"{name}_rstd2", [P, NT], FP32))
        yn = ctx.enter_context(nc.sbuf_tensor(f"{name}_normed", [P, NT, P], FP32))
        if Z is None:
            Z = ctx.enter_context(nc.sbuf_tensor(f"{name}_normed2", [P, NT, P], FP32))
        ps = ctx.enter_context(nc.psum_tensor(f"{name}_ps", [P, 4, CH], FP32))
        var_ready, std_ready, z_ready, x_ready, turned, copied, stored, chain_sem = shared.sems
        stds, fours, chained = shared.stds, shared.fours, shared.chained
        block = ctx.enter_context(nc.Block())
        passes = 1 if Y is not None else 0

        @block.vector
        def _(dve):
            link = Chain(dve, chain_sem, chained)

            def normalise(src, out, stats, mean_var, std, recip, turn, ready):
                for t in range(NT):
                    last = nc.vector.bn_stats(stats[:, t, :], src[:, t, :])
                link(last)
                for t in range(NT):
                    last = nc.vector.bn_aggr(mean_var[:, t, :], stats[:, t, :])
                link(last)
                nc.vector.tensor_scalar(std[:], mean_var[:, :, 1], EPS, None, ALU.add).then_inc(var_ready, 1)
                dve.wait_ge(std_ready, stds + turn)
                link(nc.vector.reciprocal(recip[:], std[:]))
                for t in range(NT):
                    step = nc.vector.tensor_scalar(out[:, t, :], src[:, t, :], mean_var[:, t, 0:1], recip[:, t:t + 1],
                                                   ALU.subtract, ALU.mult)
                    if ready is not None and t % 4 == 3:
                        step.then_inc(ready, 1)
                return step

            if Y is not None:
                link(normalise(Y, yn, st, mv, sd, rstd, 1, None))
                step = nc.vector.tensor_tensor(X[:], X[:], yn[:], ALU.add)
                if store is not None:
                    step.then_inc(x_ready, 1)
                else:
                    link(step)
            if store is None:
                normalise(X, Z, st2, mv2, sd2, rstd2, passes + 1, z_ready)
            shared.chained = link.count

        @block.scalar
        def _(act):
            if Y is not None:
                act.wait_ge(var_ready, stds + 1)
                nc.scalar.activation(sd[:], sd[:], ACT.Sqrt).then_inc(std_ready, 1)
            if store is None:
                act.wait_ge(var_ready, stds + passes + 1)
                nc.scalar.activation(sd2[:], sd2[:], ACT.Sqrt).then_inc(std_ready, 1)
                for g in range(4):
                    act.wait_ge(turned, fours + g + 1)
                    nc.scalar.activation(ZT[:, CH * g:CH * (g + 1)], ps[:, g, :], ACT.Copy).then_inc(copied, 1)

        @block.tensor
        def _(pe):
            if store is None:
                for g in range(4):
                    pe.wait_ge(z_ready, fours + g + 1)
                    for t in range(4 * g, 4 * g + 4):
                        step = nc.tensor.transpose(ps[:, g, P * (t % 4):P * (t % 4) + P], Z[:, t, :], ident[:])
                    step.then_inc(turned, 1)

        @block.sync
        def _(sp):
            if store is not None:
                sp.wait_ge(x_ready, 1)
                sp.dma_start(store, X[:]).then_inc(stored, 16)
                sp.wait_ge(stored, 16)

        shared.stds += passes + (store is None)
        shared.fours += 4 * (store is None)


def mamba_stage(nc, sems, XT, Y, ident, w, dram):
    with ExitStack() as ctx:
        def sb(name, shape, dt=FP32):
            return ctx.enter_context(nc.sbuf_tensor(f"m_{name}", shape, dt))

        def sem(name):
            return sems.enter_context(nc.semaphore(f"m_{name}"))

        w_in, w_x, w_out, conv_w, conv_b, w_dt, b_dt, a_log, d_par, sel = (
            sb("w_in", [P, 4 * P]), sb("w_x", [P, DC, 2 * NS + 1]), sb("w_out", [P, DC, P]), sb("conv_w", [P, DC, TAPS]),
            sb("conv_b", [P, DC]), sb("w_dt", [P, DC]), sb("b_dt", [P, DC]), sb("a_log", [P, DC, NS]), sb("d_par", [P, DC]),
            sb("sel", [96, 2 * NS, P], BF16))
        dt_col = sb("dt_col", [P, DC, P])
        A = sb("A", [P, DC, NS])
        pad = sb("pad", [P, DC, B, TAPS - 1 + L])
        conv = sb("conv", [P, DC, B, L])
        xc = sb("xc", [P, DC, B, L])
        zs = sb("zs", [P, DC, B, L])
        delta = sb("delta", [P, DC, B, L])
        du = conv
        ex, u = pad, sb("u", [P, DC, B, L])
        bc = sb("bc", [32, 3, T], BF16)
        rest = sb("rest", [32, 2, T])
        stack = sb("stack", [96, T], BF16)
        dA = sb("dA", [P, 2, L])
        dbx = sb("dbx", [P, 2, L])
        h = sb("h", [P, 2, L])
        c_sb = sb("c_sb", [P, 2, L])
        hc = sb("hc", [P, 2, L])
        yT = u
        ps = ctx.enter_context(nc.psum_tensor("m_ps", [P, 8, CH], FP32))
        loaded, ready0, xz, xz_used, conved, silued = sem("loaded"), sem("ready0"), sem("xz"), sem("xz_used"), sem("conved"), sem("silued")
        bc_ps, dt_ps, split, stacked, dt_used, soft, softed = sem("bc_ps"), sem("dt_ps"), sem("split"), sem("stacked"), sem("dt_used"), sem("soft"), sem("softed")
        b_ready, c_ready, c_copied, dA_ready, dbx_done, scanned, hc_done, y_acc, y_used = (
            sem("b_ready"), sem("c_ready"), sem("c_copied"), sem("dA_ready"), sem("dbx_done"), sem("scanned"), sem("hc_done"),
            sem("y_acc"), sem("y_used"))
        out_ps, out_done, du_done, chain_sem, achain_sem = sem("out_ps"), sem("out_done"), sem("du_done"), sem("chain"), sem("achain")
        block = ctx.enter_context(nc.Block())
        LOADS = [(w_in, dram["w_in"]), (w_x, dram["w_x"]), (w_out, dram["w_out"]), (conv_w, dram["conv_w"]), (conv_b, dram["conv_b"]),
                 (w_dt, dram["w_dt"]), (b_dt, dram["b_dt"]), (a_log, dram["a_log"]), (d_par, dram["d_par"]), (sel, dram["sel"])]
        units = [(b, n, dc) for b in range(B) for n in range(NS) for dc in range(DC)]

        @block.sync
        def _(sp):
            for dst, src in LOADS:
                sp.dma_start(dst[:], src).then_inc(loaded, 16)

        @block.tensor
        def _(pe):
            pe.wait_ge(loaded, 16 * len(LOADS))
            for i in range(16):
                c, e = i // 4, i % 4
                if i >= 8:
                    pe.wait_ge(xz_used, i - 7)
                nc.tensor.matmul(ps[:, i % 8, :], w_in[:, P * e:P * e + P], XT[:, CH * c:CH * c + CH], start=True,
                                 stop=True).then_inc(xz, 1)
            pe.wait_ge(silued, DC)
            pe.wait_ge(xz_used, 16)
            pe.wait_ge(ready0, 1)
            for c in range(4):
                b, o = c // 2, CH * (c % 2)
                for dc in range(DC):
                    step = nc.tensor.matmul(ps[0:32, c, :], w_x[:, dc, 0:32], xc[:, dc, b, o:o + CH], start=dc == 0, stop=dc == DC - 1)
                step.then_inc(bc_ps, 1)
            for c in range(4):
                b, o = c // 2, CH * (c % 2)
                for dc in range(DC):
                    step = nc.tensor.matmul(ps[:, 4 + c, :], dt_col[:, dc, :], xc[:, dc, b, o:o + CH], start=dc == 0, stop=dc == DC - 1)
                step.then_inc(dt_ps, 1)
            pe.wait_ge(stacked, 3)
            pe.wait_ge(dt_used, 4)
            pe.wait_ge(split, 1)

            def spread(v):
                b, n = divmod(v, NS)
                if v >= 1:
                    pe.wait_ge(dbx_done, DC * v)
                for i in range(2):
                    step = nc.tensor.matmul(ps[:, 4 + i, :], sel[:, n, :], stack[:, L * b + CH * i:L * b + CH * i + CH], start=True, stop=True)
                step.then_inc(b_ready, 1)
                if v >= 1:
                    pe.wait_ge(c_copied, v)
                for i in range(2):
                    step = nc.tensor.matmul(ps[:, 6 + i, :], sel[:, NS + n, :], stack[:, L * b + CH * i:L * b + CH * i + CH], start=True, stop=True)
                step.then_inc(c_ready, 1)

            spread(0)
            for v in range(B * NS):
                b, n = divmod(v, NS)
                if v + 1 < B * NS:
                    spread(v + 1)
                if n == 0 and b:
                    pe.wait_ge(y_used, DC * b)
                for dc in range(DC):
                    pe.wait_ge(hc_done, DC * v + dc + 1)
                    for i in range(2):
                        step = nc.tensor.matmul(ps[:, 2 * dc + i, :], ident[:], hc[:, dc, CH * i:CH * i + CH], start=n == 0, stop=n == NS - 1)
                    step.then_inc(y_acc, 1)
            pe.wait_ge(y_used, DC * B)
            for t in range(NT):
                b, o = t // NB, P * (t % NB)
                for dc in range(DC):
                    step = nc.tensor.matmul(ps[:, t // 4, P * (t % 4):P * (t % 4) + P], yT[:, dc, b, o:o + P], w_out[:, dc, :],
                                            start=dc == 0, stop=dc == DC - 1)
                if t % 4 == 3:
                    step.then_inc(out_ps, 1)

        @block.scalar
        def _(act):
            act.wait_ge(loaded, 16 * len(LOADS))
            link = Chain(act, achain_sem)
            for i in range(16):
                c, e = i // 4, i % 4
                b, o = c // 2, CH * (c % 2)
                act.wait_ge(xz, i + 1)
                if e < 2:
                    step = nc.scalar.activation(pad[:, e, b, TAPS - 1 + o:TAPS - 1 + o + CH], ps[:, i % 8, :], ACT.Copy)
                else:
                    step = nc.scalar.activation(zs[:, e - 2, b, o:o + CH], ps[:, i % 8, :], ACT.Silu)
                step.then_inc(xz_used, 1)
            for dc in range(DC):
                act.wait_ge(conved, dc + 1)
                nc.scalar.activation(xc[:, dc], conv[:, dc], ACT.Silu).then_inc(silued, 1)
            link(nc.scalar.activation(A[:], a_log[:], ACT.Exp))
            act.wait_ge(conved, DC)
            for dc in range(DC):
                for c in range(4):
                    b, o = c // 2, CH * (c % 2)
                    act.wait_ge(dt_ps, c + 1)
                    nc.scalar.activation(ex[:, dc, b, o:o + CH], ps[:, 4 + c, :], ACT.Abs, bias=b_dt[:, dc:dc + 1], scale=w_dt[:, dc:dc + 1])
                    step = nc.scalar.activation(delta[:, dc, b, o:o + CH], ps[:, 4 + c, :], ACT.Relu, bias=b_dt[:, dc:dc + 1],
                                                scale=w_dt[:, dc:dc + 1])
                    if dc == DC - 1:
                        step.then_inc(dt_used, 1)
            act.wait_ge(dt_used, 4)
            for dc in range(DC):
                nc.scalar.activation(u[:, dc], ex[:, dc, :, 0:L], ACT.Exp, scale=-1.0).then_inc(soft, 1)
            for i in range(3):
                if i == 0:
                    act.wait_ge(split, 1)
                nc.scalar.activation(stack[32 * i:32 * i + 32, :], bc[:, i, :], ACT.Copy).then_inc(stacked, 1)
            for dc in range(DC):
                act.wait_ge(softed, dc + 1)
                nc.scalar.activation(ex[:, dc, :, 0:L], ex[:, dc, :, 0:L], ACT.Ln).then_inc(soft, 1)
            act.wait_ge(du_done, DC)
            for v in range(B * NS):
                b, n = divmod(v, NS)
                for dc in range(DC):
                    k = DC * v + dc
                    if k >= 2:
                        act.wait_ge(scanned, k - 1)
                    nc.scalar.activation(dA[:, dc], delta[:, dc, b], ACT.Exp, scale=A[:, dc, n:n + 1]).then_inc(dA_ready, 1)
                act.wait_ge(c_ready, v + 1)
                if v >= 2:
                    act.wait_ge(hc_done, DC * (v - 1))
                nc.scalar.activation(c_sb[:, v % 2], ps[:, 6:8, :].rearrange("p a c -> p (a c)"), ACT.Copy).then_inc(c_copied, 1)
            for g in range(4):
                act.wait_ge(out_ps, g + 1)
                nc.scalar.activation(Y[:, 4 * g:4 * g + 4, :].rearrange("p a c -> p (a c)"), ps[:, g, :], ACT.Copy).then_inc(out_done, 1)

        @block.vector
        def _(dve):
            link = Chain(dve, chain_sem)
            nc.vector.memset(pad[:, :, :, 0:TAPS - 1], 0.0)
            dve.wait_ge(loaded, 16 * len(LOADS))
            nc.vector.tensor_copy(dt_col[:], w_x[:, :, 2 * NS:2 * NS + 1].to_broadcast([P, DC, P])).then_inc(ready0, 1)
            dve.wait_ge(ready0, 1)
            dve.wait_ge(xz_used, 16)
            for k in range(TAPS):
                for dc in range(DC):
                    src = pad[:, dc, :, k:k + L]
                    if k == 0:
                        step = nc.vector.tensor_scalar(conv[:, dc], src, conv_w[:, dc, 0:1], conv_b[:, dc:dc + 1], ALU.mult, ALU.add)
                    else:
                        step = nc.vector.scalar_tensor_tensor(conv[:, dc], src, conv_w[:, dc, k:k + 1], conv[:, dc], ALU.mult, ALU.add)
                    if k == TAPS - 1:
                        step.then_inc(conved, 1)
                if k < TAPS - 1:
                    link(step)
            dve.wait_ge(bc_ps, 4)
            src = ps[0:32, 0:4, :].rearrange("p a c -> p (a c)")
            link(nc.vector.tensor_copy(bc[:, 0, :], src))
            link(nc.vector.tensor_tensor(rest[:, 0, :], src, bc[:, 0, :], ALU.subtract))
            link(nc.vector.tensor_copy(bc[:, 1, :], rest[:, 0, :]))
            link(nc.vector.tensor_tensor(rest[:, 1, :], rest[:, 0, :], bc[:, 1, :], ALU.subtract))
            nc.vector.tensor_copy(bc[:, 2, :], rest[:, 1, :]).then_inc(split, 1)
            for dc in range(DC):
                dve.wait_ge(soft, dc + 1)
                link(nc.vector.tensor_scalar(ex[:, dc, :, 0:L], u[:, dc], 1.0, None, ALU.add))
                link(nc.vector.scalar_tensor_tensor(delta[:, dc], u[:, dc], 1.0, delta[:, dc], ALU.mult, ALU.add))
                nc.vector.tensor_scalar(u[:, dc], ex[:, dc, :, 0:L], 1.0, None, ALU.subtract).then_inc(softed, 1)
            dve.wait_ge(softed, DC)
            link(nc.vector.tensor_scalar(A[:], A[:], -1.0, None, ALU.mult))
            for dc in range(DC):
                dve.wait_ge(soft, DC + dc + 1)
                link(nc.vector.tensor_tensor(delta[:, dc], delta[:, dc], u[:, dc], ALU.subtract))
                link(nc.vector.tensor_tensor(delta[:, dc], delta[:, dc], ex[:, dc, :, 0:L], ALU.add))
                nc.vector.tensor_tensor(du[:, dc], delta[:, dc], xc[:, dc], ALU.mult).then_inc(du_done, 1)
            dve.wait_ge(du_done, DC)

            def times_b(k):
                b, n, dc = units[k]
                if dc == 0:
                    dve.wait_ge(b_ready, k // DC + 1)
                if k >= 2:
                    dve.wait_ge(scanned, k - 1)
                nc.vector.tensor_tensor(dbx[:, dc], du[:, dc, b], ps[:, 4:6, :].rearrange("p a c -> p (a c)"), ALU.mult)\
                    .then_inc(dbx_done, 1)

            times_b(0)
            for k, (b, n, dc) in enumerate(units):
                if k + 1 < len(units):
                    times_b(k + 1)
                dve.wait_ge(dA_ready, k + 1)
                dve.wait_ge(dbx_done, k + 1)
                if k >= 2:
                    dve.wait_ge(hc_done, k - 1)
                nc.vector.tensor_tensor_scan(h[:, dc], dA[:, dc], dbx[:, dc], 0.0, ALU.mult, ALU.add).then_inc(scanned, 1)
                if n == NS - 1:
                    dve.wait_ge(y_acc, k + 1)
                    link(nc.vector.scalar_tensor_tensor(yT[:, dc, b], xc[:, dc, b], d_par[:, dc:dc + 1],
                                                        ps[:, 2 * dc:2 * dc + 2, :].rearrange("p a c -> p (a c)"), ALU.mult, ALU.add))
                    nc.vector.tensor_tensor(yT[:, dc, b], yT[:, dc, b], zs[:, dc, b], ALU.mult).then_inc(y_used, 1)

        @block.gpsimd
        def _(pool):
            for k, (b, n, dc) in enumerate(units):
                pool.wait_ge(scanned, k + 1)
                if dc == 0:
                    pool.wait_ge(c_copied, k // DC + 1)
                if k >= 2:
                    pool.wait_ge(y_acc, k - 1)
                nc.gpsimd.tensor_tensor(hc[:, dc], h[:, dc], c_sb[:, (k // DC) % 2], ALU.mult).then_inc(hc_done, 1)

DEPTH = 6
H2, D2 = 16, 64
INNER = H2 * D2
HP = H2 // 2
WIN = 32
NW = P // WIN
FF = 341
FC = 3
FROWS = [128, 128, FF - 256]
QK_SCALE = 8.0
TABLES = "natural_log_exp_and_others"
SPLIT = NB
FFN_START = NB + 2


def local_stage(nc, sems, XT, Y, ident, dram):
    with ExitStack() as ctx:
        def sb(name, shape, dt=FP32):
            return ctx.enter_context(nc.sbuf_tensor(f"l_{name}", shape, dt))

        def sem(name):
            return sems.enter_context(nc.semaphore(f"l_{name}"))

        x = XT
        wqk, wv, wo = sb("wqk", [P, 2 * INNER]), sb("wv", [P, 2, HP * D2]), sb("wo", [P, HP, P])
        w1, w2, vec = sb("w1", [P, 2 * FF]), sb("w2", [P, FC, P]), sb("vec", [P, 9])
        scales, base, table = sb("scales", [P, 4, 1, D2]), sb("base", [P, 4, NB, D2]), sb("table", [P, 4, NB, D2])
        mask = sb("mask", [P, 2, 1, 2 * WIN])
        mean_w, eps, ln256 = sb("mean_w", [P, P]), sb("eps", [P, 1]), sb("ln256", [P, 1])
        xs = sb("xs", [P, B, WIN + L])
        raw, sq, tc, ts, qk = (sb(n, [P, 2, H2, D2]) for n in ("raw", "sq", "tc", "ts", "qk"))
        ssq, lnq, rn = sb("ssq", [P, 2, H2, 1]), sb("lnq", [P, 2 * H2]), sb("rn", [P, 2, H2, 1])
        qT, kT, vw = sb("qT", [P, HP, P]), sb("kT", [P, 2, HP, WIN + P]), sb("vw", [P, 2, NW, HP * D2])
        vt = sb("vt", [P, 2, 2, HP * D2])
        E, PT = sb("E", [P, H2, 2 * WIN]), sb("PT", [P, HP, P])
        mx, rs = sb("mx", [P, H2, 1]), sb("rs", [P, H2, 1])
        O, OT = sb("O", [P, H2, D2]), sb("OT", [P, HP, P])
        cen, csq, rstd, xn = (sb(n, [P, 2, CH]) for n in ("cen", "csq", "rstd", "xn"))
        gl, hb = sb("gl", [P, 2, CH]), sb("hb", [P, 2, FC, CH])
        ps = ctx.enter_context(nc.psum_tensor("l_ps", [P, 8, CH], FP32))

        PIECES = {(0, "X"): ("mean", 0), (1, "X"): ("var", 0), (2, "X"): ("inner", 0), (2, "Y"): ("inner", 1), (3, "X"): ("inner", 2),
                  (3, "Y"): ("inner", 3), (4, "X"): ("inner", 4), (4, "Y"): ("inner", 5), (5, "X"): ("outer", 0)}

        def piece(n, place):
            m, k = divmod(n - FFN_START, NB)
            return (m,) + PIECES[k, place] if n >= FFN_START and (k, place) in PIECES else (None, None, None)

        def layers(engine, steps, end=None):
            steps(0, range(SPLIT), None)
            with engine.Fori(0, DEPTH - 1) as i:
                steps(i, range(SPLIT, SPLIT + NT), None)
            steps(DEPTH - 1, range(SPLIT, SPLIT + NT), NT)

        def slot(i):
            return ps[:, 2 * i:2 * i + 2, :].rearrange("p a c -> p (a c)")

        consts_in, wqk_in, wv_in, wo_in, w1_in, w2_in, vec_in, scales_in, table_ready = (
            sem("consts_in"), sem("wqk_in"), sem("wv_in"), sem("wo_in"), sem("w1_in"), sem("w2_in"), sem("vec_in"), sem("scales_in"),
            sem("table_ready"))
        consts_set, k_zero, xa_ready, xf_ready = sem("consts_set"), sem("k_zero"), sem("xa_ready"), sem("xf_ready")
        q_ps, k_ps, v_ps, pt_ps, o_ps, qt_ps, kt_ps, ot_ps, wo_ps, s_ps = (
            sem(n) for n in ("q_ps", "k_ps", "v_ps", "pt_ps", "o_ps", "qt_ps", "kt_ps", "ot_ps", "wo_ps", "s_ps"))
        q_raw, k_raw, sq_done, v_done, pt_done, rn_half, rn_done, qt_done, kt_done, ot_done, exp_done = (
            sem(n) for n in ("q_raw", "k_raw", "sq_done", "v_done", "pt_done", "rn_half", "rn_done", "qt_done", "kt_done", "ot_done",
                             "exp_done"))
        masked, sub_done, rotq, rotk, ssq_done, qn_done, kn_done, o_done, wo_used, addq, addk = (
            sem(n) for n in ("masked", "sub_done", "rotq", "rotk", "ssq_done", "qn_done", "kn_done", "o_done", "wo_used", "addq", "addk"))
        m_ps, cen_done, csq_done, var_ps, lv_done, rstd_done, xn_done, y_ps, y_used = (
            sem(n) for n in ("m_ps", "cen_done", "csq_done", "var_ps", "lv_done", "rstd_done", "xn_done", "y_ps", "y_used"))
        vw_in = sem("vw_in")
        V_MOVES = 2 * (NW + 1)
        mx_done, sum_done, rs_done, ssq_sum, mul_done = (sem(n) for n in ("mx_done", "sum_done", "rs_done", "ssq_sum", "mul_done"))
        ag_ps, gl_done, h_done = sem("ag_ps"), sem("gl_done"), sem("h_done")
        out_ps, out_done, pe_passed, pool_passed, sp_passed = (sem(n) for n in ("out_ps", "out_done", "pe_passed", "pool_passed", "sp_passed"))
        block = ctx.enter_context(nc.Block())

        @block.sync
        def _(sp):
            for dst, name in ((base, "base"), (mask, "mask")):
                sp.dma_start(dst[:], dram[name]).then_inc(consts_in, 16)

            def load(dst, name, i, done):
                src = dram[name][bass.ds(i, 1)]
                src = src.rearrange("a p n -> p (a n)") if len(src.shape) == 3 else \
                    src.rearrange("a p k n -> p (a k) n") if len(src.shape) == 4 else src.rearrange("a p k o d -> p (a k) o d")
                sp.dma_start(dst[:], src).then_inc(done, 16)

            for dst, name, done in ((scales, "scales", scales_in), (wqk, "wqk", wqk_in), (wv, "wvl", wv_in), (wo, "wo", wo_in),
                                    (w1, "w1l", w1_in), (w2, "w2l", w2_in), (vec, "vec", vec_in)):
                load(dst, name, 0, done)

            def settled(done, value):
                sp.wait_ge(done, value)
                sp.sem_inc(sp_passed, 1)

            def steps(i, span, end):
                for n in span:
                    more = end is None and n >= SPLIT
                    if more and n == SPLIT:
                        settled(table_ready, i + 2)
                        load(scales, "scales", i + 1, scales_in)
                    if more and n == NT - 1:
                        settled(k_ps, i * 16 + 16)
                        load(wqk, "wqk", i + 1, wqk_in)
                    if end is None or n < end:
                        if n >= 1:
                            settled(vw_in, (i * 16 + n) * V_MOVES * 16)
                        if n >= 2:
                            settled(o_ps, i * 16 + (n - 1))
                        if n == 0:
                            sp.wait_ge(consts_set, 4)
                        settled(v_done, i * 16 + (n + 1))
                        for par in range(2):
                            rows = 64 * par
                            sp.dma_start(vw[rows:rows + WIN, n % 2, 0, :], vt[P - WIN:P, (n + 1) % 2, par, :]).then_inc(vw_in, 16)
                            sp.dma_start(vw[rows + WIN:rows + 2 * WIN, n % 2, 0, :], vt[0:WIN, n % 2, par, :]).then_inc(vw_in, 16)
                            for w in range(1, NW):
                                sp.dma_start(vw[rows:rows + 2 * WIN, n % 2, w, :], vt[WIN * w - WIN:WIN * w + WIN, n % 2, par, :]).then_inc(vw_in, 16)
                    if more and n == NT - 1:
                        load(wv, "wvl", i + 1, wv_in)
                    if more and n == NT + 1:
                        settled(wo_ps, i * 16 + 16)
                        load(wo, "wo", i + 1, wo_in)
                    if more and n == SPLIT + NT - 1:
                        settled(y_used, i * 4 + 4)
                        load(w1, "w1l", i + 1, w1_in)
                        load(w2, "w2l", i + 1, w2_in)
                        load(vec, "vec", i + 1, vec_in)

            layers(sp, steps)

        @block.gpsimd
        def _(pool):
            nc.gpsimd.memset(xs[:], 0.0).then_inc(consts_set, 1)
            nc.gpsimd.memset(vt[:, 1], 0.0).then_inc(consts_set, 1)
            nc.gpsimd.memset(kT[:, 0, :, 0:WIN], 0.0).then_inc(k_zero, 1)
            nc.gpsimd.memset(mean_w[:], 1.0 / P).then_inc(consts_set, 1)
            nc.gpsimd.memset(eps[:], EPS).then_inc(consts_set, 1)
            nc.gpsimd.memset(ln256[:], float(np.log(256.0))).then_inc(table_ready, 1)
            pool.wait_ge(consts_in, 32)

            def tables(turn):
                pool.wait_ge(scales_in, turn * 16)
                for k in range(4):
                    step = nc.gpsimd.tensor_tensor(table[:, k], base[:, k], scales[:, k].to_broadcast([P, NB, D2]), ALU.mult)
                step.then_inc(table_ready, 1)

            tables(1)

            def steps(i, span, end):
                for n in span:
                    if end is not None and n >= end:
                        continue
                    for half, rot, turned, add in ((0, rotq, qt_ps, addq), (1, rotk, kt_ps, addk)):
                        if n >= 1:
                            pool.wait_ge(turned, i * 16 + n)
                        pool.wait_ge(rot, i * 16 + (n + 1))
                        nc.gpsimd.tensor_tensor(qk[:, half], tc[:, half], ts[:, half], ALU.add).then_inc(add, 1)
                    if n % NB == 0 and n:
                        pool.wait_ge(s_ps, i * 16 + (n - 1))
                        pool.sem_inc(pool_passed, 1)
                        nc.gpsimd.memset(kT[:, 0, :, 0:WIN], 0.0).then_inc(k_zero, 1)
                    if n == NT - 1 and end is None:
                        tables(i + 2)

            layers(pool, steps)

        @block.tensor
        def _(pe):
            pe.wait_ge(consts_set, 4)

            def steps(i, span, end):
                def at(n):
                    return i * 16 + (n + 1)

                def mlp(n, place, used, value):
                    m, what, j = piece(n, place)
                    if what is None:
                        return
                    b = m % B
                    pe.wait_ge(used, value)
                    if what == "mean":
                        pe.wait_ge(xf_ready, i * 2 + (m + 1))
                        for c in range(2):
                            step = nc.tensor.matmul(ps[:, 6 + c, :], mean_w[:], xs[:, b, WIN + CH * c:WIN + CH * c + CH], start=True, stop=True)
                        step.then_inc(m_ps, 1)
                    if what == "var":
                        pe.wait_ge(csq_done, i * 2 + (m + 1))
                        for c in range(2):
                            step = nc.tensor.matmul(ps[:, 6 + c, :], mean_w[:], csq[:, c, :], start=True, stop=True)
                        step.then_inc(var_ps, 1)
                    if what == "inner":
                        c, k = divmod(j, FC)
                        if j == 0:
                            pe.wait_ge(xn_done, i * 2 + (m + 1))
                            if b == 0:
                                pe.wait_ge(w1_in, i * 16 + 16 * (m // B + 1))
                                pe.wait_ge(w2_in, i * 16 + 16 * (m // B + 1))
                        for part in range(2):
                            step = nc.tensor.matmul(ps[0:FROWS[k], 6 + part, :], w1[:, FF * part + P * k:FF * part + P * k + FROWS[k]],
                                                    xn[:, c, :], start=True, stop=True)
                        step.then_inc(ag_ps, 1)
                    if what == "outer":
                        pe.wait_ge(h_done, i * 12 + 6 * (m + 1))
                        for c in range(2):
                            for k in range(FC):
                                step = nc.tensor.matmul(ps[:, 6 + c, :], w2[0:FROWS[k], k, :], hb[0:FROWS[k], c, k, :], start=k == 0, stop=k == FC - 1)
                        step.then_inc(y_ps, 1)

                def used_by(n, place):
                    m, what, j = piece(n, place)
                    if what == "inner":
                        return h_done, i * 12 + (6 * m + j + 1)
                    return {"mean": cen_done, "var": rstd_done, "outer": y_used}[what], \
                        i * 4 + 2 * (m + 1) if what == "outer" else i * 2 + (m + 1)

                for n in span:
                    a, b1, c2 = (0 <= k and (end is None or k < end) for k in (n, n - 1, n - 2))
                    b, t = (n // NB) % B, n % NB
                    cols = slice(WIN + P * t, WIN + P * t + P)
                    if a:
                        if t == 0:
                            pe.wait_ge(xa_ready, i * 2 + (n // NB + 1))
                        if n % NT == 0:
                            pe.wait_ge(wqk_in, i * 16 + 16 * (n // NT + 1))
                        for half, done in ((0, q_ps), (1, k_ps)):
                            if half == 0 and n >= 3:
                                pe.wait_ge(o_done, at(n - 3))
                            elif half == 0 and n >= 1:
                                pe.wait_ge(q_raw, at(n - 1))
                            if half == 1 and n >= 2:
                                pe.wait_ge(masked, at(n - 2))
                            if half == 1 and n == 1:
                                pe.wait_ge(k_raw, at(0))
                            for c in range(2):
                                step = nc.tensor.matmul(ps[:, 2 * half + c, :], xs[:, b, cols], wqk[:, INNER * half + CH * c:INNER * half + CH * c + CH],
                                                        start=True, stop=True)
                            step.then_inc(done, 1)
                    if c2:
                        if n >= 3:
                            pe.wait_ge(wo_used, at(n - 3))
                        else:
                            pe.wait_ge(v_done, at(n - 1))
                        pe.wait_ge(exp_done, at(n - 2))
                        for hp in range(HP):
                            step = nc.tensor.transpose(ps[:, 4 + hp // 4, P * (hp % 4):P * (hp % 4) + P], E[:, 2 * hp:2 * hp + 2, :], ident[:])
                        step.then_inc(pt_ps, 1)
                    if b1:
                        if piece(n - 1, "Y")[1]:
                            pe.wait_ge(*used_by(n - 1, "Y"))
                        elif n >= 3:
                            pe.wait_ge(ot_done, at(n - 3))
                        if a:
                            used = (None, k_raw, at(n))
                        else:
                            used = (None, masked, at(n - 2))
                        for half, ready, done in ((0, qn_done, qt_ps), (1, kn_done, kt_ps)):
                            if half:
                                pe.wait_ge(used[1], used[2])
                            pe.wait_ge(ready, at(n - 1))
                            for hp in range(HP):
                                step = nc.tensor.transpose(ps[:, (6, 2)[half] + hp // 4, P * (hp % 4):P * (hp % 4) + P],
                                                           qk[:, half, 2 * hp:2 * hp + 2, :], ident[:])
                            step.then_inc(done, 1)
                    if c2:
                        if a:
                            pe.wait_ge(q_raw, at(n))
                        else:
                            pe.wait_ge(o_done, at(n - 3))
                        pe.wait_ge(vw_in, at(n - 2) * V_MOVES * 16)
                        pe.wait_ge(pt_done, at(n - 2))
                        pe.sem_inc(pe_passed, 1)
                        for h in range(H2):
                            hp, rows = h // 2, slice(64 * (h % 2), 64 * (h % 2) + 64)
                            for w in range(NW):
                                step = nc.tensor.matmul(ps[WIN * w:WIN * w + WIN, h % 2, D2 * hp:D2 * hp + D2],
                                                        PT[rows, hp, WIN * w:WIN * w + WIN], vw[rows, n % 2, w, D2 * hp:D2 * hp + D2],
                                                        start=True, stop=True)
                        step.then_inc(o_ps, 1)
                    if b1:
                        mlp(n, "X", qt_done, at(n - 1))
                    elif piece(n, "X")[1]:
                        before = (n, "X")
                        k = n if not piece(n - 1, "Y")[1] and not piece(n - 1, "X")[1] else n - 1
                        place = "Y" if piece(n - 1, "Y")[1] else "X"
                        mlp(n, "X", *(used_by(n - 1, place) if k == n - 1 else (ot_done, at(NT - 1))))
                    if a:
                        if n >= 2:
                            pe.wait_ge(pt_done, at(n - 2))
                        elif n >= 1:
                            pe.wait_ge(v_done, at(n - 1))
                        if n % NT == 0:
                            pe.wait_ge(wv_in, i * 16 + 16 * (n // NT + 1))
                        for par in range(2):
                            step = nc.tensor.matmul(ps[:, 4 + par, :], xs[:, b, cols], wv[:, par, :], start=True, stop=True)
                        step.then_inc(v_ps, 1)
                    if c2:
                        if piece(n, "X")[1]:
                            pe.wait_ge(*used_by(n, "X"))
                        elif b1:
                            pe.wait_ge(qt_done, at(n - 1))
                        else:
                            pe.wait_ge(ot_done, at(n - 3))
                        pe.wait_ge(o_done, at(n - 2))
                        for hp in range(HP):
                            step = nc.tensor.transpose(ps[:, 6 + hp // 4, P * (hp % 4):P * (hp % 4) + P], O[:, 2 * hp:2 * hp + 2, :], ident[:])
                        step.then_inc(ot_ps, 1)
                    if b1:
                        pe.wait_ge(kt_done, at(n - 1))
                        if (n - 1) % NB == 0:
                            pe.wait_ge(k_zero, i * 2 + ((n - 1) // NB + 1))
                        pe.sem_inc(pe_passed, 1)
                        for h in range(H2):
                            hp, rows = h // 2, slice(64 * (h % 2), 64 * (h % 2) + 64)
                            for w in range(NW):
                                step = nc.tensor.matmul(ps[WIN * w:WIN * w + WIN, 2 + h % 2, D2 * hp:D2 * hp + D2],
                                                        qT[rows, hp, WIN * w:WIN * w + WIN], kT[rows, (n - 1) % 2, hp, WIN * w:WIN * w + 2 * WIN],
                                                        start=True, stop=True)
                        step.then_inc(s_ps, 1)
                    if c2:
                        if a:
                            pe.wait_ge(v_done, at(n))
                        if (n - 2) % NT == 0:
                            pe.wait_ge(wo_in, i * 16 + 16 * ((n - 2) // NT + 1))
                        pe.wait_ge(ot_done, at(n - 2))
                        for hp in range(HP):
                            step = nc.tensor.matmul(ps[:, 4, 0:P], wo[:, hp, :], OT[:, hp, :], start=hp == 0, stop=hp == HP - 1)
                        step.then_inc(wo_ps, 1)
                        mlp(n, "Y", ot_done, at(n - 2))
                    elif piece(n, "Y")[1]:
                        mlp(n, "Y", *used_by(n, "X"))

            layers(pe, steps)
            pe.wait_ge(y_used, 4 * DEPTH)
            for g in range(4):
                for t in range(4):
                    step = nc.tensor.transpose(ps[:, g, P * t:P * t + P], x[:, CH * g + P * t:CH * g + P * t + P], ident[:])
                step.then_inc(out_ps, 1)

        @block.scalar
        def _(act):
            act.wait_ge(consts_set, 4)
            act.wait_ge(table_ready, 1)
            act.preload_act_table_set(TABLES)

            def steps(i, span, end):
                def at(n):
                    return i * 16 + (n + 1)

                def gelu(m, j, back=True):
                    k = j % FC
                    if j == 0 and m % B == 0:
                        act.wait_ge(vec_in, i * 16 + 16 * (m // B + 1))
                    act.wait_ge(ag_ps, i * 12 + (6 * m + j + 1))
                    if j >= 2:
                        act.wait_ge(h_done, i * 12 + (6 * m + j - 1))
                    nc.scalar.activation(gl[0:FROWS[k], j % 2, :], ps[0:FROWS[k], 7, :], ACT.Gelu, bias=vec[0:FROWS[k], 5 + k:6 + k]).then_inc(gl_done, 1)
                    if back:
                        act.preload_act_table_set(TABLES)

                for n in span:
                    a, b1, c2 = (0 <= k and (end is None or k < end) for k in (n, n - 1, n - 2))
                    if c2:
                        act.wait_ge(sub_done, at(n - 2))
                        nc.scalar.activation(E[:], E[:], ACT.Exp).then_inc(exp_done, 1)
                    m, what, j = piece(n - 1, "Y")
                    if what == "inner":
                        gelu(m, j, piece(n, "X")[1] != "inner")
                    if a:
                        act.wait_ge(q_ps, at(n))
                        nc.scalar.activation(raw[:, 0].rearrange("p h d -> p (h d)"), slot(0), ACT.Copy).then_inc(q_raw, 1)
                    if a:
                        act.wait_ge(k_ps, at(n))
                        nc.scalar.activation(raw[:, 1].rearrange("p h d -> p (h d)"), slot(1), ACT.Copy).then_inc(k_raw, 1)
                    if c2:
                        act.wait_ge(pt_ps, at(n - 2))
                        nc.scalar.activation(PT[:].rearrange("p h c -> p (h c)"), slot(2), ACT.Copy).then_inc(pt_done, 1)
                    if b1:
                        act.wait_ge(qt_ps, at(n - 1))
                        nc.scalar.activation(qT[:].rearrange("p h c -> p (h c)"), slot(3), ACT.Copy).then_inc(qt_done, 1)
                        act.wait_ge(kt_ps, at(n - 1))
                        src = slot(1).rearrange("p (h c) -> p h c", h=HP)
                        if n % NB:
                            nc.scalar.activation(kT[:, n % 2, :, 0:WIN], src[:, :, P - WIN:P], ACT.Copy)
                        nc.scalar.activation(kT[:, (n - 1) % 2, :, WIN:WIN + P], src, ACT.Copy).then_inc(kt_done, 1)
                    if a:
                        act.wait_ge(k_raw, at(n))
                        nc.scalar.activation(sq[:], raw[:], ACT.Square).then_inc(sq_done, 1)
                    m, what, j = piece(n, "X")
                    if what == "inner":
                        gelu(m, j)
                    if what == "var":
                        act.wait_ge(var_ps, i * 2 + (m + 1))
                        nc.scalar.activation(rstd[:].rearrange("p a c -> p (a c)"), slot(3), ACT.Ln, bias=eps[:, 0:1]).then_inc(lv_done, 1)
                        act.wait_ge(lv_done, i * 2 + (m + 1))
                        nc.scalar.activation(rstd[:], rstd[:], ACT.Exp, scale=-0.5).then_inc(rstd_done, 1)
                    if a:
                        act.wait_ge(v_ps, at(n))
                        if n >= 1:
                            act.wait_ge(vw_in, at(n - 1) * V_MOVES * 16)
                        nc.scalar.activation(vt[:, n % 2].rearrange("p a c -> p (a c)"), slot(2), ACT.Copy).then_inc(v_done, 1)
                    if c2:
                        act.wait_ge(ot_ps, at(n - 2))
                        nc.scalar.activation(OT[:].rearrange("p h c -> p (h c)"), slot(3), ACT.Copy).then_inc(ot_done, 1)
                    if a:
                        act.wait_ge(ssq_done, at(n))
                        nc.scalar.activation(lnq[:], ssq[:].rearrange("p a h o -> p (a h o)"), ACT.Ln, scale=65536.0).then_inc(rn_half, 1)
                        act.wait_ge(rn_half, at(n))
                        nc.scalar.activation(rn[:].rearrange("p a h o -> p (a h o)"), lnq[:], ACT.Exp, bias=ln256[:, 0:1], scale=-0.5).then_inc(rn_done, 1)
                    if what == "mean":
                        act.wait_ge(cen_done, i * 2 + (m + 1))
                        nc.scalar.activation(csq[:], cen[:], ACT.Square).then_inc(csq_done, 1)

            layers(act, steps)
            for g in range(4):
                act.wait_ge(out_ps, g + 1)
                nc.scalar.activation(Y[:, 4 * g:4 * g + 4, :].rearrange("p a c -> p (a c)"), ps[:, g, :], ACT.Copy).then_inc(out_done, 1)

        @block.vector
        def _(dve):
            dve.wait_ge(consts_set, 4)
            dve.wait_ge(consts_in, 32)

            def shift(b, ready):
                nc.vector.tensor_copy(xs[0:64, b, WIN:WIN + L], x[0:64, L * b:L * b + L])
                nc.vector.tensor_copy(xs[64:P, b, WIN + 1:WIN + L], x[64:P, L * b:L * b + L - 1]).then_inc(ready, 1)

            for b in range(B):
                shift(b, xa_ready)

            def steps(i, span, end):
                def at(n):
                    return i * 16 + (n + 1)

                def hidden(m, j):
                    c, k = divmod(j, FC)
                    dve.wait_ge(gl_done, i * 12 + (6 * m + j + 1))
                    nc.vector.scalar_tensor_tensor(hb[0:FROWS[k], c, k, :], ps[0:FROWS[k], 6, :], vec[0:FROWS[k], 2 + k:3 + k],
                                                   gl[0:FROWS[k], j % 2, :], ALU.add, ALU.mult).then_inc(h_done, 1)

                for n in span:
                    a, b1, c2, c3 = (0 <= k and (end is None or k < end) for k in (n, n - 1, n - 2, n - 3))
                    t = n % NB
                    if c2:
                        dve.wait_ge(s_ps, at(n - 2))
                        for par in range(2):
                            step = nc.vector.scalar_tensor_tensor(E[:, par::2, :], ps[:, 2 + par, :].rearrange("p (h k) -> p h k", h=HP), QK_SCALE,
                                                                  mask[:, 0 if (n - 2) % NB == 0 else 1].to_broadcast([P, HP, 2 * WIN]),
                                                                  ALU.mult, ALU.add)
                        step.then_inc(masked, 1)
                        dve.wait_ge(masked, at(n - 2))
                        nc.vector.tensor_reduce(mx[:, :, 0], E[:], AX.X, ALU.max).then_inc(mx_done, 1)
                        dve.wait_ge(mx_done, at(n - 2))
                        nc.vector.tensor_tensor(E[:], E[:], mx[:].to_broadcast([P, H2, 2 * WIN]), ALU.subtract).then_inc(sub_done, 1)
                    if c3:
                        dve.wait_ge(wo_ps, at(n - 3))
                        c = L * (((n - 3) // NB) % B) + P * ((n - 3) % NB)
                        nc.vector.tensor_tensor(x[:, c:c + P], x[:, c:c + P], ps[:, 4, 0:P], ALU.add).then_inc(wo_used, 1)
                        if (n - 3) % NB == NB - 1:
                            dve.wait_ge(wo_used, at(n - 3))
                            shift(((n - 3) // NB) % B, xf_ready)
                    if b1:
                        dve.wait_ge(rn_done, at(n - 1))
                        for half, add, done in ((0, addq, qn_done), (1, addk, kn_done)):
                            dve.wait_ge(add, at(n - 1))
                            nc.vector.tensor_tensor(qk[:, half], qk[:, half], rn[:, half].to_broadcast([P, H2, D2]), ALU.mult).then_inc(done, 1)
                    m, what, j = piece(n - 1, "Y")
                    if what == "inner":
                        hidden(m, j)
                    if a:
                        if n % NT == 0:
                            dve.wait_ge(table_ready, i + (n // NT + 2))
                        for half, src, done in ((0, q_raw, rotq), (1, k_raw, rotk)):
                            dve.wait_ge(src, at(n))
                            tab = [table[:, 2 * half + k, t:t + 1, :] for k in range(2)]
                            nc.vector.tensor_tensor(tc[:, half], raw[:, half], tab[0].to_broadcast([P, H2, D2]), ALU.mult)
                            hd = D2 // 2
                            nc.vector.tensor_tensor(ts[:, half, :, 0:hd], raw[:, half, :, hd:D2], tab[1][:, :, 0:hd].to_broadcast([P, H2, hd]), ALU.mult)
                            nc.vector.tensor_tensor(ts[:, half, :, hd:D2], raw[:, half, :, 0:hd], tab[1][:, :, hd:D2].to_broadcast([P, H2, hd]), ALU.mult)\
                                .then_inc(done, 1)
                    if c2:
                        dve.wait_ge(exp_done, at(n - 2))
                        nc.vector.tensor_reduce(rs[:, :, 0], E[:], AX.X, ALU.add).then_inc(sum_done, 1)
                        dve.wait_ge(sum_done, at(n - 2))
                        nc.vector.reciprocal(rs[:], rs[:]).then_inc(rs_done, 1)
                    if c2:
                        dve.wait_ge(rs_done, at(n - 2))
                        dve.wait_ge(o_ps, at(n - 2))
                        nc.vector.tensor_tensor(O[:].rearrange("p (h a) d -> p a h d", a=2), slot(0).rearrange("p (a h d) -> p a h d", a=2, h=HP),
                                                rs[:].rearrange("p (h a) o -> p a h o", a=2).to_broadcast([P, 2, HP, D2]), ALU.mult)\
                            .then_inc(o_done, 1)
                    m, what, j = piece(n, "X")
                    if what == "inner":
                        hidden(m, j)
                    if what == "mean":
                        b = m % B
                        dve.wait_ge(m_ps, i * 2 + (m + 1))
                        dve.wait_ge(xf_ready, i * 2 + (m + 1))
                        nc.vector.tensor_tensor(cen[:].rearrange("p a c -> p (a c)"), xs[:, b, WIN:WIN + L], slot(3), ALU.subtract).then_inc(cen_done, 1)
                    if a:
                        dve.wait_ge(sq_done, at(n))
                        nc.vector.tensor_reduce(ssq[:, :, :, 0], sq[:], AX.X, ALU.add).then_inc(ssq_sum, 1)
                        dve.wait_ge(ssq_sum, at(n))
                        nc.vector.tensor_scalar(ssq[:], ssq[:], 1e-24, None, ALU.max).then_inc(ssq_done, 1)
                    if what == "outer":
                        b = m % B
                        dve.wait_ge(y_ps, i * 2 + (m + 1))
                        nc.vector.scalar_tensor_tensor(x[:, L * b:L * b + L], slot(3), vec[:, 8:9], x[:, L * b:L * b + L], ALU.add, ALU.add)\
                            .then_inc(y_used, 2)
                        dve.wait_ge(y_used, i * 4 + 2 * (m + 1))
                        if end is None:
                            shift(b, xa_ready)
                    if what == "var":
                        if m % B == 0:
                            dve.wait_ge(vec_in, i * 16 + 16 * (m // B + 1))
                        dve.wait_ge(rstd_done, i * 2 + (m + 1))
                        nc.vector.tensor_tensor(xn[:], cen[:], rstd[:], ALU.mult).then_inc(mul_done, 1)
                        dve.wait_ge(mul_done, i * 2 + (m + 1))
                        nc.vector.tensor_scalar(xn[:], xn[:], vec[:, 0:1], vec[:, 1:2], ALU.mult, ALU.add).then_inc(xn_done, 1)

            layers(dve, steps)


H3 = 16
D3 = P // H3
LM = 128
SEG = L // LM
NU = B * H3
NG = NU // 4
ITERS = 6
E1 = D3 + 1


def nystrom_stage(nc, sems, XT, Y, ident, dram):
    with ExitStack() as ctx:
        def sb(name, shape, dt=FP32):
            return ctx.enter_context(nc.sbuf_tensor(f"y_{name}", shape, dt))

        def sem(name):
            return sems.enter_context(nc.semaphore(f"y_{name}"))

        wq, wk, wv = sb("wq", [P, P]), sb("wk", [P, P]), sb("wv", [P, P])
        bq, bk, bv = sb("bq", [P, 1]), sb("bk", [P, 1]), sb("bv", [P, P])
        head_mask = sb("head_mask", [P, H3, 1])
        eyes = sb("eyes", [P, 3, 1, P])
        ones = sb("ones", [P, P])
        QT, KT = sb("QT", [P, T]), sb("KT", [P, T])
        V9 = sb("V9", [P, NT, H3, E1])
        q_lm, k_lm = sb("q_lm", [P, B * LM]), sb("k_lm", [P, B * LM])
        QM, KM = sb("QM", [P, B, H3, LM]), sb("KM", [P, B, H3, LM])
        K2T, V, W = sb("K2T", [P, NG, 4, LM]), sb("V", [P, NG, 4, LM]), sb("W", [P, NG, 4, LM])
        KV, A = sb("KV", [P, NG, 4, LM]), sb("A", [P, NG, 4, LM])
        P3, P3T = KV[:, 0:4].rearrange("p a h m -> p (a h m)"), KV[:, 4:8].rearrange("p a h m -> p (a h m)")
        E, ET = KV[:, 0:4].rearrange("p (u a) h m -> p u (a h) m", u=2), KV[:, 4:8].rearrange("p (u a) h m -> p u (a h) m", u=2)
        m2, s2 = sb("m2", [P, NG, 4, 1]), sb("s2", [P, NG, 4, 1])
        cmax, rc = sb("cmax", [P, NG]), sb("rc", [P, 2])
        m3 = sb("m3", [P, 2, 2])
        T3, r3 = sb("T3", [P, NU, D3]), sb("r3", [P, NU, 1])
        G, Y9 = sb("G", [P, NU, D3]), sb("Y9", [P, NU, E1])
        m1, r1 = sb("m1", [P, 2, 8, 1]), sb("r1", [P, 2, H3, 1])
        ps = ctx.enter_context(nc.psum_tensor("y_ps", [P, 8, CH], FP32))

        def bank(i, n=1):
            return ps[:, i:i + n, :].rearrange("p a c -> p (a c)")

        loaded, qkv, qkv_used, masked, k2_ps, k2_sub, k2_exp, k2_done, col_ps, col_max = (
            sem("loaded"), sem("qkv"), sem("qkv_used"), sem("masked"), sem("k2_ps"), sem("k2_sub"), sem("k2_exp"), sem("k2_done"),
            sem("col_ps"), sem("col_max"))
        tr2, tr2_used, v0, s3, m3_ready, e3, tr3, tr3_a, tr3_d, t3 = (
            sem("tr2"), sem("tr2_used"), sem("v0"), sem("s3"), sem("m3_ready"), sem("e3"), sem("tr3"), sem("tr3_a"), sem("tr3_d"), sem("t3"))
        t3_done, kv_ps, kv_act, a_ready, p_ps, v_ps, w_ps, v_ready, w_ready = (
            sem("t3_done"), sem("kv_ps"), sem("kv_act"), sem("a_ready"), sem("p_ps"), sem("v_ps"), sem("w_ps"), sem("v_ready"), sem("w_ready"))
        g_ps, g_done, y_ps, y_done, s1, e1_sub, e1_exp, tr1, tr1_used, o1, o1_used = (
            sem("g_ps"), sem("g_done"), sem("y_ps"), sem("y_done"), sem("s1"), sem("e1_sub"), sem("e1_exp"), sem("tr1"), sem("tr1_used"),
            sem("o1"), sem("o1_used"))
        chain_sem = sem("chain")
        block = ctx.enter_context(nc.Block())
        LOADS = [(wq, "wq"), (wk, "wk"), (wv, "wv"), (bq, "bq"), (bk, "bk"), (bv, "bv"), (head_mask, "head_mask"), (eyes, "eyes")]
        SC = float(np.float32(1.0 / np.sqrt(np.sqrt(D3))))
        QUARTER = 0.25

        @block.sync
        def _(sp):
            for dst, name in LOADS:
                sp.dma_start(dst[:], dram[name]).then_inc(loaded, 16)

        @block.tensor
        def _(pe):
            pe.wait_ge(loaded, 16 * len(LOADS))
            for i in range(12):
                if i >= 8:
                    pe.wait_ge(qkv_used, i - 7)
                if i < 8:
                    c = i % 4
                    step = nc.tensor.matmul(bank(i), (wq if i < 4 else wk)[:], XT[:, CH * c:CH * c + CH], start=True, stop=True)
                else:
                    for t in range(4 * (i - 8), 4 * (i - 8) + 4):
                        step = nc.tensor.matmul(ps[:, i - 8, P * (t % 4):P * (t % 4) + P], XT[:, P * t:P * t + P], wv[:],
                                                start=True, stop=True)
                step.then_inc(qkv, 1)
            pe.wait_ge(masked, 4)
            pe.wait_ge(qkv_used, 12)
            for g in range(NG):
                b, o = g // 4, 4 * (g % 4)
                nc.tensor.matmul(bank(g), q_lm[:, LM * b:LM * b + LM], KM[:, b, o:o + 4, :], start=True, stop=True).then_inc(k2_ps, 1)
            for g in range(NG):
                pe.wait_ge(k2_done, g + 1)
                nc.tensor.matmul(bank(g), ones[:], W[:, g], start=True, stop=True).then_inc(col_ps, 1)
            for g in range(NG):
                pe.wait_ge(col_max, g + 1)
                for i in range(4):
                    step = nc.tensor.transpose(ps[:, g, LM * i:LM * i + LM], W[:, g, i, :], ident[:])
                step.then_inc(tr2, 1)

            def scores3(u):
                b, h = divmod(u, H3)
                pe.wait_ge(tr2_used, NG) if u < 2 else pe.wait_ge(e3, u - 1)
                for i in range(2):
                    step = nc.tensor.matmul(bank(2 * (u % 2) + i), QM[:, b, h, :], KT[:, L * b + CH * i:L * b + CH * i + CH], start=True, stop=True)
                step.then_inc(s3, 1)

            scores3(0)
            for u in range(NU):
                b, h = divmod(u, H3)
                if u + 1 < NU:
                    scores3(u + 1)
                pe.wait_ge(e3, u + 1)
                if u:
                    pe.wait_ge(tr3_a, u)
                    pe.wait_ge(tr3_d, u)
                for i in range(NB):
                    step = nc.tensor.transpose(ps[:, 4 + i // 4, LM * (i % 4):LM * (i % 4) + LM], P3[:, L * (u % 2) + P * i:L * (u % 2) + P * i + P], ident[:])
                step.then_inc(tr3, 1)
                pe.wait_ge(tr3_a, u + 1)
                pe.wait_ge(tr3_d, u + 1)
                for i in range(NB):
                    step = nc.tensor.matmul(ps[:, 6, E1 * u:E1 * u + E1], P3T[:, L * (u % 2) + P * i:L * (u % 2) + P * i + P], V9[:, NB * b + i, h, :],
                                            start=i == 0, stop=i == NB - 1)
                step.then_inc(t3, 1)
            pe.wait_ge(t3_done, 1)
            pe.wait_ge(v0, NG)
            bnk = [0]

            def four(lhs, rhs, g, used, value, done):
                if used is not None:
                    pe.wait_ge(used, value)
                for i in range(4):
                    step = nc.tensor.matmul(ps[:, g, LM * i:LM * i + LM], lhs[:, g, i, :], rhs[:, g, i, :], start=True, stop=True)
                step.then_inc(done, 1)

            for it in range(ITERS):
                last = it == ITERS - 1
                for g in range(NG):
                    if it:
                        pe.wait_ge(v_ready, NG * (it - 1) + g + 1)
                    four(K2T, V, g, w_ready if it else None, NG * (it - 1) + g + 1, kv_ps)
                for k in range(2):
                    for g in range(NG):
                        pe.wait_ge(kv_act, NG * it + g + 1)
                        four(KV, A, g, a_ready, 3 * NG * it + NG * k + g + 1, p_ps)
                if not last:
                    for g in range(NG):
                        four(W, A, g, a_ready, 3 * NG * it + 2 * NG + g + 1, v_ps)
                    for g in range(NG):
                        four(A, W, g, v_ready, NG * it + g + 1, w_ps)
            for g in range(NG):
                pe.wait_ge(a_ready, 3 * NG * (ITERS - 1) + 2 * NG + g + 1)
            for u in range(NU):
                step = nc.tensor.matmul(ps[:, 0, D3 * u:D3 * u + D3], A[:, u // 4, u % 4, :], T3[:, u, :], start=True, stop=True)
            step.then_inc(g_ps, 1)
            pe.wait_ge(g_done, 1)
            for u in range(NU):
                step = nc.tensor.matmul(ps[:, 1, D3 * u:D3 * u + D3], W[:, u // 4, u % 4, :], G[:, u, :], start=True, stop=True)
            step.then_inc(y_ps, 1)

            def scores1(u):
                t, half = divmod(u, 2)
                b = t // NB
                pe.wait_ge(y_done, 1) if u < 2 else pe.wait_ge(e1_sub, u - 1)
                for i in range(2):
                    step = nc.tensor.matmul(bank(2 * (u % 2) + i), QT[:, P * t:P * t + P], KM[:, b, 8 * half + 4 * i:8 * half + 4 * i + 4, :], start=True, stop=True)
                step.then_inc(s1, 1)

            def turn(u):
                pe.wait_ge(e1_exp, u + 1)
                if u:
                    pe.wait_ge(tr1_used, u)
                for i in range(8):
                    step = nc.tensor.transpose(ps[:, 4 + i // 4, LM * (i % 4):LM * (i % 4) + LM], E[:, u % 2, i, :], ident[:])
                step.then_inc(tr1, 1)

            scores1(0)
            scores1(1)
            turn(0)
            for u in range(2 * NT):
                t, half = divmod(u, 2)
                b = t // NB
                if u + 2 < 2 * NT:
                    scores1(u + 2)
                pe.wait_ge(tr1_used, u + 1)
                if half == 0 and t >= 2:
                    pe.wait_ge(o1_used, t - 1)
                for i in range(8):
                    h = 8 * half + i
                    step = nc.tensor.matmul(ps[:, 6 + t % 2, E1 * h:E1 * h + E1], ET[:, u % 2, i, :], Y9[:, H3 * b + h, :], start=True, stop=True)
                if half:
                    step.then_inc(o1, 1)
                if u + 1 < 2 * NT:
                    turn(u + 1)

        @block.scalar
        def _(act):
            act.wait_ge(loaded, 16 * len(LOADS))
            for g in range(NG):
                act.wait_ge(k2_sub, g + 1)
                nc.scalar.activation(W[:, g], W[:, g], ACT.Exp).then_inc(k2_exp, 1)
            for g in range(NG):
                act.wait_ge(tr2, g + 1)
                nc.scalar.activation(K2T[:, g].rearrange("p h m -> p (h m)"), bank(g), ACT.Copy).then_inc(tr2_used, 1)
            for u in range(NU):
                act.wait_ge(m3_ready, u + 1)
                if u >= 2:
                    act.wait_ge(tr3, u - 1)
                nc.scalar.activation(P3[:, L * (u % 2):L * (u % 2) + L], bank(2 * (u % 2), 2), ACT.Exp, bias=m3[:, u % 2, 1:2]).then_inc(e3, 1)
                act.wait_ge(tr3, u + 1)
                if u >= 2:
                    act.wait_ge(t3, u - 1)
                nc.scalar.activation(P3T[:, L * (u % 2):L * (u % 2) + CH], bank(4), ACT.Copy).then_inc(tr3_a, 1)
            for it in range(ITERS):
                for g in range(NG):
                    act.wait_ge(kv_ps, NG * it + g + 1)
                    if it == 0:
                        act.wait_ge(t3, NU)
                    nc.scalar.activation(KV[:, g].rearrange("p h m -> p (h m)"), bank(g), ACT.Copy).then_inc(kv_act, 1)
                if it == ITERS - 1:
                    break
                for g in range(NG):
                    act.wait_ge(v_ps, NG * it + g + 1)
                    nc.scalar.activation(V[:, g].rearrange("p h m -> p (h m)"), bank(g), ACT.Copy, scale=QUARTER).then_inc(v_ready, 1)
                for g in range(NG):
                    act.wait_ge(w_ps, NG * it + g + 1)
                    nc.scalar.activation(W[:, g].rearrange("p h m -> p (h m)"), bank(g), ACT.Copy, scale=QUARTER).then_inc(w_ready, 1)
            act.wait_ge(g_ps, 1)
            nc.scalar.activation(G[:].rearrange("p u d -> p (u d)"), ps[:, 0, 0:NU * D3], ACT.Copy).then_inc(g_done, 1)
            for u in range(2 * NT):
                act.wait_ge(e1_sub, u + 1)
                nc.scalar.activation(E[:, u % 2], E[:, u % 2], ACT.Exp).then_inc(e1_exp, 1)
                act.wait_ge(tr1, u + 1)
                if u >= 4:
                    act.wait_ge(o1, (u - 2) // 2)
                nc.scalar.activation(ET[:, u % 2].rearrange("p h m -> p (h m)"), bank(4, 2), ACT.Copy).then_inc(tr1_used, 1)

        @block.vector
        def _(dve):
            link = Chain(dve, chain_sem)
            nc.vector.memset(ones[:], 1.0)
            nc.vector.memset(V9[:, :, :, D3:E1], 1.0)
            nc.vector.memset(Y9[:, :, D3:E1], 1.0)
            dve.wait_ge(loaded, 16 * len(LOADS))
            for i in range(12):
                dve.wait_ge(qkv, i + 1)
                if i < 8:
                    dst, bias = (QT, bq) if i < 4 else (KT, bk)
                    c = i % 4
                    step = nc.vector.tensor_scalar(dst[:, CH * c:CH * c + CH], bank(i), bias[:, 0:1], SC, ALU.add, ALU.mult)
                else:
                    c = i - 8
                    for t in range(4):
                        step = nc.vector.tensor_tensor(V9[:, 4 * c + t, :, 0:D3], ps[:, c, P * t:P * t + P].rearrange("p (h d) -> p h d", h=H3),
                                                       bv[:].rearrange("p (h d) -> p h d", h=H3), ALU.add)
                step.then_inc(qkv_used, 1)
            dve.wait_ge(qkv_used, 12)
            for src, lm in ((QT, q_lm), (KT, k_lm)):
                step = nc.vector.tensor_reduce(lm[:], src[:].rearrange("p (m s) -> p m s", s=SEG), AX.X, ALU.add)
            link(step)
            for lm in (q_lm, k_lm):
                step = nc.vector.tensor_scalar(lm[:], lm[:], 1.0 / SEG, None, ALU.mult)
            link(step)
            for b in range(B):
                for lm, dst in ((q_lm, QM), (k_lm, KM)):
                    nc.vector.tensor_tensor(dst[:, b], lm[:, LM * b:LM * b + LM].rearrange("p (o m) -> p o m", o=1).to_broadcast([P, H3, LM]),
                                            head_mask[:].to_broadcast([P, H3, LM]), ALU.mult).then_inc(masked, 1)
            for g in range(NG):
                src = ps[:, g, :].rearrange("p (h m) -> p h m", h=4)
                dve.wait_ge(k2_ps, g + 1)
                link(nc.vector.tensor_reduce(m2[:, g, :, 0], src, AX.X, ALU.max))
                nc.vector.tensor_tensor(W[:, g], src, m2[:, g].to_broadcast([P, 4, LM]), ALU.subtract).then_inc(k2_sub, 1)
            for g in range(NG):
                dve.wait_ge(k2_exp, g + 1)
                link(nc.vector.tensor_reduce(s2[:, g, :, 0], W[:, g], AX.X, ALU.add))
                link(nc.vector.reciprocal(s2[:, g], s2[:, g]))
                nc.vector.tensor_tensor(W[:, g], W[:, g], s2[:, g].to_broadcast([P, 4, LM]), ALU.mult).then_inc(k2_done, 1)
            for g in range(NG):
                dve.wait_ge(col_ps, g + 1)
                nc.vector.tensor_reduce(cmax[:, g:g + 1], bank(g), AX.X, ALU.max).then_inc(col_max, 1)
            dve.wait_ge(col_max, NG)
            link(nc.vector.tensor_reduce(rc[:, 0:1], cmax[:], AX.X, ALU.max))
            link(nc.vector.reciprocal(rc[:, 1:2], rc[:, 0:1]))
            dve.wait_ge(tr2_used, NG)
            for g in range(NG):
                nc.vector.tensor_scalar(V[:, g], K2T[:, g], rc[:, 1:2], None, ALU.mult)
                nc.vector.tensor_scalar(W[:, g], W[:, g], rc[:, 1:2], None, ALU.mult).then_inc(v0, 1)
            dve.wait_ge(v0, NG)
            for u in range(NU):
                dve.wait_ge(s3, u + 1)
                if u >= 2:
                    dve.wait_ge(e3, u - 1)
                link(nc.vector.tensor_reduce(m3[:, u % 2, 0:1], bank(2 * (u % 2), 2), AX.X, ALU.max))
                nc.vector.tensor_scalar(m3[:, u % 2, 1:2], m3[:, u % 2, 0:1], -1.0, None, ALU.mult).then_inc(m3_ready, 1)
                if u:
                    dve.wait_ge(tr3, u)
                    if u >= 3:
                        dve.wait_ge(t3, u - 2)
                    nc.vector.tensor_copy(P3T[:, L * ((u - 1) % 2) + CH:L * ((u - 1) % 2) + L], bank(5)).then_inc(tr3_d, 1)
            dve.wait_ge(tr3, NU)
            dve.wait_ge(t3, NU - 2)
            nc.vector.tensor_copy(P3T[:, L * ((NU - 1) % 2) + CH:L * ((NU - 1) % 2) + L], bank(5)).then_inc(tr3_d, 1)
            dve.wait_ge(t3, NU)
            t3v = ps[:, 6, 0:NU * E1].rearrange("p (u e) -> p u e", e=E1)
            link(nc.vector.reciprocal(r3[:], t3v[:, :, D3:E1]))
            nc.vector.tensor_tensor(T3[:], t3v[:, :, 0:D3], r3[:].to_broadcast([P, NU, D3]), ALU.mult).then_inc(t3_done, 1)
            for it in range(ITERS):
                for k in range(3):
                    for g in range(NG):
                        if k == 0:
                            dve.wait_ge(kv_act, NG * it + g + 1)
                        else:
                            dve.wait_ge(p_ps, 2 * NG * it + NG * (k - 1) + g + 1)
                        src = ps[:, g, :].rearrange("p (h m) -> p h m", h=4)
                        nc.vector.scalar_tensor_tensor(A[:, g], src, -1.0, eyes[:, k].to_broadcast([P, 4, P]), ALU.mult, ALU.add)\
                            .then_inc(a_ready, 1)
            dve.wait_ge(y_ps, 1)
            nc.vector.tensor_scalar(Y9[:, :, 0:D3], ps[:, 1, 0:NU * D3].rearrange("p (u d) -> p u d", d=D3), QUARTER, None, ALU.mult)\
                .then_inc(y_done, 1)

            def finish(t):
                dve.wait_ge(o1, t + 1)
                ov = ps[:, 6 + t % 2, 0:H3 * E1].rearrange("p (h e) -> p h e", e=E1)
                link(nc.vector.reciprocal(r1[:, t % 2], ov[:, :, D3:E1]))
                nc.vector.tensor_tensor(Y[:, t, :].rearrange("p (h d) -> p h d", h=H3), ov[:, :, 0:D3], r1[:, t % 2].to_broadcast([P, H3, D3]),
                                        ALU.mult).then_inc(o1_used, 1)

            for u in range(2 * NT):
                src = ps[:, 2 * (u % 2):2 * (u % 2) + 2, :].rearrange("p a (h m) -> p (a h) m", m=LM)
                dve.wait_ge(s1, u + 1)
                link(nc.vector.tensor_reduce(m1[:, u % 2, :, 0], src, AX.X, ALU.max))
                if u >= 2:
                    dve.wait_ge(tr1, u - 1)
                nc.vector.tensor_tensor(E[:, u % 2], src, m1[:, u % 2].to_broadcast([P, 8, LM]), ALU.subtract).then_inc(e1_sub, 1)
                if u % 2 == 1 and u >= 3:
                    finish(u // 2 - 1)
            finish(NT - 1)


NE = 8
HID = 4 * P
HC = HID // P


def moe_stage(nc, sems, XT, Y, dram):
    with ExitStack() as ctx:
        def sb(name, shape, dt=FP32):
            return ctx.enter_context(nc.sbuf_tensor(f"e_{name}", shape, dt))

        def sem(name):
            return sems.enter_context(nc.semaphore(f"e_{name}"))

        router, w1, w2, prio = sb("router", [P, NE]), sb("w1", [P, NE, HID]), sb("w2", [P, NE, HC, P]), sb("prio", [P, 1, NE])
        pr, eq, f1, f2, p2 = (sb(n, [P, NT, NE]) for n in ("pr", "eq", "f1", "f2", "p2"))
        mx, sm = sb("mx", [P, NT, 1]), sb("sm", [P, NT, 1])
        gate = sb("gate", [P, NT, NE])
        Hb = sb("H", [P, 2, HC, CH])
        ps = ctx.enter_context(nc.psum_tensor("e_ps", [P, 8, CH], FP32))
        loaded, w1_in, w2_in, lg_ps, sub_done, exp_done, gelu, up, down, scaled, chain_sem = (
            sem("loaded"), sem("w1_in"), sem("w2_in"), sem("lg_ps"), sem("sub_done"), sem("exp_done"), sem("gelu"), sem("up"), sem("down"),
            sem("scaled"), sem("chain"))
        block = ctx.enter_context(nc.Block())
        units = [(e, c) for e in range(NE) for c in range(T // CH)]
        logits = ps[:, 6, 0:NT * NE].rearrange("p (t e) -> p t e", e=NE)

        @block.sync
        def _(sp):
            sp.dma_start(router[:], dram["router"]).then_inc(loaded, 16)
            sp.dma_start(prio[:], dram["prio"]).then_inc(loaded, 16)
            sp.dma_start(w1[:], dram["w1"]).then_inc(w1_in, 16)
            sp.dma_start(w2[:], dram["w2"]).then_inc(w2_in, 16)

        @block.tensor
        def _(pe):
            pe.wait_ge(loaded, 32)
            for t in range(NT):
                step = nc.tensor.matmul(ps[:, 6, NE * t:NE * t + NE], XT[:, P * t:P * t + P], router[:], start=True, stop=True)
            step.then_inc(lg_ps, 1)
            pe.wait_ge(w1_in, 16)

            def hidden(k):
                e, c = units[k]
                for j in range(HC):
                    if k:
                        pe.wait_ge(gelu, HC * (k - 1) + j + 1)
                    nc.tensor.matmul(ps[:, j, :], w1[:, e, P * j:P * j + P], XT[:, CH * c:CH * c + CH], start=True, stop=True).then_inc(up, 1)

            hidden(0)
            pe.wait_ge(w2_in, 16)
            for k, (e, c) in enumerate(units):
                if k + 1 < len(units):
                    hidden(k + 1)
                pe.wait_ge(gelu, HC * (k + 1))
                if k >= 2:
                    pe.wait_ge(scaled, k - 1)
                for t in range(4):
                    for j in range(HC):
                        step = nc.tensor.matmul(ps[:, 4 + k % 2, P * t:P * t + P], Hb[:, k % 2, j, P * t:P * t + P], w2[:, e, j, :],
                                                start=j == 0, stop=j == HC - 1)
                step.then_inc(down, 1)

        @block.scalar
        def _(act):
            act.wait_ge(sub_done, 1)
            nc.scalar.activation(pr[:], pr[:], ACT.Exp).then_inc(exp_done, 1)
            for k, (e, c) in enumerate(units):
                if k >= 2:
                    act.wait_ge(down, k - 1)
                for j in range(HC):
                    act.wait_ge(up, HC * k + j + 1)
                    nc.scalar.activation(Hb[:, k % 2, j, :], ps[:, j, :], ACT.Gelu).then_inc(gelu, 1)

        @block.vector
        def _(dve):
            link = Chain(dve, chain_sem)
            full = [P, NT, NE]
            dve.wait_ge(lg_ps, 1)
            link(nc.vector.tensor_reduce(mx[:, :, 0], logits, AX.X, ALU.max))
            nc.vector.tensor_tensor(pr[:], logits, mx[:].to_broadcast(full), ALU.subtract).then_inc(sub_done, 1)
            dve.wait_ge(exp_done, 1)
            link(nc.vector.tensor_reduce(sm[:, :, 0], pr[:], AX.X, ALU.add))
            link(nc.vector.reciprocal(sm[:], sm[:]))
            link(nc.vector.tensor_tensor(pr[:], pr[:], sm[:].to_broadcast(full), ALU.mult))
            for src, found in ((pr, f1), (p2, f2)):
                link(nc.vector.tensor_reduce(mx[:, :, 0], src[:], AX.X, ALU.max))
                link(nc.vector.tensor_tensor(eq[:], src[:], mx[:].to_broadcast(full), ALU.is_equal))
                link(nc.vector.tensor_tensor(eq[:], eq[:], prio[:].to_broadcast(full), ALU.mult))
                link(nc.vector.tensor_reduce(mx[:, :, 0], eq[:], AX.X, ALU.max))
                link(nc.vector.tensor_tensor(found[:], eq[:], mx[:].to_broadcast(full), ALU.is_equal))
                if src is pr:
                    link(nc.vector.scalar_tensor_tensor(p2[:], f1[:], -2.0, pr[:], ALU.mult, ALU.add))
            link(nc.vector.tensor_tensor(f1[:], f1[:], f2[:], ALU.add))
            link(nc.vector.tensor_tensor(gate[:], pr[:], f1[:], ALU.mult))
            for k, (e, c) in enumerate(units):
                dve.wait_ge(down, k + 1)
                if k >= 4:
                    dve.wait_ge(scaled, k - 3)
                for i in range(4):
                    t = 4 * c + i
                    src = ps[:, 4 + k % 2, P * i:P * i + P]
                    if e == 0:
                        step = nc.vector.tensor_scalar(Y[:, t, :], src, gate[:, t, e:e + 1], None, ALU.mult)
                    else:
                        step = nc.vector.scalar_tensor_tensor(Y[:, t, :], src, gate[:, t, e:e + 1], Y[:, t, :], ALU.mult, ALU.add)
                step.then_inc(scaled, 1)



STAGES = [0, 1, 2, 3]


def load_stage(nc, sems, X, ident, dram):
    with ExitStack() as ctx:
        loaded = sems.enter_context(nc.semaphore("x_loaded"))
        block = ctx.enter_context(nc.Block())

        @block.sync
        def _(sp):
            sp.dma_start(X[:], dram["x"].rearrange("(t p) d -> p t d", p=P)).then_inc(loaded, 16)
            sp.dma_start(ident[:], dram["ident"]).then_inc(loaded, 16)
            sp.wait_ge(loaded, 32)


def program(nc, dram, out, upto=9):
    with ExitStack() as ctx, ExitStack() as sems:
        X = ctx.enter_context(nc.sbuf_tensor("X", [P, NT, P], FP32))
        Y = ctx.enter_context(nc.sbuf_tensor("Y", [P, NT, P], FP32))
        XT = ctx.enter_context(nc.sbuf_tensor("XT", [P, T], FP32))
        ident = ctx.enter_context(nc.sbuf_tensor("ident", [P, P], FP32))
        shared = NormSemaphores(nc, sems)
        load_stage(nc, sems, X, ident, dram)
        stages = STAGES
        norm_stage(nc, shared, "n0", X, None, XT, ident)
        for i, s in enumerate(stages):
            if s == 0:
                mamba_stage(nc, sems, XT, Y, ident, None, dram)
            if s == 1:
                local_stage(nc, sems, XT, Y, ident, dram)
            if s == 2:
                nystrom_stage(nc, sems, XT, Y, ident, dram)
            if s == 3:
                moe_stage(nc, sems, XT, Y, dram)
            if i + 1 < len(stages):
                norm_stage(nc, shared, f"n{i + 1}", X, Y, XT, ident)
        norm_stage(nc, shared, "n9", X, Y, None, ident, store=out.rearrange("(t p) d -> p t d", p=P))


def kernel(**inputs):
    import concourse.bacc as _bacc
    from concourse import bass_utils
    import ml_dtypes
    a = {k: np.asarray(v) for k, v in inputs.items()}
    split = lambda v: np.ascontiguousarray(v.reshape((DC, P) + v.shape[1:]).swapaxes(0, 1))
    sel = np.zeros((96, 2 * NS, P), ml_dtypes.bfloat16)
    for r in range(96):
        sel[r, r % 32, :] = 1
    arrays = {
        "x": a["L0_attn_x"].reshape(T, P), "ident": np.eye(P, dtype=np.float32), "sel": sel,
        "w_in": np.ascontiguousarray(a["L0_attn_W_in"].T), "w_x": split(np.ascontiguousarray(a["L0_attn_W_x"].T)),
        "w_out": split(np.ascontiguousarray(a["L0_attn_W_out"].T)), "conv_w": split(a["L0_attn_conv_w"].reshape(DI, TAPS)),
        "conv_b": split(a["L0_attn_conv_b"]), "w_dt": split(a["L0_attn_w_dt"]), "b_dt": split(a["L0_attn_b_dt"]),
        "wq": a["L1_attn_Wq"].T, "wk": a["L1_attn_Wk"].T, "wv": a["L1_attn_Wv"].T, "bq": a["L1_attn_bq"].reshape(P, 1),
        "bk": a["L1_attn_bk"].reshape(P, 1), "bv": np.broadcast_to(a["L1_attn_bv"], (P, P)),
        "head_mask": np.repeat(np.eye(H3, dtype=np.float32), D3, axis=0).reshape(P, H3, 1),
        "eyes": np.stack([np.eye(P, dtype=np.float32) * k for k in (7, 15, 13)], axis=1).reshape(P, 3, 1, P),
        "router": a["L1_ffn_router_w"].T, "w1": a["L1_ffn_w1"].transpose(2, 0, 1),
        "w2": a["L1_ffn_w2"].reshape(NE, P, HC, P).transpose(3, 0, 2, 1),
        "prio": np.broadcast_to(np.arange(NE, 0, -1, dtype=np.float32), (P, 1, NE)),
        "a_log": split(a["L0_attn_A_log"]), "d_par": split(a["L0_attn_D_param"]),
    }
    qkv = a["L0_ffn_Wqkv"]
    half = np.arange(0, D2, 2, dtype=np.float32)
    freqs = np.arange(L, dtype=np.float32)[:, None] * (np.float32(1) / np.float32(10000.0) ** (half / np.float32(D2)))[None, :]
    freqs = np.concatenate([freqs, freqs], -1)
    power = ((np.arange(L) - L // 2) / (WIN // 2)).astype(np.float32)
    scale = ((half + np.float32(0.4 * D2)) / np.float32(1.4 * D2))[None, :] ** power[:, None]
    scale = np.concatenate([scale, scale], -1)
    sign = np.where(np.arange(D2) < D2 // 2, -1, 1).astype(np.float32)
    cos, sin = np.cos(freqs), np.sin(freqs) * sign
    base = np.stack([cos * scale, sin * scale, cos / scale, sin / scale]).astype(np.float32)
    q, key = np.arange(P)[:, None] % WIN, np.arange(2 * WIN)[None, :] - WIN
    seen = (key <= q) & (q - key <= WIN)
    first = seen & ((np.arange(P)[:, None] >= WIN) | (key >= 0))
    swap = lambda v: np.concatenate([v[:, D2 // 2:], v[:, :D2 // 2]], -1)
    qs, ks = a["L0_ffn_q_scale"], a["L0_ffn_k_scale"]
    chunks = lambda v: np.pad(v, [(0, 0), (0, FC * P - FF)]).reshape(DEPTH, FC, P).transpose(0, 2, 1)
    arrays |= {
        "wqk": qkv[:, :, :2 * INNER], "wvl": qkv[:, :, 2 * INNER:].reshape(DEPTH, P, HP, 2, D2).transpose(0, 1, 3, 2, 4).reshape(DEPTH, P, 2, HP * D2),
        "wo": a["L0_ffn_Wo"].reshape(DEPTH, HP, P, P).transpose(0, 2, 1, 3), "w1l": a["L0_ffn_W1"],
        "w2l": np.pad(a["L0_ffn_W2"], [(0, 0), (0, FC * P - FF), (0, 0)]).reshape(DEPTH, FC, P, P).transpose(0, 2, 1, 3),
        "vec": np.concatenate([a["L0_ffn_ln_g"][:, :, None], a["L0_ffn_ln_b"][:, :, None], chunks(a["L0_ffn_b1"][:, :FF]), chunks(a["L0_ffn_b1"][:, FF:]),
                               a["L0_ffn_b2"][:, :, None]], axis=2),
        "scales": np.broadcast_to(np.stack([qs, swap(qs), ks, swap(ks)], 1)[:, None, :, None, :], (DEPTH, P, 4, 1, D2)),
        "base": base.reshape(4, NB, P, D2).transpose(2, 0, 1, 3),
        "mask": np.where(np.stack([first, seen]), 0, -3e38).astype(np.float32).transpose(1, 0, 2).reshape(P, 2, 1, 2 * WIN),
    }
    arrays = {n: np.ascontiguousarray(v) for n, v in arrays.items()}
    nc = _bacc.Bacc("TRN2", target_bir_lowering=False, num_devices=1)
    dram = {n: nc.dram_tensor(f"in_{n}", v.shape, mybir.dt.from_np(v.dtype), kind="ExternalInput").ap() for n, v in arrays.items()}
    out = nc.dram_tensor("out", (T, P), FP32, kind="ExternalOutput").ap()
    program(nc, dram, out)
    r = bass_utils.run_bass_kernel_spmd(nc, [{f"in_{n}": v for n, v in arrays.items()}], core_ids=[0])
    return r.results[0]["out"].reshape(B, L, P)
```

```python
from contextlib import ExitStack

import numpy as np
import concourse.bass as bass
from concourse import mybir

FP32 = mybir.dt.float32
BF16 = mybir.dt.bfloat16
F32R = mybir.dt.float32r
ACT = mybir.ActivationFunctionType
ALU = mybir.AluOpType
AX = mybir.AxisListType

P = 128
B, L = 2, 1024
T = B * L
NT = T // P
NB = L // P
CH = 512
EPS = 1e-5

DI = 256
DC = DI // P
NS = 16
TAPS = 4
DEEP = 4


class Chain:

    def __init__(self, engine, sem, count=0):
        self.engine, self.sem, self.count = engine, sem, count

    def __call__(self, step):
        self.count += 1
        step.then_inc(self.sem, 1)
        self.engine.wait_ge(self.sem, self.count)


class NormSemaphores:

    def __init__(self, nc, sems):
        self.sems = [sems.enter_context(nc.semaphore(f"n_{n}")) for n in
                     ("var_ready", "std_ready", "z_ready", "x_ready", "turned", "copied", "stored", "chain")]
        self.stds = self.fours = self.chained = 0


def norm_stage(nc, shared, name, X, Y, ZT, ident, store=None, ahead=()):
    with ExitStack() as ctx:
        st = ctx.enter_context(nc.sbuf_tensor(f"{name}_stats", [P, NT, 6], FP32))
        mv = ctx.enter_context(nc.sbuf_tensor(f"{name}_mean_var", [P, NT, 2], FP32))
        sd = ctx.enter_context(nc.sbuf_tensor(f"{name}_std", [P, NT], FP32))
        rstd = ctx.enter_context(nc.sbuf_tensor(f"{name}_rstd", [P, NT], FP32))
        st2 = ctx.enter_context(nc.sbuf_tensor(f"{name}_stats2", [P, NT, 6], FP32))
        mv2 = ctx.enter_context(nc.sbuf_tensor(f"{name}_mean_var2", [P, NT, 2], FP32))
        sd2 = ctx.enter_context(nc.sbuf_tensor(f"{name}_std2", [P, NT], FP32))
        rstd2 = ctx.enter_context(nc.sbuf_tensor(f"{name}_rstd2", [P, NT], FP32))
        yn = ctx.enter_context(nc.sbuf_tensor(f"{name}_normed", [P, NT, P], FP32))
        Z = ctx.enter_context(nc.sbuf_tensor(f"{name}_normed2", [P, NT, P], FP32))
        ps = ctx.enter_context(nc.psum_tensor(f"{name}_ps", [P, 4, CH], FP32))
        var_ready, std_ready, z_ready, x_ready, turned, copied, stored, chain_sem = shared.sems
        stds, fours, chained = shared.stds, shared.fours, shared.chained
        block = ctx.enter_context(nc.Block())
        passes = 1 if Y is not None else 0

        @block.vector
        def _(dve):
            link = Chain(dve, chain_sem, chained)

            def normalise(src, out, stats, mean_var, std, recip, turn, ready):
                for t in range(NT):
                    last = nc.vector.bn_stats(stats[:, t, :], src[:, t, :])
                link(last)
                for t in range(NT):
                    last = nc.vector.bn_aggr(mean_var[:, t, :], stats[:, t, :])
                link(last)
                nc.vector.tensor_scalar(std[:], mean_var[:, :, 1], EPS, None, ALU.add).then_inc(var_ready, 1)
                dve.wait_ge(std_ready, stds + turn)
                link(nc.vector.reciprocal(recip[:], std[:]))
                for t in range(NT):
                    step = nc.vector.tensor_scalar(out[:, t, :], src[:, t, :], mean_var[:, t, 0:1], recip[:, t:t + 1],
                                                   ALU.subtract, ALU.mult)
                    if ready is not None and t % 4 == 3:
                        step.then_inc(ready, 1)
                return step

            if Y is not None:
                link(normalise(Y, yn, st, mv, sd, rstd, 1, None))
                step = nc.vector.tensor_tensor(X[:], X[:], yn[:], ALU.add)
                if store is not None:
                    step.then_inc(x_ready, 1)
                else:
                    link(step)
            if store is None:
                normalise(X, Z, st2, mv2, sd2, rstd2, passes + 1, z_ready)
            shared.chained = link.count

        @block.scalar
        def _(act):
            if Y is not None:
                act.wait_ge(var_ready, stds + 1)
                nc.scalar.activation(sd[:], sd[:], ACT.Sqrt).then_inc(std_ready, 1)
            if store is None:
                act.wait_ge(var_ready, stds + passes + 1)
                nc.scalar.activation(sd2[:], sd2[:], ACT.Sqrt).then_inc(std_ready, 1)
                for g in range(4):
                    act.wait_ge(turned, fours + g + 1)
                    nc.scalar.activation(ZT[:, CH * g:CH * (g + 1)], ps[:, g, :], ACT.Copy).then_inc(copied, 1)

        @block.tensor
        def _(pe):
            if store is None:
                for g in range(4):
                    pe.wait_ge(z_ready, fours + g + 1)
                    for t in range(4 * g, 4 * g + 4):
                        step = nc.tensor.transpose(ps[:, g, P * (t % 4):P * (t % 4) + P], Z[:, t, :], ident[:])
                    step.then_inc(turned, 1)

        @block.sync
        def _(sp):
            for dst, src, done in ahead:
                sp.dma_start(dst, src).then_inc(done, 16)
            if store is not None:
                sp.wait_ge(x_ready, 1)
                sp.dma_start(store, X[:]).then_inc(stored, 16)
                sp.wait_ge(stored, 16)

        shared.stds += passes + (store is None)
        shared.fours += 4 * (store is None)


class MambaWeights:

    def __init__(self, nc, ctx, sems, dram):
        shapes = [("w_in", [P, 4 * P]), ("w_x", [P, DC, 2 * NS + 1]), ("w_out", [P, DC, P]), ("conv_w", [P, DC, TAPS]), ("conv_b", [P, DC]),
                  ("w_dt", [P, DC]), ("b_dt", [P, DC]), ("a_log", [P, DC, NS]), ("d_par", [P, DC]), ("sel", [96, 2 * NS, P])]
        self.buffers = [ctx.enter_context(nc.sbuf_tensor(f"m_{n}", shape, BF16 if n == "sel" else FP32)) for n, shape in shapes]
        self.loaded = sems.enter_context(nc.semaphore("m_loaded"))
        self.loads = [(buf[:], dram[n], self.loaded) for buf, (n, _) in zip(self.buffers, shapes)]


def mamba_stage(nc, sems, shared, XT, Y, ident, weights):
    with ExitStack() as ctx:
        def sb(name, shape, dt=FP32):
            return ctx.enter_context(nc.sbuf_tensor(f"m_{name}", shape, dt))

        def sem(name):
            return sems.enter_context(nc.semaphore(f"m_{name}"))

        w_in, w_x, w_out, conv_w, conv_b, w_dt, b_dt, a_log, d_par, sel = weights.buffers
        dt_col = sb("dt_col", [P, DC, P])
        A = sb("A", [P, DC, NS])
        pad = sb("pad", [P, DC, B, TAPS - 1 + L])
        conv = sb("conv", [P, DC, B, L])
        xc = sb("xc", [P, DC, B, L])
        zs = sb("zs", [P, DC, B, L])
        delta = sb("delta", [P, DC, B, L])
        du = conv
        ex, u = pad, sb("u", [P, DC, B, L])
        bc = sb("bc", [32, 3, T], BF16)
        hc = sb("hc", [P, DEEP, L])
        rest = hc[0:32].rearrange("p (a b) l -> p a (b l)", a=2)
        stack = sb("stack", [96, T], BF16)
        dA = sb("dA", [P, 2, L])
        dbx = sb("dbx", [P, 2, L])
        h = sb("h", [P, DEEP, L])
        c_sb = sb("c_sb", [P, 2, L])
        yT = u
        ps = ctx.enter_context(nc.psum_tensor("m_ps", [P, 8, CH], FP32))
        loaded, ready0, xz, xz_used, conved, silued = weights.loaded, sem("ready0"), sem("xz"), sem("xz_used"), sem("conved"), sem("silued")
        bc_ps, dt_ps, split, stacked, dt_used, soft, softed = sem("bc_ps"), sem("dt_ps"), sem("split"), sem("stacked"), sem("dt_used"), sem("soft"), sem("softed")
        b_ready, c_ready, c_copied, dA_ready, dbx_done, scanned, hc_done, y_acc, y_used = (
            sem("b_ready"), sem("c_ready"), sem("c_copied"), sem("dA_ready"), sem("dbx_done"), sem("scanned"), sem("hc_done"),
            sem("y_acc"), sem("y_used"))
        out_ps, du_done, achain_sem = sem("out_ps"), sem("du_done"), sem("achain")
        block = ctx.enter_context(nc.Block())
        LOADED = 16 * len(weights.loads)
        units = [(b, n, dc) for b in range(B) for n in range(NS) for dc in range(DC)]
        PROJECTIONS = [(2 * gate + e, c) for gate in range(2) for c in range(4) for e in range(2)]

        @block.tensor
        def _(pe):
            pe.wait_ge(loaded, LOADED)
            for i, (e, c) in enumerate(PROJECTIONS):
                if i >= 8:
                    pe.wait_ge(xz_used, i - 7)
                nc.tensor.matmul(ps[:, i % 8, :], w_in[:, P * e:P * e + P], XT[:, CH * c:CH * c + CH], start=True,
                                 stop=True).then_inc(xz, 1)
            pe.wait_ge(silued, DC)
            pe.wait_ge(xz_used, 16)
            pe.wait_ge(ready0, 1)
            for c in range(4):
                b, o = c // 2, CH * (c % 2)
                for dc in range(DC):
                    step = nc.tensor.matmul(ps[0:32, c, :], w_x[:, dc, 0:32], xc[:, dc, b, o:o + CH], start=dc == 0, stop=dc == DC - 1)
                step.then_inc(bc_ps, 1)
            for c in range(4):
                b, o = c // 2, CH * (c % 2)
                for dc in range(DC):
                    step = nc.tensor.matmul(ps[:, 4 + c, :], dt_col[:, dc, :], xc[:, dc, b, o:o + CH], start=dc == 0, stop=dc == DC - 1)
                step.then_inc(dt_ps, 1)
            pe.wait_ge(stacked, 3)
            pe.wait_ge(dt_used, 4)
            pe.wait_ge(split, 1)

            def spread_b(v):
                b, n = divmod(v, NS)
                if v >= 1:
                    pe.wait_ge(dbx_done, DC * v)
                for i in range(2):
                    step = nc.tensor.matmul(ps[:, 4 + i, :], sel[:, n, :], stack[:, L * b + CH * i:L * b + CH * i + CH], start=True, stop=True)
                step.then_inc(b_ready, 1)

            def spread_c(v):
                b, n = divmod(v, NS)
                if v >= 1:
                    pe.wait_ge(c_copied, v)
                for i in range(2):
                    step = nc.tensor.matmul(ps[:, 6 + i, :], sel[:, NS + n, :], stack[:, L * b + CH * i:L * b + CH * i + CH], start=True, stop=True)
                step.then_inc(c_ready, 1)

            def sum_y(k):
                b, n, dc = units[k]
                if n == 0 and b:
                    pe.wait_ge(y_used, DC * b)
                pe.wait_ge(hc_done, k + 1)
                for i in range(2):
                    step = nc.tensor.matmul(ps[:, 2 * dc + i, :], ident[:], hc[:, k % DEEP, CH * i:CH * i + CH], start=n == 0, stop=n == NS - 1)
                step.then_inc(y_acc, 1)

            spread_b(0)
            spread_c(0)
            for v in range(B * NS + 1):
                if v + 1 < B * NS:
                    spread_b(v + 1)
                if v:
                    sum_y(DC * (v - 1))
                if v + 1 < B * NS:
                    spread_c(v + 1)
                if v:
                    sum_y(DC * (v - 1) + 1)
            pe.wait_ge(y_used, DC * B)
            for t in range(NT):
                b, o = t // NB, P * (t % NB)
                for dc in range(DC):
                    step = nc.tensor.matmul(ps[:, t // 4, P * (t % 4):P * (t % 4) + P], yT[:, dc, b, o:o + P], w_out[:, dc, :],
                                            start=dc == 0, stop=dc == DC - 1)
                if t % 4 == 3:
                    step.then_inc(out_ps, 1)

        @block.scalar
        def _(act):
            act.wait_ge(loaded, LOADED)
            link = Chain(act, achain_sem)
            for i, (e, c) in enumerate(PROJECTIONS):
                b, o = c // 2, CH * (c % 2)
                act.wait_ge(xz, i + 1)
                if e < 2:
                    step = nc.scalar.activation(pad[:, e, b, TAPS - 1 + o:TAPS - 1 + o + CH], ps[:, i % 8, :], ACT.Copy)
                else:
                    step = nc.scalar.activation(zs[:, e - 2, b, o:o + CH], ps[:, i % 8, :], ACT.Silu)
                step.then_inc(xz_used, 1)
            for dc in range(DC):
                act.wait_ge(conved, dc + 1)
                nc.scalar.activation(xc[:, dc], conv[:, dc], ACT.Silu).then_inc(silued, 1)
            link(nc.scalar.activation(A[:], a_log[:], ACT.Exp))
            act.wait_ge(conved, DC)
            for dc in range(DC):
                for c in range(4):
                    b, o = c // 2, CH * (c % 2)
                    act.wait_ge(dt_ps, c + 1)
                    nc.scalar.activation(ex[:, dc, b, o:o + CH], ps[:, 4 + c, :], ACT.Abs, bias=b_dt[:, dc:dc + 1], scale=w_dt[:, dc:dc + 1])
                    step = nc.scalar.activation(delta[:, dc, b, o:o + CH], ps[:, 4 + c, :], ACT.Relu, bias=b_dt[:, dc:dc + 1],
                                                scale=w_dt[:, dc:dc + 1])
                    if dc == DC - 1:
                        step.then_inc(dt_used, 1)
            act.wait_ge(dt_used, 4)
            for dc in range(DC):
                nc.scalar.activation(u[:, dc], ex[:, dc, :, 0:L], ACT.Exp, scale=-1.0).then_inc(soft, 1)
            for i in range(3):
                if i == 0:
                    act.wait_ge(split, 1)
                nc.scalar.activation(stack[32 * i:32 * i + 32, :], bc[:, i, :], ACT.Copy).then_inc(stacked, 1)
            for dc in range(DC):
                act.wait_ge(softed, dc + 1)
                nc.scalar.activation(ex[:, dc, :, 0:L], ex[:, dc, :, 0:L], ACT.Ln).then_inc(soft, 1)
            act.wait_ge(du_done, DC)
            for v in range(B * NS):
                b, n = divmod(v, NS)
                for dc in range(DC):
                    k = DC * v + dc
                    if k >= 2:
                        act.wait_ge(scanned, k - 1)
                    nc.scalar.activation(dA[:, dc], delta[:, dc, b], ACT.Exp, scale=A[:, dc, n:n + 1]).then_inc(dA_ready, 1)
                act.wait_ge(c_ready, v + 1)
                if v >= 2:
                    act.wait_ge(hc_done, DC * (v - 1))
                nc.scalar.activation(c_sb[:, v % 2], ps[:, 6:8, :].rearrange("p a c -> p (a c)"), ACT.Copy).then_inc(c_copied, 1)
            for g in range(4):
                act.wait_ge(out_ps, g + 1)
                nc.scalar.activation(Y[:, 4 * g:4 * g + 4, :].rearrange("p a c -> p (a c)"), ps[:, g, :], ACT.Copy)

        @block.vector
        def _(dve):
            link = Chain(dve, shared.sems[-1], shared.chained)
            nc.vector.memset(pad[:, :, :, 0:TAPS - 1], 0.0)
            dve.wait_ge(loaded, LOADED)
            nc.vector.tensor_copy(dt_col[:], w_x[:, :, 2 * NS:2 * NS + 1].to_broadcast([P, DC, P])).then_inc(ready0, 1)
            dve.wait_ge(ready0, 1)
            dve.wait_ge(xz_used, 8)
            for k in range(TAPS):
                for dc in range(DC):
                    src = pad[:, dc, :, k:k + L]
                    if k == 0:
                        step = nc.vector.tensor_scalar(conv[:, dc], src, conv_w[:, dc, 0:1], conv_b[:, dc:dc + 1], ALU.mult, ALU.add)
                    else:
                        step = nc.vector.scalar_tensor_tensor(conv[:, dc], src, conv_w[:, dc, k:k + 1], conv[:, dc], ALU.mult, ALU.add)
                    if k == TAPS - 1:
                        step.then_inc(conved, 1)
                if k < TAPS - 1:
                    link(step)
            dve.wait_ge(bc_ps, 4)
            src = ps[0:32, 0:4, :].rearrange("p a c -> p (a c)")
            link(nc.vector.tensor_copy(bc[:, 0, :], src))
            link(nc.vector.tensor_tensor(rest[:, 0, :], src, bc[:, 0, :], ALU.subtract))
            link(nc.vector.tensor_copy(bc[:, 1, :], rest[:, 0, :]))
            link(nc.vector.tensor_tensor(rest[:, 1, :], rest[:, 0, :], bc[:, 1, :], ALU.subtract))
            nc.vector.tensor_copy(bc[:, 2, :], rest[:, 1, :]).then_inc(split, 1)
            for dc in range(DC):
                dve.wait_ge(soft, dc + 1)
                link(nc.vector.tensor_scalar(ex[:, dc, :, 0:L], u[:, dc], 1.0, None, ALU.add))
                link(nc.vector.scalar_tensor_tensor(delta[:, dc], u[:, dc], 1.0, delta[:, dc], ALU.mult, ALU.add))
                nc.vector.tensor_scalar(u[:, dc], ex[:, dc, :, 0:L], 1.0, None, ALU.subtract).then_inc(softed, 1)
            dve.wait_ge(softed, DC)
            link(nc.vector.tensor_scalar(A[:], A[:], -1.0, None, ALU.mult))
            for dc in range(DC):
                dve.wait_ge(soft, DC + dc + 1)
                link(nc.vector.tensor_tensor(delta[:, dc], delta[:, dc], u[:, dc], ALU.subtract))
                link(nc.vector.tensor_tensor(delta[:, dc], delta[:, dc], ex[:, dc, :, 0:L], ALU.add))
                nc.vector.tensor_tensor(du[:, dc], delta[:, dc], xc[:, dc], ALU.mult).then_inc(du_done, 1)
            dve.wait_ge(du_done, DC)

            def times_b(k):
                b, n, dc = units[k]
                if dc == 0:
                    dve.wait_ge(b_ready, k // DC + 1)
                if k >= 2:
                    dve.wait_ge(scanned, k - 1)
                nc.vector.tensor_tensor(dbx[:, dc], du[:, dc, b], ps[:, 4:6, :].rearrange("p a c -> p (a c)"), ALU.mult)\
                    .then_inc(dbx_done, 1)

            def finish(b):
                for dc in range(DC):
                    dve.wait_ge(y_acc, DC * (NS * (b + 1) - 1) + dc + 1)
                    link(nc.vector.scalar_tensor_tensor(yT[:, dc, b], xc[:, dc, b], d_par[:, dc:dc + 1],
                                                        ps[:, 2 * dc:2 * dc + 2, :].rearrange("p a c -> p (a c)"), ALU.mult, ALU.add))
                    nc.vector.tensor_tensor(yT[:, dc, b], yT[:, dc, b], zs[:, dc, b], ALU.mult).then_inc(y_used, 1)

            times_b(0)
            for k, (b, n, dc) in enumerate(units):
                if k + 1 < len(units):
                    times_b(k + 1)
                dve.wait_ge(dA_ready, k + 1)
                dve.wait_ge(dbx_done, k + 1)
                if k >= DEEP:
                    dve.wait_ge(hc_done, k - DEEP + 1)
                nc.vector.tensor_tensor_scan(h[:, k % DEEP], dA[:, dc], dbx[:, dc], 0.0, ALU.mult, ALU.add).then_inc(scanned, 1)
                if k == DC * (NS + 1) - 1:
                    finish(0)
            finish(B - 1)
            shared.chained = link.count

        @block.gpsimd
        def _(pool):
            for k, (b, n, dc) in enumerate(units):
                pool.wait_ge(scanned, k + 1)
                if dc == 0:
                    pool.wait_ge(c_copied, k // DC + 1)
                if k >= DEEP:
                    pool.wait_ge(y_acc, k - DEEP + 1)
                nc.gpsimd.tensor_tensor(hc[:, k % DEEP], h[:, k % DEEP], c_sb[:, (k // DC) % 2], ALU.mult).then_inc(hc_done, 1)

DEPTH = 6
H2, D2 = 16, 64
INNER = H2 * D2
HP = H2 // 2
WIN = 32
NW = P // WIN
FF = 341
FC = 3
FROWS = [128, 128, FF - 256]
QK_SCALE = 8.0
TABLES = "natural_log_exp_and_others"
SPLIT = NB
FFN_START = NB + 2


class LocalWeights:

    def __init__(self, nc, ctx, sems, dram):
        self.dram = dram
        self.base, self.mask = (ctx.enter_context(nc.sbuf_tensor(f"l_{n}", shape, FP32)) for n, shape in
                                (("base", [P, 4, NB, D2]), ("mask", [P, 2, 1, 2 * WIN])))
        self.consts_in = sems.enter_context(nc.semaphore("l_consts_in"))
        shapes = [("scales", [P, 4, 1, D2]), ("wqk", [P, 2 * INNER]), ("wvl", [P, 2, HP * D2]), ("wo", [P, HP, P]), ("w1l", [P, 2 * FF]),
                  ("w2l", [P, FC, P]), ("vec", [P, 9])]
        self.layer = {n: (ctx.enter_context(nc.sbuf_tensor(f"l_{n}", shape, FP32)), sems.enter_context(nc.semaphore(f"l_{n}_in"))) for n, shape in shapes}
        self.loads = [(self.base[:], dram["base"], self.consts_in), (self.mask[:], dram["mask"], self.consts_in)]
        self.loads += [self.load(n, 0) for n in self.layer]

    def load(self, name, i):
        dst, done = self.layer[name]
        src = self.dram[name][bass.ds(i, 1)]
        src = src.rearrange("a p n -> p (a n)") if len(src.shape) == 3 else \
            src.rearrange("a p k n -> p (a k) n") if len(src.shape) == 4 else src.rearrange("a p k o d -> p (a k) o d")
        return dst[:], src, done


def local_stage(nc, sems, XT, Y, ident, weights):
    with ExitStack() as ctx:
        def sb(name, shape, dt=FP32):
            return ctx.enter_context(nc.sbuf_tensor(f"l_{name}", shape, dt))

        def sem(name):
            return sems.enter_context(nc.semaphore(f"l_{name}"))

        x = XT
        (scales, scales_in), (wqk, wqk_in), (wv, wv_in), (wo, wo_in), (w1, w1_in), (w2, w2_in), (vec, vec_in) = weights.layer.values()
        base, mask, consts_in = weights.base, weights.mask, weights.consts_in
        table = sb("table", [P, 4, NB, D2])
        centre, mean_w, eps, ln256 = sb("centre", [P, P]), sb("mean_w", [P, P]), sb("eps", [P, 1]), sb("ln256", [P, 1])
        xs = sb("xs", [P, B, WIN + L])
        raw, sq, tc, ts, qk = (sb(n, [P, 2, H2, D2]) for n in ("raw", "sq", "tc", "ts", "qk"))
        ssq, lnq, rn = sb("ssq", [P, 2, H2, 1]), sb("lnq", [P, 2 * H2]), sb("rn", [P, 2, H2, 1])
        qT, kT, vw = sb("qT", [P, HP, P]), sb("kT", [P, 2, HP, WIN + P]), sb("vw", [P, 2, NW, HP * D2])
        vt = sb("vt", [P, 2, 2, HP * D2])
        E, PT = sb("E", [P, H2, 2 * WIN]), sb("PT", [P, HP, P])
        mx, rs = sb("mx", [P, H2, 1]), sb("rs", [P, H2, 1])
        O, OT = sb("O", [P, H2, D2]), sb("OT", [P, HP, P])
        cen, csq, rstd, xn = (sb(n, [P, 2, CH]) for n in ("cen", "csq", "rstd", "xn"))
        gl, hb = sb("gl", [P, 2, CH]), sb("hb", [P, 2, FC, CH])
        ps = ctx.enter_context(nc.psum_tensor("l_ps", [P, 8, CH], FP32))

        PIECES = {(0, "X"): ("centre", 0), (1, "X"): ("var", 0), (2, "X"): ("inner", 0), (2, "Y"): ("inner", 1), (3, "X"): ("inner", 2),
                  (3, "Y"): ("inner", 3), (4, "X"): ("inner", 4), (4, "Y"): ("inner", 5), (5, "X"): ("outer", 0)}

        def piece(n, place):
            m, k = divmod(n - FFN_START, NB)
            return (m,) + PIECES[k, place] if n >= FFN_START and (k, place) in PIECES else (None, None, None)

        def layers(engine, steps, end=None):
            steps(0, range(SPLIT), None)
            with engine.Fori(0, DEPTH - 1) as i:
                steps(i, range(SPLIT, SPLIT + NT), None)
            steps(DEPTH - 1, range(SPLIT, SPLIT + NT), NT)

        def slot(i):
            return ps[:, 2 * i:2 * i + 2, :].rearrange("p a c -> p (a c)")

        table_ready = sem("table_ready")
        consts_set, k_zero, xa_ready, xf_ready = sem("consts_set"), sem("k_zero"), sem("xa_ready"), sem("xf_ready")
        q_ps, k_ps, v_ps, pt_ps, o_ps, qt_ps, kt_ps, ot_ps, wo_ps, s_ps = (
            sem(n) for n in ("q_ps", "k_ps", "v_ps", "pt_ps", "o_ps", "qt_ps", "kt_ps", "ot_ps", "wo_ps", "s_ps"))
        q_raw, k_raw, sq_done, v_done, pt_done, rn_half, rn_done, qt_done, kt_done, ot_done, exp_done = (
            sem(n) for n in ("q_raw", "k_raw", "sq_done", "v_done", "pt_done", "rn_half", "rn_done", "qt_done", "kt_done", "ot_done",
                             "exp_done"))
        masked, sub_done, rotq, rotk, ssq_done, qn_done, kn_done, o_done, wo_used, addq, addk = (
            sem(n) for n in ("masked", "sub_done", "rotq", "rotk", "ssq_done", "qn_done", "kn_done", "o_done", "wo_used", "addq", "addk"))
        m_ps, cen_done, csq_done, var_ps, lv_done, rstd_done, xn_done, y_ps, y_used = (
            sem(n) for n in ("m_ps", "cen_done", "csq_done", "var_ps", "lv_done", "rstd_done", "xn_done", "y_ps", "y_used"))
        vw_in = sem("vw_in")
        V_MOVES = 2 * (NW + 1)
        mx_done, sum_done, rs_done, ssq_sum, mul_done = (sem(n) for n in ("mx_done", "sum_done", "rs_done", "ssq_sum", "mul_done"))
        ag_ps, gl_done, h_done = sem("ag_ps"), sem("gl_done"), sem("h_done")
        out_ps, passed = sem("out_ps"), sem("passed")
        block = ctx.enter_context(nc.Block())

        @block.sync
        def _(sp):
            def load(name, i):
                dst, src, done = weights.load(name, i)
                sp.dma_start(dst, src).then_inc(done, 16)

            def settled(done, value):
                sp.wait_ge(done, value)
                sp.sem_inc(passed, 1)

            def steps(i, span, end):
                for n in span:
                    more = end is None and n >= SPLIT
                    if more and n == SPLIT:
                        settled(table_ready, i + 2)
                        load("scales", i + 1)
                    if more and n == NT - 1:
                        settled(k_ps, i * 16 + 16)
                        load("wqk", i + 1)
                    if end is None or n < end:
                        if n >= 1:
                            settled(vw_in, (i * 16 + n) * V_MOVES * 16)
                        if n >= 2:
                            settled(o_ps, i * 16 + (n - 1))
                        if n == 0:
                            sp.wait_ge(consts_set, 4)
                        settled(v_done, i * 16 + (n + 1))
                        for par in range(2):
                            rows = 64 * par
                            sp.dma_start(vw[rows:rows + WIN, n % 2, 0, :], vt[P - WIN:P, (n + 1) % 2, par, :]).then_inc(vw_in, 16)
                            sp.dma_start(vw[rows + WIN:rows + 2 * WIN, n % 2, 0, :], vt[0:WIN, n % 2, par, :]).then_inc(vw_in, 16)
                            for w in range(1, NW):
                                sp.dma_start(vw[rows:rows + 2 * WIN, n % 2, w, :], vt[WIN * w - WIN:WIN * w + WIN, n % 2, par, :]).then_inc(vw_in, 16)
                    if more and n == NT - 1:
                        load("wvl", i + 1)
                    if more and n == NT + 1:
                        settled(wo_ps, i * 16 + 16)
                        load("wo", i + 1)
                    if more and n == SPLIT + NT - 1:
                        settled(y_used, i * 4 + 4)
                        load("w1l", i + 1)
                        load("w2l", i + 1)
                        load("vec", i + 1)

            layers(sp, steps)

        @block.gpsimd
        def _(pool):
            nc.gpsimd.memset(xs[:], 0.0).then_inc(consts_set, 1)
            nc.gpsimd.memset(vt[:, 1], 0.0).then_inc(consts_set, 1)
            nc.gpsimd.memset(kT[:, 0, :, 0:WIN], 0.0).then_inc(k_zero, 1)
            nc.gpsimd.memset(mean_w[:], 1.0 / P).then_inc(consts_set, 1)
            nc.gpsimd.memset(eps[:], EPS).then_inc(consts_set, 1)
            nc.gpsimd.memset(ln256[:], float(np.log(256.0))).then_inc(table_ready, 1)
            pool.wait_ge(consts_in, 32)

            def tables(turn):
                pool.wait_ge(scales_in, turn * 16)
                for k in range(4):
                    step = nc.gpsimd.tensor_tensor(table[:, k], base[:, k], scales[:, k].to_broadcast([P, NB, D2]), ALU.mult)
                step.then_inc(table_ready, 1)

            tables(1)

            def steps(i, span, end):
                for n in span:
                    if end is not None and n >= end:
                        continue
                    for half, rot, turned, add in ((0, rotq, qt_ps, addq), (1, rotk, kt_ps, addk)):
                        if n >= 1:
                            pool.wait_ge(turned, i * 16 + n)
                        pool.wait_ge(rot, i * 16 + (n + 1))
                        nc.gpsimd.tensor_tensor(qk[:, half], tc[:, half], ts[:, half], ALU.add).then_inc(add, 1)
                    if n % NB == 0 and n:
                        pool.wait_ge(s_ps, i * 16 + (n - 1))
                        pool.sem_inc(passed, 1)
                        nc.gpsimd.memset(kT[:, 0, :, 0:WIN], 0.0).then_inc(k_zero, 1)
                    if n == NT - 1 and end is None:
                        tables(i + 2)

            layers(pool, steps)

        @block.tensor
        def _(pe):
            pe.wait_ge(consts_set, 5)

            def steps(i, span, end):
                def at(n):
                    return i * 16 + (n + 1)

                def mlp(n, place, used, value):
                    m, what, j = piece(n, place)
                    if what is None:
                        return
                    b = m % B
                    pe.wait_ge(used, value)
                    if what == "centre":
                        pe.wait_ge(xf_ready, i * 2 + (m + 1))
                        for c in range(2):
                            step = nc.tensor.matmul(ps[:, 6 + c, :], centre[:], xs[:, b, WIN + CH * c:WIN + CH * c + CH], start=True, stop=True)
                        step.then_inc(m_ps, 1)
                    if what == "var":
                        pe.wait_ge(csq_done, i * 2 + (m + 1))
                        for c in range(2):
                            step = nc.tensor.matmul(ps[:, 6 + c, :], mean_w[:], csq[:, c, :], start=True, stop=True)
                        step.then_inc(var_ps, 1)
                    if what == "inner":
                        c, k = divmod(j, FC)
                        if j == 0:
                            pe.wait_ge(xn_done, i * 2 + (m + 1))
                            if b == 0:
                                pe.wait_ge(w1_in, i * 16 + 16 * (m // B + 1))
                                pe.wait_ge(w2_in, i * 16 + 16 * (m // B + 1))
                        for part in range(2):
                            step = nc.tensor.matmul(ps[0:FROWS[k], 6 + part, :], w1[:, FF * part + P * k:FF * part + P * k + FROWS[k]],
                                                    xn[:, c, :], start=True, stop=True)
                        step.then_inc(ag_ps, 1)
                    if what == "outer":
                        pe.wait_ge(h_done, i * 12 + 6 * (m + 1))
                        for c in range(2):
                            for k in range(FC):
                                step = nc.tensor.matmul(ps[:, 6 + c, :], w2[0:FROWS[k], k, :], hb[0:FROWS[k], c, k, :], start=k == 0, stop=k == FC - 1)
                        step.then_inc(y_ps, 1)

                def used_by(n, place):
                    m, what, j = piece(n, place)
                    if what == "inner":
                        return h_done, i * 12 + (6 * m + j + 1)
                    return {"centre": cen_done, "var": lv_done, "outer": y_used}[what], \
                        i * 4 + 2 * (m + 1) if what == "outer" else i * 2 + (m + 1)

                for n in span:
                    a, b1, c2 = (0 <= k and (end is None or k < end) for k in (n, n - 1, n - 2))
                    b, t = (n // NB) % B, n % NB
                    cols = slice(WIN + P * t, WIN + P * t + P)
                    if a:
                        if t == 0:
                            pe.wait_ge(xa_ready, i * 2 + (n // NB + 1))
                        if n % NT == 0:
                            pe.wait_ge(wqk_in, i * 16 + 16 * (n // NT + 1))
                        for half, done in ((0, q_ps), (1, k_ps)):
                            if half == 0 and n >= 3:
                                pe.wait_ge(o_done, at(n - 3))
                            elif half == 0 and n >= 1:
                                pe.wait_ge(q_raw, at(n - 1))
                            if half == 1 and n >= 2:
                                pe.wait_ge(masked, at(n - 2))
                            if half == 1 and n == 1:
                                pe.wait_ge(k_raw, at(0))
                            for c in range(2):
                                step = nc.tensor.matmul(ps[:, 2 * half + c, :], xs[:, b, cols], wqk[:, INNER * half + CH * c:INNER * half + CH * c + CH],
                                                        start=True, stop=True)
                            step.then_inc(done, 1)
                    if c2:
                        if n >= 3:
                            pe.wait_ge(wo_used, at(n - 3))
                        else:
                            pe.wait_ge(v_done, at(n - 1))
                        pe.wait_ge(exp_done, at(n - 2))
                        for hp in range(HP):
                            step = nc.tensor.transpose(ps[:, 4 + hp // 4, P * (hp % 4):P * (hp % 4) + P], E[:, 2 * hp:2 * hp + 2, :], ident[:])
                        step.then_inc(pt_ps, 1)
                    if b1:
                        if piece(n - 1, "Y")[1]:
                            pe.wait_ge(*used_by(n - 1, "Y"))
                        elif n >= 3:
                            pe.wait_ge(ot_done, at(n - 3))
                        if a:
                            used = (None, k_raw, at(n))
                        else:
                            used = (None, masked, at(n - 2))
                        for half, ready, done in ((0, qn_done, qt_ps), (1, kn_done, kt_ps)):
                            if half:
                                pe.wait_ge(used[1], used[2])
                            pe.wait_ge(ready, at(n - 1))
                            for hp in range(HP):
                                step = nc.tensor.transpose(ps[:, (6, 2)[half] + hp // 4, P * (hp % 4):P * (hp % 4) + P],
                                                           qk[:, half, 2 * hp:2 * hp + 2, :], ident[:])
                            step.then_inc(done, 1)
                    if c2:
                        if a:
                            pe.wait_ge(q_raw, at(n))
                        else:
                            pe.wait_ge(o_done, at(n - 3))
                        pe.wait_ge(vw_in, at(n - 2) * V_MOVES * 16)
                        pe.wait_ge(pt_done, at(n - 2))
                        pe.sem_inc(passed, 1)
                        for h in range(H2):
                            hp, rows = h // 2, slice(64 * (h % 2), 64 * (h % 2) + 64)
                            for w in range(NW):
                                step = nc.tensor.matmul(ps[WIN * w:WIN * w + WIN, h % 2, D2 * hp:D2 * hp + D2],
                                                        PT[rows, hp, WIN * w:WIN * w + WIN], vw[rows, n % 2, w, D2 * hp:D2 * hp + D2],
                                                        start=True, stop=True)
                        step.then_inc(o_ps, 1)
                    if b1:
                        mlp(n, "X", qt_done, at(n - 1))
                    elif piece(n, "X")[1]:
                        k = n if not piece(n - 1, "Y")[1] and not piece(n - 1, "X")[1] else n - 1
                        place = "Y" if piece(n - 1, "Y")[1] else "X"
                        mlp(n, "X", *(used_by(n - 1, place) if k == n - 1 else (ot_done, at(NT - 1))))
                    if a:
                        if n >= 2:
                            pe.wait_ge(pt_done, at(n - 2))
                        elif n >= 1:
                            pe.wait_ge(v_done, at(n - 1))
                        if n % NT == 0:
                            pe.wait_ge(wv_in, i * 16 + 16 * (n // NT + 1))
                        for par in range(2):
                            step = nc.tensor.matmul(ps[:, 4 + par, :], xs[:, b, cols], wv[:, par, :], start=True, stop=True)
                        step.then_inc(v_ps, 1)
                    if c2:
                        if piece(n, "X")[1]:
                            pe.wait_ge(*used_by(n, "X"))
                        elif b1:
                            pe.wait_ge(qt_done, at(n - 1))
                        else:
                            pe.wait_ge(ot_done, at(n - 3))
                        pe.wait_ge(o_done, at(n - 2))
                        for hp in range(HP):
                            step = nc.tensor.transpose(ps[:, 6 + hp // 4, P * (hp % 4):P * (hp % 4) + P], O[:, 2 * hp:2 * hp + 2, :], ident[:])
                        step.then_inc(ot_ps, 1)
                    if b1:
                        pe.wait_ge(kt_done, at(n - 1))
                        if (n - 1) % NB == 0:
                            pe.wait_ge(k_zero, i * 2 + ((n - 1) // NB + 1))
                        pe.sem_inc(passed, 1)
                        for h in range(H2):
                            hp, rows = h // 2, slice(64 * (h % 2), 64 * (h % 2) + 64)
                            for w in range(NW):
                                step = nc.tensor.matmul(ps[WIN * w:WIN * w + WIN, 2 + h % 2, D2 * hp:D2 * hp + D2],
                                                        qT[rows, hp, WIN * w:WIN * w + WIN], kT[rows, (n - 1) % 2, hp, WIN * w:WIN * w + 2 * WIN],
                                                        start=True, stop=True)
                        step.then_inc(s_ps, 1)
                    if c2:
                        if a:
                            pe.wait_ge(v_done, at(n))
                        if (n - 2) % NT == 0:
                            pe.wait_ge(wo_in, i * 16 + 16 * ((n - 2) // NT + 1))
                        pe.wait_ge(ot_done, at(n - 2))
                        for hp in range(HP):
                            step = nc.tensor.matmul(ps[:, 4, 0:P], wo[:, hp, :], OT[:, hp, :], start=hp == 0, stop=hp == HP - 1)
                        step.then_inc(wo_ps, 1)
                        mlp(n, "Y", ot_done, at(n - 2))
                    elif piece(n, "Y")[1]:
                        mlp(n, "Y", *used_by(n, "X"))

            layers(pe, steps)
            pe.wait_ge(y_used, 4 * DEPTH)
            for g in range(4):
                for t in range(4):
                    step = nc.tensor.transpose(ps[:, g, P * t:P * t + P], x[:, CH * g + P * t:CH * g + P * t + P], ident[:])
                step.then_inc(out_ps, 1)

        @block.scalar
        def _(act):
            act.wait_ge(consts_set, 4)
            act.wait_ge(table_ready, 1)
            act.preload_act_table_set(TABLES)

            def steps(i, span, end):
                def at(n):
                    return i * 16 + (n + 1)

                def gelu(m, j, back=True):
                    k = j % FC
                    if j == 0 and m % B == 0:
                        act.wait_ge(vec_in, i * 16 + 16 * (m // B + 1))
                    act.wait_ge(ag_ps, i * 12 + (6 * m + j + 1))
                    if j >= 2:
                        act.wait_ge(h_done, i * 12 + (6 * m + j - 1))
                    nc.scalar.activation(gl[0:FROWS[k], j % 2, :], ps[0:FROWS[k], 7, :], ACT.Gelu, bias=vec[0:FROWS[k], 5 + k:6 + k]).then_inc(gl_done, 1)
                    if back:
                        act.preload_act_table_set(TABLES)

                for n in span:
                    a, b1, c2 = (0 <= k and (end is None or k < end) for k in (n, n - 1, n - 2))
                    if c2:
                        act.wait_ge(sub_done, at(n - 2))
                        nc.scalar.activation(E[:], E[:], ACT.Exp).then_inc(exp_done, 1)
                    m, what, j = piece(n - 1, "Y")
                    if what == "inner":
                        gelu(m, j, False)
                    if a:
                        act.wait_ge(q_ps, at(n))
                        nc.scalar.activation(raw[:, 0].rearrange("p h d -> p (h d)"), slot(0), ACT.Copy).then_inc(q_raw, 1)
                    if a:
                        act.wait_ge(k_ps, at(n))
                        nc.scalar.activation(raw[:, 1].rearrange("p h d -> p (h d)"), slot(1), ACT.Copy).then_inc(k_raw, 1)
                    if c2:
                        act.wait_ge(pt_ps, at(n - 2))
                        nc.scalar.activation(PT[:].rearrange("p h c -> p (h c)"), slot(2), ACT.Copy).then_inc(pt_done, 1)
                    if b1:
                        act.wait_ge(qt_ps, at(n - 1))
                        nc.scalar.activation(qT[:].rearrange("p h c -> p (h c)"), slot(3), ACT.Copy).then_inc(qt_done, 1)
                        act.wait_ge(kt_ps, at(n - 1))
                        src = slot(1).rearrange("p (h c) -> p h c", h=HP)
                        if n % NB:
                            nc.scalar.activation(kT[:, n % 2, :, 0:WIN], src[:, :, P - WIN:P], ACT.Copy)
                        nc.scalar.activation(kT[:, (n - 1) % 2, :, WIN:WIN + P], src, ACT.Copy).then_inc(kt_done, 1)
                    if a:
                        act.wait_ge(k_raw, at(n))
                        nc.scalar.activation(sq[:], raw[:], ACT.Square).then_inc(sq_done, 1)
                    m, what, j = piece(n, "X")
                    if piece(n - 1, "Y")[1] == "inner" and what != "inner":
                        act.preload_act_table_set(TABLES)
                    if what == "inner":
                        gelu(m, j)
                    if what == "centre":
                        act.wait_ge(m_ps, i * 2 + (m + 1))
                        nc.scalar.activation(cen[:].rearrange("p a c -> p (a c)"), slot(3), ACT.Copy).then_inc(cen_done, 1)
                    if what == "var":
                        act.wait_ge(var_ps, i * 2 + (m + 1))
                        nc.scalar.activation(rstd[:].rearrange("p a c -> p (a c)"), slot(3), ACT.Ln, bias=eps[:, 0:1]).then_inc(lv_done, 1)
                        act.wait_ge(lv_done, i * 2 + (m + 1))
                        nc.scalar.activation(rstd[:], rstd[:], ACT.Exp, scale=-0.5).then_inc(rstd_done, 1)
                    if a:
                        act.wait_ge(v_ps, at(n))
                        if n >= 1:
                            act.wait_ge(vw_in, at(n - 1) * V_MOVES * 16)
                        nc.scalar.activation(vt[:, n % 2].rearrange("p a c -> p (a c)"), slot(2), ACT.Copy).then_inc(v_done, 1)
                    if c2:
                        act.wait_ge(ot_ps, at(n - 2))
                        nc.scalar.activation(OT[:].rearrange("p h c -> p (h c)"), slot(3), ACT.Copy).then_inc(ot_done, 1)
                    if a:
                        act.wait_ge(ssq_done, at(n))
                        nc.scalar.activation(lnq[:], ssq[:].rearrange("p a h o -> p (a h o)"), ACT.Ln, scale=65536.0).then_inc(rn_half, 1)
                        act.wait_ge(rn_half, at(n))
                        nc.scalar.activation(rn[:].rearrange("p a h o -> p (a h o)"), lnq[:], ACT.Exp, bias=ln256[:, 0:1], scale=-0.5).then_inc(rn_done, 1)
                    if what == "centre":
                        act.wait_ge(cen_done, i * 2 + (m + 1))
                        nc.scalar.activation(csq[:], cen[:], ACT.Square).then_inc(csq_done, 1)

            layers(act, steps)
            for g in range(4):
                act.wait_ge(out_ps, g + 1)
                nc.scalar.activation(Y[:, 4 * g:4 * g + 4, :].rearrange("p a c -> p (a c)"), ps[:, g, :], ACT.Copy)

        @block.vector
        def _(dve):
            dve.wait_ge(consts_set, 4)
            dve.wait_ge(consts_in, 32)

            def shift(b, ready):
                nc.vector.tensor_copy(xs[0:64, b, WIN:WIN + L], x[0:64, L * b:L * b + L])
                nc.vector.tensor_copy(xs[64:P, b, WIN + 1:WIN + L], x[64:P, L * b:L * b + L - 1]).then_inc(ready, 1)

            nc.vector.tensor_scalar(centre[:], ident[:], 1.0 / P, None, ALU.subtract).then_inc(consts_set, 1)
            for b in range(B):
                shift(b, xa_ready)

            def steps(i, span, end):
                def at(n):
                    return i * 16 + (n + 1)

                def hidden(m, j):
                    c, k = divmod(j, FC)
                    dve.wait_ge(gl_done, i * 12 + (6 * m + j + 1))
                    nc.vector.scalar_tensor_tensor(hb[0:FROWS[k], c, k, :], ps[0:FROWS[k], 6, :], vec[0:FROWS[k], 2 + k:3 + k],
                                                   gl[0:FROWS[k], j % 2, :], ALU.add, ALU.mult).then_inc(h_done, 1)

                def rotate_cos(n, half, src):
                    dve.wait_ge(src, at(n))
                    nc.vector.tensor_tensor(tc[:, half], raw[:, half], table[:, 2 * half, n % NB:n % NB + 1, :].to_broadcast([P, H2, D2]), ALU.mult)

                def rotate_sin(n, half, done):
                    hd = D2 // 2
                    tab = table[:, 2 * half + 1, n % NB:n % NB + 1, :]
                    nc.vector.tensor_tensor(ts[:, half, :, 0:hd], raw[:, half, :, hd:D2], tab[:, :, 0:hd].to_broadcast([P, H2, hd]), ALU.mult)
                    nc.vector.tensor_tensor(ts[:, half, :, hd:D2], raw[:, half, :, 0:hd], tab[:, :, hd:D2].to_broadcast([P, H2, hd]), ALU.mult)\
                        .then_inc(done, 1)

                for n in span:
                    a, b1, c2, c3 = (0 <= k and (end is None or k < end) for k in (n, n - 1, n - 2, n - 3))
                    t = n % NB
                    if c2:
                        dve.wait_ge(s_ps, at(n - 2))
                        for par in range(2):
                            step = nc.vector.scalar_tensor_tensor(E[:, par::2, :], ps[:, 2 + par, :].rearrange("p (h k) -> p h k", h=HP), QK_SCALE,
                                                                  mask[:, 0 if (n - 2) % NB == 0 else 1].to_broadcast([P, HP, 2 * WIN]),
                                                                  ALU.mult, ALU.add)
                        step.then_inc(masked, 1)
                        dve.wait_ge(masked, at(n - 2))
                        nc.vector.tensor_reduce(mx[:, :, 0], E[:], AX.X, ALU.max).then_inc(mx_done, 1)
                        dve.wait_ge(mx_done, at(n - 2))
                        nc.vector.tensor_tensor(E[:], E[:], mx[:].to_broadcast([P, H2, 2 * WIN]), ALU.subtract).then_inc(sub_done, 1)
                    if c3:
                        dve.wait_ge(wo_ps, at(n - 3))
                        c = L * (((n - 3) // NB) % B) + P * ((n - 3) % NB)
                        nc.vector.tensor_tensor(x[:, c:c + P], x[:, c:c + P], ps[:, 4, 0:P], ALU.add).then_inc(wo_used, 1)
                    if b1:
                        dve.wait_ge(rn_done, at(n - 1))
                        for half, add, done in ((0, addq, qn_done), (1, addk, kn_done)):
                            dve.wait_ge(add, at(n - 1))
                            nc.vector.tensor_tensor(qk[:, half], qk[:, half], rn[:, half].to_broadcast([P, H2, D2]), ALU.mult).then_inc(done, 1)
                    if c3 and (n - 3) % NB == NB - 1:
                        dve.wait_ge(wo_used, at(n - 3))
                        shift(((n - 3) // NB) % B, xf_ready)
                    m, what, j = piece(n - 1, "Y")
                    if what == "inner":
                        hidden(m, j)
                    if a:
                        if n % NT == 0:
                            dve.wait_ge(table_ready, i + (n // NT + 2))
                        rotate_cos(n, 0, q_raw)
                        rotate_sin(n, 0, rotq)
                    if c2:
                        dve.wait_ge(exp_done, at(n - 2))
                        nc.vector.tensor_reduce(rs[:, :, 0], E[:], AX.X, ALU.add).then_inc(sum_done, 1)
                        dve.wait_ge(sum_done, at(n - 2))
                        nc.vector.reciprocal(rs[:], rs[:]).then_inc(rs_done, 1)
                    if c2:
                        dve.wait_ge(rs_done, at(n - 2))
                        dve.wait_ge(o_ps, at(n - 2))
                        nc.vector.tensor_tensor(O[:].rearrange("p (h a) d -> p a h d", a=2), slot(0).rearrange("p (a h d) -> p a h d", a=2, h=HP),
                                                rs[:].rearrange("p (h a) o -> p a h o", a=2).to_broadcast([P, 2, HP, D2]), ALU.mult)\
                            .then_inc(o_done, 1)
                    if a:
                        rotate_cos(n, 1, k_raw)
                    m, what, j = piece(n, "X")
                    if what == "inner":
                        hidden(m, j)
                    if a:
                        rotate_sin(n, 1, rotk)
                    m, what, j = piece(n, "X")
                    if a:
                        dve.wait_ge(sq_done, at(n))
                        nc.vector.tensor_reduce(ssq[:, :, :, 0], sq[:], AX.X, ALU.add).then_inc(ssq_sum, 1)
                        dve.wait_ge(ssq_sum, at(n))
                        nc.vector.tensor_scalar(ssq[:], ssq[:], 1e-24, None, ALU.max).then_inc(ssq_done, 1)
                    if what == "outer":
                        b = m % B
                        dve.wait_ge(y_ps, i * 2 + (m + 1))
                        nc.vector.scalar_tensor_tensor(x[:, L * b:L * b + L], slot(3), vec[:, 8:9], x[:, L * b:L * b + L], ALU.add, ALU.add)\
                            .then_inc(y_used, 2)
                        dve.wait_ge(y_used, i * 4 + 2 * (m + 1))
                        if end is None:
                            shift(b, xa_ready)
                    if what == "var":
                        if m % B == 0:
                            dve.wait_ge(vec_in, i * 16 + 16 * (m // B + 1))
                        dve.wait_ge(rstd_done, i * 2 + (m + 1))
                        nc.vector.tensor_tensor(xn[:], cen[:], rstd[:], ALU.mult).then_inc(mul_done, 1)
                        dve.wait_ge(mul_done, i * 2 + (m + 1))
                        nc.vector.tensor_scalar(xn[:], xn[:], vec[:, 0:1], vec[:, 1:2], ALU.mult, ALU.add).then_inc(xn_done, 1)

            layers(dve, steps)


H3 = 16
D3 = P // H3
LM = 128
SEG = L // LM
NU = B * H3
NG = NU // 4
ITERS = 6
E1 = D3 + 1
WIDE = 32


class NystromWeights:

    def __init__(self, nc, ctx, sems, dram):
        shapes = [("wq", [P, P]), ("wk", [P, P]), ("wv", [P, P]), ("bq", [P, 1]), ("bk", [P, 1]), ("bv", [P, P]),
                  ("head_mask", [P, H3, 1]),
                  ("eyes", [P, 3, 1, P]),
                  ("fold", [P, E1])]
        self.buffers = [ctx.enter_context(nc.sbuf_tensor(f"y_{n}", shape, FP32)) for n, shape in shapes]
        self.loaded = sems.enter_context(nc.semaphore("y_loaded"))
        self.loads = [(buf[:], dram[n], self.loaded) for buf, (n, _) in zip(self.buffers, shapes)]


def nystrom_stage(nc, sems, shared, XT, Y, ident, weights):
    with ExitStack() as ctx:
        def sb(name, shape, dt=FP32):
            return ctx.enter_context(nc.sbuf_tensor(f"y_{name}", shape, dt))

        def sem(name):
            return sems.enter_context(nc.semaphore(f"y_{name}"))

        wq, wk, wv, bq, bk, bv, head_mask, eyes, fold = weights.buffers
        ones = sb("ones", [P, P])
        QT, KT = sb("QT", [P, T]), sb("KT", [P, T])
        v9 = sb("v9", [P, NT * H3 * E1 + WIDE])
        V9 = v9[:, 0:NT * H3 * E1].rearrange("p (t h e) -> p t h e", t=NT, h=H3)
        q_lm, k_lm = sb("q_lm", [P, B * LM]), sb("k_lm", [P, B * LM])
        QM, KM = sb("QM", [P, B, H3, LM]), sb("KM", [P, B, H3, LM])
        K2T, V, W = sb("K2T", [P, NG, 4, LM]), sb("V", [P, NG, 4, LM]), sb("W", [P, NG, 4, LM])
        KV, A = sb("KV", [P, NG, 4, LM]), sb("A", [P, NG, 4, LM])
        P3, P3T = KV[:, 0:4].rearrange("p a h m -> p (a h m)"), KV[:, 4:8].rearrange("p a h m -> p (a h m)")
        E, ET = KV[:, 0:4].rearrange("p (u a) h m -> p u (a h) m", u=2), KV[:, 4:8].rearrange("p (u a) h m -> p u (a h) m", u=2)
        m2, s2 = sb("m2", [P, NG, 4, 1]), sb("s2", [P, NG, 4, 1])
        cmax, rc = sb("cmax", [P, NG]), sb("rc", [P, 2])
        m3 = sb("m3", [P, 2, 2])
        T3, r3 = sb("T3", [P, NU, D3]), sb("r3", [P, NU, 1])
        G, y9 = sb("G", [P, NU, D3]), sb("y9", [P, NU * E1 + WIDE])
        Y9 = y9[:, 0:NU * E1].rearrange("p (u e) -> p u e", e=E1)
        parts = A
        o1t = sb("o1t", [P, 2, 4, P])
        m1, r1 = sb("m1", [P, 2, 8, 1]), sb("r1", [P, 2, H3, 1])
        ps = ctx.enter_context(nc.psum_tensor("y_ps", [P, 8, CH], FP32))

        def bank(i, n=1):
            return ps[:, i:i + n, :].rearrange("p a c -> p (a c)")

        loaded, qkv, qkv_used, masked, k2_ps, k2_sub, k2_exp, k2_done, col_ps, col_max = (
            weights.loaded, sem("qkv"), sem("qkv_used"), sem("masked"), sem("k2_ps"), sem("k2_sub"), sem("k2_exp"), sem("k2_done"),
            sem("col_ps"), sem("col_max"))
        tr2, tr2_used, v0, s3, m3_ready, e3, tr3, tr3_a, tr3_d, t3 = (
            sem("tr2"), sem("tr2_used"), sem("v0"), sem("s3"), sem("m3_ready"), sem("e3"), sem("tr3"), sem("tr3_a"), sem("tr3_d"), sem("t3"))
        t3_done, kv_ps, kv_act, a_ready, p_ps, v_ps, w_ps, v_ready, w_ready = (
            sem("t3_done"), sem("kv_ps"), sem("kv_act"), sem("a_ready"), sem("p_ps"), sem("v_ps"), sem("w_ps"), sem("v_ready"), sem("w_ready"))
        g_ps, g_done, y_ps, y_done, s1, e1_sub, e1_exp, tr1, tr1_used, o1, o1_used = (
            sem("g_ps"), sem("g_done"), sem("y_ps"), sem("y_done"), sem("s1"), sem("e1_sub"), sem("e1_exp"), sem("tr1"), sem("tr1_used"),
            sem("o1"), sem("o1_used"))
        lm_ready, q_masked = sem("lm_ready"), sem("q_masked")
        parts_done, t3_ps, o1t_ps, o1t_done = sem("parts_done"), sem("t3_ps"), sem("o1t_ps"), sem("o1t_done")
        block = ctx.enter_context(nc.Block())
        LOADED = 16 * len(weights.loads)
        SC = float(np.float32(1.0 / np.sqrt(np.sqrt(D3))))
        QUARTER = 0.25

        def mask_heads(engine, dst, lm, b):
            return engine.tensor_tensor(dst[:, b], lm[:, LM * b:LM * b + LM].rearrange("p (o m) -> p o m", o=1).to_broadcast([P, H3, LM]),
                                        head_mask[:].to_broadcast([P, H3, LM]), ALU.mult)

        @block.gpsimd
        def _(pool):
            pool.wait_ge(loaded, LOADED)
            pool.wait_ge(lm_ready, 1)
            for b in range(B):
                mask_heads(nc.gpsimd, QM, q_lm, b).then_inc(q_masked, 1)

        @block.tensor
        def _(pe):
            pe.wait_ge(loaded, LOADED)
            for i in range(12):
                if i >= 8:
                    pe.wait_ge(qkv_used, i - 7)
                if i < 8:
                    c = i % 4
                    step = nc.tensor.matmul(bank(i), (wq if i < 4 else wk)[:], XT[:, CH * c:CH * c + CH], start=True, stop=True)
                else:
                    for t in range(4 * (i - 8), 4 * (i - 8) + 4):
                        step = nc.tensor.matmul(ps[:, i - 8, P * (t % 4):P * (t % 4) + P], XT[:, P * t:P * t + P], wv[:],
                                                start=True, stop=True)
                step.then_inc(qkv, 1)
            pe.wait_ge(masked, B)
            pe.wait_ge(qkv_used, 12)
            for g in range(NG):
                b, o = g // 4, 4 * (g % 4)
                nc.tensor.matmul(bank(g), q_lm[:, LM * b:LM * b + LM], KM[:, b, o:o + 4, :], start=True, stop=True).then_inc(k2_ps, 1)
            for g in range(NG):
                pe.wait_ge(k2_done, g + 1)
                nc.tensor.matmul(bank(g), ones[:], W[:, g], start=True, stop=True).then_inc(col_ps, 1)
            for g in range(NG):
                pe.wait_ge(col_max, g + 1)
                for i in range(4):
                    step = nc.tensor.transpose(ps[:, g, LM * i:LM * i + LM], W[:, g, i, :], ident[:])
                step.then_inc(tr2, 1)

            def scores3(u):
                b, h = divmod(u, H3)
                pe.wait_ge(tr2_used, NG) if u < 2 else pe.wait_ge(e3, u - 1)
                for i in range(2):
                    step = nc.tensor.matmul(bank(2 * (u % 2) + i), QM[:, b, h, :], KT[:, L * b + CH * i:L * b + CH * i + CH], start=True, stop=True)
                step.then_inc(s3, 1)

            def values3(u):
                b, h = divmod(u, H3)
                pe.wait_ge(tr3_a, u + 1)
                pe.wait_ge(tr3_d, u + 1)
                if u % 4 == 0 and u >= 8:
                    pe.wait_ge(parts_done, u // 4 - 1)
                for i in range(NB):
                    j, v = WIDE * (i % 4), E1 * (H3 * (NB * b + i) + h)
                    step = nc.tensor.matmul(ps[j:j + WIDE, 6 + (u // 4) % 2, LM * (u % 4):LM * (u % 4) + LM], v9[:, v:v + WIDE],
                                            P3T[:, L * (u % 2) + P * i:L * (u % 2) + P * i + P], start=i < 4, stop=i >= 4)
                step.then_inc(t3, 1)

            pe.wait_ge(q_masked, B)
            scores3(0)
            scores3(1)
            for u in range(NU):
                pe.wait_ge(e3, u + 1)
                if u:
                    pe.wait_ge(tr3_a, u)
                    pe.wait_ge(tr3_d, u)
                for i in range(NB):
                    step = nc.tensor.transpose(ps[:, 4 + i // 4, LM * (i % 4):LM * (i % 4) + LM], P3[:, L * (u % 2) + P * i:L * (u % 2) + P * i + P], ident[:])
                step.then_inc(tr3, 1)
                if u + 2 < NU:
                    scores3(u + 2)
                if u:
                    values3(u - 1)
            values3(NU - 1)
            pe.wait_ge(parts_done, NU // 4)
            for u in range(NU):
                step = nc.tensor.matmul(ps[:, 6, E1 * u:E1 * u + E1], parts[:, u // 4, u % 4, :], fold[:], start=True, stop=True)
            step.then_inc(t3_ps, 1)
            pe.wait_ge(t3_done, 1)
            pe.wait_ge(v0, NG)
            bnk = [0]

            def four(lhs, rhs, g, used, value, done):
                if used is not None:
                    pe.wait_ge(used, value)
                for i in range(4):
                    step = nc.tensor.matmul(ps[:, g, LM * i:LM * i + LM], lhs[:, g, i, :], rhs[:, g, i, :], start=True, stop=True)
                step.then_inc(done, 1)

            for it in range(ITERS):
                last = it == ITERS - 1
                for g in range(NG):
                    if it:
                        pe.wait_ge(v_ready, NG * (it - 1) + g + 1)
                    four(K2T, V, g, w_ready if it else None, NG * (it - 1) + g + 1, kv_ps)
                for k in range(2):
                    for g in range(NG):
                        pe.wait_ge(kv_act, NG * it + g + 1)
                        four(KV, A, g, a_ready, 3 * NG * it + NG * k + g + 1, p_ps)
                if not last:
                    for g in range(NG):
                        four(W, A, g, a_ready, 3 * NG * it + 2 * NG + g + 1, v_ps)
                    for g in range(NG):
                        pe.wait_ge(v_ready, NG * it + g + 1)
                        for i in range(4):
                            step = nc.tensor.transpose(ps[:, g, LM * i:LM * i + LM], V[:, g, i, :], ident[:])
                        step.then_inc(w_ps, 1)
            for g in range(NG):
                pe.wait_ge(a_ready, 3 * NG * (ITERS - 1) + 2 * NG + g + 1)
            for u in range(NU):
                step = nc.tensor.matmul(ps[:, 0, D3 * u:D3 * u + D3], A[:, u // 4, u % 4, :], T3[:, u, :], start=True, stop=True)
            step.then_inc(g_ps, 1)
            pe.wait_ge(g_done, 1)
            for u in range(NU):
                step = nc.tensor.matmul(ps[:, 1, D3 * u:D3 * u + D3], W[:, u // 4, u % 4, :], G[:, u, :], start=True, stop=True)
            step.then_inc(y_ps, 1)

            def scores1(u):
                t, half = divmod(u, 2)
                b = t // NB
                pe.wait_ge(y_done, 1) if u < 2 else pe.wait_ge(e1_sub, u - 1)
                for i in range(2):
                    step = nc.tensor.matmul(bank(2 * (u % 2) + i), QT[:, P * t:P * t + P], KM[:, b, 8 * half + 4 * i:8 * half + 4 * i + 4, :], start=True, stop=True)
                step.then_inc(s1, 1)

            def turn(u):
                pe.wait_ge(e1_exp, u + 1)
                if u:
                    pe.wait_ge(tr1_used, u)
                for i in range(8):
                    step = nc.tensor.transpose(ps[:, 4 + i // 4, LM * (i % 4):LM * (i % 4) + LM], E[:, u % 2, i, :], ident[:])
                step.then_inc(tr1, 1)

            def tokens_back(t):
                if t >= 1:
                    pe.wait_ge(o1_used, t)
                pe.wait_ge(o1t_done, t + 1)
                for k in range(4):
                    step = nc.tensor.transpose(ps[:, 7, P * k:P * k + P], o1t[:, t % 2, k, :], ident[:])
                step.then_inc(o1, 1)

            scores1(0)
            scores1(1)
            turn(0)
            for u in range(2 * NT):
                t, half = divmod(u, 2)
                b = t // NB
                if u + 2 < 2 * NT:
                    scores1(u + 2)
                if half == 0 and t >= 1:
                    tokens_back(t - 1)
                pe.wait_ge(tr1_used, u + 1)
                for i in range(8):
                    k, y = 2 * half + i // 4, E1 * (H3 * b + 8 * half + i)
                    step = nc.tensor.matmul(ps[WIDE * (i % 4):WIDE * (i % 4) + WIDE, 6, P * k:P * k + P], y9[:, y:y + WIDE], ET[:, u % 2, i, :],
                                            start=True, stop=True)
                if half:
                    step.then_inc(o1t_ps, 1)
                if u + 1 < 2 * NT:
                    turn(u + 1)
            tokens_back(NT - 1)

        @block.scalar
        def _(act):
            act.wait_ge(loaded, LOADED)
            for g in range(NG):
                act.wait_ge(k2_sub, g + 1)
                nc.scalar.activation(W[:, g], W[:, g], ACT.Exp).then_inc(k2_exp, 1)
            for g in range(NG):
                act.wait_ge(tr2, g + 1)
                nc.scalar.activation(K2T[:, g].rearrange("p h m -> p (h m)"), bank(g), ACT.Copy).then_inc(tr2_used, 1)

            def gather(q):
                act.wait_ge(t3, 4 * q + 4)
                nc.scalar.activation(parts[:, q].rearrange("p h m -> p (h m)"), bank(6 + q % 2), ACT.Copy).then_inc(parts_done, 1)

            for u in range(NU):
                act.wait_ge(m3_ready, u + 1)
                if u >= 2:
                    act.wait_ge(tr3, u - 1)
                nc.scalar.activation(P3[:, L * (u % 2):L * (u % 2) + L], bank(2 * (u % 2), 2), ACT.Exp, bias=m3[:, u % 2, 1:2]).then_inc(e3, 1)
                act.wait_ge(tr3, u + 1)
                if u >= 2:
                    act.wait_ge(t3, u - 1)
                nc.scalar.activation(P3T[:, L * (u % 2):L * (u % 2) + CH], bank(4), ACT.Copy).then_inc(tr3_a, 1)
                if u % 4 == 1 and u >= 4:
                    gather(u // 4 - 1)
            gather(NU // 4 - 1)
            for it in range(ITERS):
                for g in range(NG):
                    act.wait_ge(kv_ps, NG * it + g + 1)
                    if it == 0:
                        act.wait_ge(t3, NU)
                    nc.scalar.activation(KV[:, g].rearrange("p h m -> p (h m)"), bank(g), ACT.Copy).then_inc(kv_act, 1)
                if it == ITERS - 1:
                    break
                for g in range(NG):
                    act.wait_ge(v_ps, NG * it + g + 1)
                    nc.scalar.activation(V[:, g].rearrange("p h m -> p (h m)"), bank(g), ACT.Copy, scale=QUARTER).then_inc(v_ready, 1)
                for g in range(NG):
                    act.wait_ge(w_ps, NG * it + g + 1)
                    nc.scalar.activation(W[:, g].rearrange("p h m -> p (h m)"), bank(g), ACT.Copy).then_inc(w_ready, 1)
            act.wait_ge(g_ps, 1)
            nc.scalar.activation(G[:].rearrange("p u d -> p (u d)"), ps[:, 0, 0:NU * D3], ACT.Copy).then_inc(g_done, 1)

            def turned(t):
                act.wait_ge(o1t_ps, t + 1)
                if t >= 2:
                    act.wait_ge(o1, t - 1)
                nc.scalar.activation(o1t[:, t % 2].rearrange("p k c -> p (k c)"), bank(6), ACT.Copy).then_inc(o1t_done, 1)

            for u in range(2 * NT):
                act.wait_ge(e1_sub, u + 1)
                nc.scalar.activation(E[:, u % 2], E[:, u % 2], ACT.Exp).then_inc(e1_exp, 1)
                if u % 2 == 0 and u:
                    turned(u // 2 - 1)
                act.wait_ge(tr1, u + 1)
                if u >= 2:
                    act.wait_ge(o1t_ps, u // 2)
                nc.scalar.activation(ET[:, u % 2].rearrange("p h m -> p (h m)"), bank(4, 2), ACT.Copy).then_inc(tr1_used, 1)
            turned(NT - 1)

        @block.vector
        def _(dve):
            link = Chain(dve, shared.sems[-1], shared.chained)
            nc.vector.memset(ones[:], 1.0)
            nc.vector.memset(v9[:], 1.0)
            link(nc.vector.memset(y9[:], 1.0))
            dve.wait_ge(loaded, LOADED)
            for i in range(12):
                dve.wait_ge(qkv, i + 1)
                if i < 8:
                    dst, bias = (QT, bq) if i < 4 else (KT, bk)
                    c = i % 4
                    step = nc.vector.tensor_scalar(dst[:, CH * c:CH * c + CH], bank(i), bias[:, 0:1], SC, ALU.add, ALU.mult)
                else:
                    c = i - 8
                    for t in range(4):
                        step = nc.vector.tensor_tensor(V9[:, 4 * c + t, :, 0:D3], ps[:, c, P * t:P * t + P].rearrange("p (h d) -> p h d", h=H3),
                                                       bv[:].rearrange("p (h d) -> p h d", h=H3), ALU.add)
                step.then_inc(qkv_used, 1)
            dve.wait_ge(qkv_used, 12)
            for src, lm in ((QT, q_lm), (KT, k_lm)):
                link(nc.vector.tensor_reduce(lm[:], src[:].rearrange("p (m s) -> p m s", s=SEG), AX.X, ALU.add))
                nc.vector.tensor_scalar(lm[:], lm[:], 1.0 / SEG, None, ALU.mult).then_inc(lm_ready, 1)
            dve.wait_ge(lm_ready, 2)
            for b in range(B):
                mask_heads(nc.vector, KM, k_lm, b).then_inc(masked, 1)
            for g in range(NG):
                src = ps[:, g, :].rearrange("p (h m) -> p h m", h=4)
                dve.wait_ge(k2_ps, g + 1)
                link(nc.vector.tensor_reduce(m2[:, g, :, 0], src, AX.X, ALU.max))
                nc.vector.tensor_tensor(W[:, g], src, m2[:, g].to_broadcast([P, 4, LM]), ALU.subtract).then_inc(k2_sub, 1)
            for g in range(NG):
                dve.wait_ge(k2_exp, g + 1)
                link(nc.vector.tensor_reduce(s2[:, g, :, 0], W[:, g], AX.X, ALU.add))
                link(nc.vector.reciprocal(s2[:, g], s2[:, g]))
                nc.vector.tensor_tensor(W[:, g], W[:, g], s2[:, g].to_broadcast([P, 4, LM]), ALU.mult).then_inc(k2_done, 1)
            for g in range(NG):
                dve.wait_ge(col_ps, g + 1)
                nc.vector.tensor_reduce(cmax[:, g:g + 1], bank(g), AX.X, ALU.max).then_inc(col_max, 1)
            dve.wait_ge(col_max, NG)
            link(nc.vector.tensor_reduce(rc[:, 0:1], cmax[:], AX.X, ALU.max))
            link(nc.vector.reciprocal(rc[:, 1:2], rc[:, 0:1]))
            dve.wait_ge(tr2_used, NG)
            for g in range(NG):
                nc.vector.tensor_scalar(V[:, g], K2T[:, g], rc[:, 1:2], None, ALU.mult)
                nc.vector.tensor_scalar(W[:, g], W[:, g], rc[:, 1:2], None, ALU.mult).then_inc(v0, 1)
            dve.wait_ge(v0, NG)

            def maximum3(u):
                dve.wait_ge(s3, u + 1)
                if u >= 2:
                    dve.wait_ge(e3, u - 1)
                link(nc.vector.tensor_reduce(m3[:, u % 2, 0:1], bank(2 * (u % 2), 2), AX.X, ALU.max))
                nc.vector.tensor_scalar(m3[:, u % 2, 1:2], m3[:, u % 2, 0:1], -1.0, None, ALU.mult).then_inc(m3_ready, 1)

            maximum3(0)
            maximum3(1)
            for u in range(NU):
                dve.wait_ge(tr3, u + 1)
                if u >= 2:
                    dve.wait_ge(t3, u - 1)
                nc.vector.tensor_copy(P3T[:, L * (u % 2) + CH:L * (u % 2) + L], bank(5)).then_inc(tr3_d, 1)
                if u + 2 < NU:
                    maximum3(u + 2)
            dve.wait_ge(t3_ps, 1)
            t3v = ps[:, 6, 0:NU * E1].rearrange("p (u e) -> p u e", e=E1)
            link(nc.vector.reciprocal(r3[:], t3v[:, :, D3:E1]))
            nc.vector.tensor_tensor(T3[:], t3v[:, :, 0:D3], r3[:].to_broadcast([P, NU, D3]), ALU.mult).then_inc(t3_done, 1)
            for it in range(ITERS):
                for k in range(3):
                    for g in range(NG):
                        if k == 0:
                            dve.wait_ge(kv_act, NG * it + g + 1)
                        else:
                            dve.wait_ge(p_ps, 2 * NG * it + NG * (k - 1) + g + 1)
                        src = ps[:, g, :].rearrange("p (h m) -> p h m", h=4)
                        nc.vector.scalar_tensor_tensor(A[:, g], src, -1.0, eyes[:, k].to_broadcast([P, 4, P]), ALU.mult, ALU.add)\
                            .then_inc(a_ready, 1)
            dve.wait_ge(y_ps, 1)
            nc.vector.tensor_scalar(Y9[:, :, 0:D3], ps[:, 1, 0:NU * D3].rearrange("p (u d) -> p u d", d=D3), QUARTER, None, ALU.mult)\
                .then_inc(y_done, 1)

            def finish(t):
                dve.wait_ge(o1, t + 1)
                ov = ps[:, 7, :].rearrange("p (h e) -> p h e", e=WIDE)
                link(nc.vector.reciprocal(r1[:, t % 2], ov[:, :, D3:E1]))
                nc.vector.tensor_tensor(Y[:, t, :].rearrange("p (h d) -> p h d", h=H3), ov[:, :, 0:D3], r1[:, t % 2].to_broadcast([P, H3, D3]),
                                        ALU.mult).then_inc(o1_used, 1)

            for u in range(2 * NT):
                src = ps[:, 2 * (u % 2):2 * (u % 2) + 2, :].rearrange("p a (h m) -> p (a h) m", m=LM)
                dve.wait_ge(s1, u + 1)
                link(nc.vector.tensor_reduce(m1[:, u % 2, :, 0], src, AX.X, ALU.max))
                if u >= 2:
                    dve.wait_ge(tr1, u - 1)
                nc.vector.tensor_tensor(E[:, u % 2], src, m1[:, u % 2].to_broadcast([P, 8, LM]), ALU.subtract).then_inc(e1_sub, 1)
                if u % 2 == 1 and u >= 3:
                    finish(u // 2 - 1)
            finish(NT - 1)
            shared.chained = link.count


NE = 8
HID = 4 * P
HC = HID // P


def split(engine, src, high, low, done):
    engine.tensor_copy(high, src).then_inc(done, 1)
    return lambda: engine.tensor_tensor(low, src, high.bitcast(FP32), ALU.subtract).then_inc(done, 1)


def products(nc, out, left, right, start, stop):
    (lh, ll), (rh, rl) = left, right
    nc.tensor.matmul(out, lh, rh, start=start, stop=False)
    nc.tensor.matmul(out, lh, rl, start=False, stop=False)
    return nc.tensor.matmul(out, ll, rh, start=False, stop=stop)


class MoeWeights:

    def __init__(self, nc, ctx, sems, dram):
        sb = lambda n, shape: ctx.enter_context(nc.sbuf_tensor(f"e_{n}", shape, FP32))
        self.router, self.prio, self.w1, self.w2 = sb("router", [P, NE]), sb("prio", [P, 1, NE]), sb("w1", [P, NE, HID]), sb("w2", [P, NE, HC, P])
        self.loaded, self.w1_in, self.w2_in = (sems.enter_context(nc.semaphore(f"e_{n}")) for n in ("loaded", "w1_in", "w2_in"))
        self.loads = [(self.router[:], dram["router"], self.loaded), (self.prio[:], dram["prio"], self.loaded),
                      (self.w1[:], dram["w1"], self.w1_in), (self.w2[:], dram["w2"], self.w2_in)]


def moe_stage(nc, sems, shared, XT, Y, weights):
    with ExitStack() as ctx:
        def sb(name, shape, dt=FP32):
            return ctx.enter_context(nc.sbuf_tensor(f"e_{name}", shape, dt))

        def sem(name):
            return sems.enter_context(nc.semaphore(f"e_{name}"))

        router, w1, w2, prio = weights.router, weights.w1, weights.w2, weights.prio
        pr, eq, f1, f2, p2 = (sb(n, [P, NT, NE]) for n in ("pr", "eq", "f1", "f2", "p2"))
        mx, sm = sb("mx", [P, NT, 1]), sb("sm", [P, NT, 1])
        gate = sb("gate", [P, NT, NE])
        xh, xl = sb("xh", [P, T], F32R), sb("xl", [P, T], F32R)
        w1h, w1l = sb("w1h", [P, 2, HID], F32R), sb("w1l", [P, 2, HID], F32R)
        Hb = sb("H", [P, 2, HC, CH])
        ps = ctx.enter_context(nc.psum_tensor("e_ps", [P, 8, CH], FP32))
        loaded, w1_in, w2_in, lg_ps, sub_done, exp_done, gelu, up, down, scaled = (
            weights.loaded, weights.w1_in, weights.w2_in, sem("lg_ps"), sem("sub_done"), sem("exp_done"), sem("gelu"), sem("up"), sem("down"),
            sem("scaled"))
        x_split, w_split = sem("x_split"), sem("w_split")
        block = ctx.enter_context(nc.Block())
        NC = T // CH
        units = [(e, c) for e in range(NE) for c in range(NC)]
        logits = ps[:, 6, 0:NT * NE].rearrange("p (t e) -> p t e", e=NE)

        @block.tensor
        def _(pe):
            pe.wait_ge(loaded, 32)
            for t in range(NT):
                step = nc.tensor.matmul(ps[:, 6, NE * t:NE * t + NE], XT[:, P * t:P * t + P], router[:], start=True, stop=True)
            step.then_inc(lg_ps, 1)

            def hidden(k):
                e, c = units[k]
                pe.wait_ge(x_split, 2 * (c + 1))
                if c == 0:
                    pe.wait_ge(w_split, 2 * e + 2)
                for j in range(HC):
                    if k:
                        pe.wait_ge(gelu, HC * (k - 1) + j + 1)
                    cols, tokens = slice(P * j, P * j + P), slice(CH * c, CH * c + CH)
                    products(nc, ps[:, j, :], (w1h[:, e % 2, cols], w1l[:, e % 2, cols]), (xh[:, tokens], xl[:, tokens]), True, True)\
                        .then_inc(up, 1)

            hidden(0)
            pe.wait_ge(w2_in, 16)
            for k, (e, c) in enumerate(units):
                if k + 1 < len(units):
                    hidden(k + 1)
                pe.wait_ge(gelu, HC * (k + 1))
                if k >= 2:
                    pe.wait_ge(scaled, k - 1)
                for t in range(4):
                    for j in range(HC):
                        step = nc.tensor.matmul(ps[:, 4 + k % 2, P * t:P * t + P], Hb[:, k % 2, j, P * t:P * t + P], w2[:, e, j, :],
                                                start=j == 0, stop=j == HC - 1)
                step.then_inc(down, 1)

        @block.gpsimd
        def _(pool):
            pool.wait_ge(w1_in, 16)
            for e in range(NE):
                if e >= 2:
                    pool.wait_ge(up, HC * NC * (e - 1))
                lower = split(nc.gpsimd, w1[:, e, :], w1h[:, e % 2], w1l[:, e % 2], w_split)
                pool.wait_ge(w_split, 2 * e + 1)
                lower()

        @block.scalar
        def _(act):
            act.wait_ge(sub_done, 1)
            nc.scalar.activation(pr[:], pr[:], ACT.Exp).then_inc(exp_done, 1)
            for k, (e, c) in enumerate(units):
                if k >= 2:
                    act.wait_ge(down, k - 1)
                for j in range(HC):
                    act.wait_ge(up, HC * k + j + 1)
                    nc.scalar.activation(Hb[:, k % 2, j, :], ps[:, j, :], ACT.Gelu).then_inc(gelu, 1)

        @block.vector
        def _(dve):
            link = Chain(dve, shared.sems[-1], shared.chained)
            full = [P, NT, NE]
            for c in range(NC):
                cols = slice(CH * c, CH * c + CH)
                lower = split(nc.vector, XT[:, cols], xh[:, cols], xl[:, cols], x_split)
                dve.wait_ge(x_split, 2 * c + 1)
                lower()
            dve.wait_ge(lg_ps, 1)
            link(nc.vector.tensor_reduce(mx[:, :, 0], logits, AX.X, ALU.max))
            nc.vector.tensor_tensor(pr[:], logits, mx[:].to_broadcast(full), ALU.subtract).then_inc(sub_done, 1)
            dve.wait_ge(exp_done, 1)
            link(nc.vector.tensor_reduce(sm[:, :, 0], pr[:], AX.X, ALU.add))
            link(nc.vector.reciprocal(sm[:], sm[:]))
            link(nc.vector.tensor_tensor(pr[:], pr[:], sm[:].to_broadcast(full), ALU.mult))
            for src, found in ((pr, f1), (p2, f2)):
                link(nc.vector.tensor_reduce(mx[:, :, 0], src[:], AX.X, ALU.max))
                link(nc.vector.tensor_tensor(eq[:], src[:], mx[:].to_broadcast(full), ALU.is_equal))
                link(nc.vector.tensor_tensor(eq[:], eq[:], prio[:].to_broadcast(full), ALU.mult))
                link(nc.vector.tensor_reduce(mx[:, :, 0], eq[:], AX.X, ALU.max))
                link(nc.vector.tensor_tensor(found[:], eq[:], mx[:].to_broadcast(full), ALU.is_equal))
                if src is pr:
                    link(nc.vector.scalar_tensor_tensor(p2[:], f1[:], -2.0, pr[:], ALU.mult, ALU.add))
            link(nc.vector.tensor_tensor(f1[:], f1[:], f2[:], ALU.add))
            link(nc.vector.tensor_tensor(gate[:], pr[:], f1[:], ALU.mult))
            for k, (e, c) in enumerate(units):
                dve.wait_ge(down, k + 1)
                if k >= 4:
                    dve.wait_ge(scaled, k - 3)
                for i in range(4):
                    t = 4 * c + i
                    src = ps[:, 4 + k % 2, P * i:P * i + P]
                    if e == 0:
                        step = nc.vector.tensor_scalar(Y[:, t, :], src, gate[:, t, e:e + 1], None, ALU.mult)
                    else:
                        step = nc.vector.scalar_tensor_tensor(Y[:, t, :], src, gate[:, t, e:e + 1], Y[:, t, :], ALU.mult, ALU.add)
                step.then_inc(scaled, 1)
            shared.chained = link.count



STAGES = [0, 1, 2, 3]


def load_stage(nc, sems, X, ident, dram, ahead):
    with ExitStack() as ctx:
        loaded = sems.enter_context(nc.semaphore("x_loaded"))
        block = ctx.enter_context(nc.Block())

        @block.sync
        def _(sp):
            sp.dma_start(X[:], dram["x"].rearrange("(t p) d -> p t d", p=P)).then_inc(loaded, 16)
            sp.dma_start(ident[:], dram["ident"]).then_inc(loaded, 16)
            for dst, src, done in ahead:
                sp.dma_start(dst, src).then_inc(done, 16)
            sp.wait_ge(loaded, 32)


def program(nc, dram, out):
    with ExitStack() as ctx, ExitStack() as sems:
        X = ctx.enter_context(nc.sbuf_tensor("X", [P, NT, P], FP32))
        Y = ctx.enter_context(nc.sbuf_tensor("Y", [P, NT, P], FP32))
        XT = ctx.enter_context(nc.sbuf_tensor("XT", [P, T], FP32))
        ident = ctx.enter_context(nc.sbuf_tensor("ident", [P, P], FP32))
        shared = NormSemaphores(nc, sems)
        for i, s in enumerate(STAGES):
            with ExitStack() as buffers:
                weights = (MambaWeights, LocalWeights, NystromWeights, MoeWeights)[s](nc, buffers, sems, dram)
                if i == 0:
                    load_stage(nc, sems, X, ident, dram, weights.loads)
                norm_stage(nc, shared, f"n{i}", X, Y if i else None, XT, ident, ahead=weights.loads if i else ())
                if s == 0:
                    mamba_stage(nc, sems, shared, XT, Y, ident, weights)
                if s == 1:
                    local_stage(nc, sems, XT, Y, ident, weights)
                if s == 2:
                    nystrom_stage(nc, sems, shared, XT, Y, ident, weights)
                if s == 3:
                    moe_stage(nc, sems, shared, XT, Y, weights)
        norm_stage(nc, shared, "n9", X, Y, None, ident, store=out.rearrange("(t p) d -> p t d", p=P))


def kernel(**inputs):
    import concourse.bacc as _bacc
    from concourse import bass_utils
    import ml_dtypes
    a = {k: np.asarray(v) for k, v in inputs.items()}
    split = lambda v: np.ascontiguousarray(v.reshape((DC, P) + v.shape[1:]).swapaxes(0, 1))
    sel = np.zeros((96, 2 * NS, P), ml_dtypes.bfloat16)
    for r in range(96):
        sel[r, r % 32, :] = 1
    arrays = {
        "x": a["L0_attn_x"].reshape(T, P), "ident": np.eye(P, dtype=np.float32), "sel": sel,
        "w_in": np.ascontiguousarray(a["L0_attn_W_in"].T), "w_x": split(np.ascontiguousarray(a["L0_attn_W_x"].T)),
        "w_out": split(np.ascontiguousarray(a["L0_attn_W_out"].T)), "conv_w": split(a["L0_attn_conv_w"].reshape(DI, TAPS)),
        "conv_b": split(a["L0_attn_conv_b"]), "w_dt": split(a["L0_attn_w_dt"]), "b_dt": split(a["L0_attn_b_dt"]),
        "wq": a["L1_attn_Wq"].T, "wk": a["L1_attn_Wk"].T, "wv": a["L1_attn_Wv"].T, "bq": a["L1_attn_bq"].reshape(P, 1),
        "bk": a["L1_attn_bk"].reshape(P, 1), "bv": np.broadcast_to(a["L1_attn_bv"], (P, P)),
        "head_mask": np.repeat(np.eye(H3, dtype=np.float32), D3, axis=0).reshape(P, H3, 1),
        "fold": np.concatenate([np.eye(P // 4, D3 + 1, dtype=np.float32)] * 4),
        "eyes": np.stack([np.eye(P, dtype=np.float32) * k for k in (7, 15, 13)], axis=1).reshape(P, 3, 1, P),
        "router": a["L1_ffn_router_w"].T, "w1": a["L1_ffn_w1"].transpose(2, 0, 1),
        "w2": a["L1_ffn_w2"].reshape(NE, P, HC, P).transpose(3, 0, 2, 1),
        "prio": np.broadcast_to(np.arange(NE, 0, -1, dtype=np.float32), (P, 1, NE)),
        "a_log": split(a["L0_attn_A_log"]), "d_par": split(a["L0_attn_D_param"]),
    }
    qkv = a["L0_ffn_Wqkv"]
    half = np.arange(0, D2, 2, dtype=np.float32)
    freqs = np.arange(L, dtype=np.float32)[:, None] * (np.float32(1) / np.float32(10000.0) ** (half / np.float32(D2)))[None, :]
    freqs = np.concatenate([freqs, freqs], -1)
    power = ((np.arange(L) - L // 2) / (WIN // 2)).astype(np.float32)
    scale = ((half + np.float32(0.4 * D2)) / np.float32(1.4 * D2))[None, :] ** power[:, None]
    scale = np.concatenate([scale, scale], -1)
    sign = np.where(np.arange(D2) < D2 // 2, -1, 1).astype(np.float32)
    cos, sin = np.cos(freqs), np.sin(freqs) * sign
    base = np.stack([cos * scale, sin * scale, cos / scale, sin / scale]).astype(np.float32)
    q, key = np.arange(P)[:, None] % WIN, np.arange(2 * WIN)[None, :] - WIN
    seen = (key <= q) & (q - key <= WIN)
    first = seen & ((np.arange(P)[:, None] >= WIN) | (key >= 0))
    swap = lambda v: np.concatenate([v[:, D2 // 2:], v[:, :D2 // 2]], -1)
    qs, ks = a["L0_ffn_q_scale"], a["L0_ffn_k_scale"]
    chunks = lambda v: np.pad(v, [(0, 0), (0, FC * P - FF)]).reshape(DEPTH, FC, P).transpose(0, 2, 1)
    arrays |= {
        "wqk": qkv[:, :, :2 * INNER], "wvl": qkv[:, :, 2 * INNER:].reshape(DEPTH, P, HP, 2, D2).transpose(0, 1, 3, 2, 4).reshape(DEPTH, P, 2, HP * D2),
        "wo": a["L0_ffn_Wo"].reshape(DEPTH, HP, P, P).transpose(0, 2, 1, 3), "w1l": a["L0_ffn_W1"],
        "w2l": np.pad(a["L0_ffn_W2"], [(0, 0), (0, FC * P - FF), (0, 0)]).reshape(DEPTH, FC, P, P).transpose(0, 2, 1, 3),
        "vec": np.concatenate([a["L0_ffn_ln_g"][:, :, None], a["L0_ffn_ln_b"][:, :, None], chunks(a["L0_ffn_b1"][:, :FF]), chunks(a["L0_ffn_b1"][:, FF:]),
                               a["L0_ffn_b2"][:, :, None]], axis=2),
        "scales": np.broadcast_to(np.stack([qs, swap(qs), ks, swap(ks)], 1)[:, None, :, None, :], (DEPTH, P, 4, 1, D2)),
        "base": base.reshape(4, NB, P, D2).transpose(2, 0, 1, 3),
        "mask": np.where(np.stack([first, seen]), 0, -3e38).astype(np.float32).transpose(1, 0, 2).reshape(P, 2, 1, 2 * WIN),
    }
    arrays = {n: np.ascontiguousarray(v) for n, v in arrays.items()}
    nc = _bacc.Bacc("TRN2", target_bir_lowering=False, num_devices=1)
    dram = {n: nc.dram_tensor(f"in_{n}", v.shape, mybir.dt.from_np(v.dtype), kind="ExternalInput").ap() for n, v in arrays.items()}
    out = nc.dram_tensor("out", (T, P), FP32, kind="ExternalOutput").ap()
    program(nc, dram, out)
    r = bass_utils.run_bass_kernel_spmd(nc, [{f"in_{n}": v for n, v in arrays.items()}], core_ids=[0])
    return r.results[0]["out"].reshape(B, L, P)
```
